# Optimizing a Trainium2 kernel written in Bass

```python
import numpy as np
import jax
import jax.numpy as jnp

def _softmax(x, axis=-1):
    return jax.nn.softmax(x, axis=axis)

def _gelu(x):
    return jax.nn.gelu(x, approximate=True)

def _silu(x):
    return jax.nn.silu(x)

def _sigmoid(x):
    return jax.nn.sigmoid(x)

def _layernorm(x, axis=-1, eps=1e-05):
    m = jnp.mean(x, axis=axis, keepdims=True)
    v = jnp.var(x, axis=axis, keepdims=True)
    return (x - m) / jnp.sqrt(v + eps)

def _scatter_add(tgt, idx, src, axis=0):
    return tgt.at[idx].add(src)

def _segment_sum(src, seg, n):
    return jax.ops.segment_sum(src, seg, n)
kernel_name = 'mk_gps_d1_gnn_r8_bba2ab'

def setup_inputs(seed: int=0):
    np.random.seed(seed)
    _w = jnp.asarray

    def _rec_inputs():
        import jax
        import jax.numpy as jnp
        _gk = jax.random.key(seed)
        x = -0.0002117 + 1 * jax.random.normal(jax.random.fold_in(_gk, 1), (6250, 256), jnp.float32)
        src = jax.random.randint(jax.random.fold_in(_gk, 2), (200000,), 0, 6250, jnp.int32)
        dst = jax.random.randint(jax.random.fold_in(_gk, 3), (200000,), 0, 6250, jnp.int32)
        _o = jnp.argsort(dst, stable=True)
        src = src[_o]
        dst = dst[_o]
        return (x, src, dst)
    x, src, dst = _rec_inputs()

    def _L0_gnn_setup():
        import jax, jax.numpy as jnp
        import numpy as np
        N_NODES = 12500
        N_EDGES = 200000
        IN_FEATS = 256
        OUT_FEATS = 64
        NHEAD = 4
        ALPHA = 0.2
        key = jax.random.key(seed)
        k1, k2, k3, k4, k5, k6 = jax.random.split(key, 6)
        stdv_w = np.sqrt(6.0 / (IN_FEATS + OUT_FEATS * NHEAD))
        stdv_a = np.sqrt(6.0 / (NHEAD + OUT_FEATS))
        return {'x': jax.random.normal(k1, (N_NODES, IN_FEATS), dtype=jnp.float32), 'W': jax.random.uniform(k2, (IN_FEATS, OUT_FEATS * NHEAD), minval=-stdv_w, maxval=stdv_w, dtype=jnp.float32), 'a_l': jax.random.uniform(k3, (1, NHEAD, OUT_FEATS), minval=-stdv_a, maxval=stdv_a, dtype=jnp.float32), 'a_r': jax.random.uniform(k4, (1, NHEAD, OUT_FEATS), minval=-stdv_a, maxval=stdv_a, dtype=jnp.float32), 'row': jax.random.randint(k5, (N_EDGES,), 0, N_NODES, dtype=jnp.int32), 'col': jax.random.randint(k6, (N_EDGES,), 0, N_NODES, dtype=jnp.int32)}
    _L0_gnn_all = _L0_gnn_setup()
    _L0_gnn_in = {k: v for k, v in _L0_gnn_all.items() if k in ('W', 'a_l', 'a_r')}
    del _L0_gnn_all

    def _L0_mix_setup():
        import jax, jax.numpy as jnp
        import numpy as np
        HEADS = 8
        DIM_HEAD = 64
        EPS = 1e-05

        def _inst_norm_lastdim(t):
            mu = jnp.mean(t, axis=-1, keepdims=True)
            var = jnp.mean(jnp.square(t - mu), axis=-1, keepdims=True)
            return (t - mu) * jax.lax.rsqrt(var + EPS)
        key = jax.random.key(seed)
        k1, k2, k3, k4 = jax.random.split(key, 4)
        b, n, dim = (4, 1024, 256)
        inner = HEADS * DIM_HEAD
        x = jax.random.normal(k1, (b, n, dim), dtype=jnp.float32)
        Wqkv = jax.random.normal(k2, (3 * inner, dim), dtype=jnp.float32) * (1.0 / np.sqrt(dim))
        Wout = jax.random.normal(k3, (dim, inner), dtype=jnp.float32) * (1.0 / np.sqrt(inner))
        bout = jax.random.normal(k4, (dim,), dtype=jnp.float32) * 0.01
        return {'x': x, 'Wqkv': Wqkv, 'Wout': Wout, 'bout': bout}
    _L0_mix_all = _L0_mix_setup()
    _L0_mix_in = {k: v for k, v in _L0_mix_all.items() if k in ('Wqkv', 'Wout', 'bout')}
    del _L0_mix_all

    def _L0_ffn_setup():
        import math
        import jax, jax.numpy as jnp
        import numpy as np
        CAPACITY_FACTOR = 1.25
        key = jax.random.key(seed)
        ks = jax.random.split(key, 5)
        B, L, D, F, E = (8, 1024, 256, 1024, 8)
        h = jax.random.normal(ks[0], (B, L, D), dtype=jnp.float32)
        gate_w = jax.random.normal(ks[1], (D, E), dtype=jnp.float32) * 0.02
        gate_b = jnp.zeros((E,), dtype=jnp.float32)
        w1 = jax.random.normal(ks[2], (E, D, F), dtype=jnp.float32) * (1.0 / math.sqrt(D))
        b1 = jnp.zeros((E, F), dtype=jnp.float32)
        w2 = jax.random.normal(ks[3], (E, F, D), dtype=jnp.float32) * (1.0 / math.sqrt(F))
        b2 = jnp.zeros((E, D), dtype=jnp.float32)
        return {'h': h, 'gate_w': gate_w, 'gate_b': gate_b, 'w1': w1, 'b1': b1, 'w2': w2, 'b2': b2}
    _L0_ffn_all = _L0_ffn_setup()
    _L0_ffn_in = {k: v for k, v in _L0_ffn_all.items() if k in ('gate_w', 'gate_b', 'w1', 'b1', 'w2', 'b2')}
    del _L0_ffn_all
    return {'x': x, 'src': src, 'dst': dst, 'L0_gnn_W': _L0_gnn_in['W'], 'L0_gnn_a_l': _L0_gnn_in['a_l'], 'L0_gnn_a_r': _L0_gnn_in['a_r'], 'L0_mix_Wqkv': _L0_mix_in['Wqkv'], 'L0_mix_Wout': _L0_mix_in['Wout'], 'L0_mix_bout': _L0_mix_in['bout'], 'L0_ffn_gate_w': _L0_ffn_in['gate_w'], 'L0_ffn_gate_b': _L0_ffn_in['gate_b'], 'L0_ffn_w1': _L0_ffn_in['w1'], 'L0_ffn_b1': _L0_ffn_in['b1'], 'L0_ffn_w2': _L0_ffn_in['w2'], 'L0_ffn_b2': _L0_ffn_in['b2']}

def reference(x, src, dst, L0_gnn_W, L0_gnn_a_l, L0_gnn_a_r, L0_mix_Wqkv, L0_mix_Wout, L0_mix_bout, L0_ffn_gate_w, L0_ffn_gate_b, L0_ffn_w1, L0_ffn_b1, L0_ffn_w2, L0_ffn_b2):
    import jax
    import jax.numpy as jnp

    def _L0_gnn_ref(x, W, a_l, a_r, row, col):
        import jax, jax.numpy as jnp
        import numpy as np
        N_NODES = 12500
        N_EDGES = 200000
        IN_FEATS = 256
        OUT_FEATS = 64
        NHEAD = 4
        ALPHA = 0.2
        n = x.shape[0]
        h = (x @ W).reshape(n, NHEAD, OUT_FEATS)
        h = jnp.where(jnp.isnan(h), 0.0, h)
        h_l = (a_l * h).sum(-1)
        h_r = (a_r * h).sum(-1)
        e = h_l[row] + h_r[col]
        e = jnp.where(e > 0, e, ALPHA * e)
        m = jax.ops.segment_max(e, row, num_segments=n)
        m = jnp.where(jnp.isfinite(m), m, 0.0)
        ex = jnp.exp(e - m[row])
        denom = jax.ops.segment_sum(ex, row, num_segments=n)
        att = ex / (denom[row] + 1e-16)
        msg = att[:, :, None] * h[col]
        out = jax.ops.segment_sum(msg, row, num_segments=n)
        return out.reshape(n, NHEAD * OUT_FEATS)

    def _L0_mix_ref(x, Wqkv, Wout, bout):
        import jax, jax.numpy as jnp
        import numpy as np
        HEADS = 8
        DIM_HEAD = 64
        EPS = 1e-05

        def _inst_norm_lastdim(t):
            mu = jnp.mean(t, axis=-1, keepdims=True)
            var = jnp.mean(jnp.square(t - mu), axis=-1, keepdims=True)
            return (t - mu) * jax.lax.rsqrt(var + EPS)
        b, n, dim = x.shape
        qkv = jnp.einsum('bnc,fc->bnf', x, Wqkv)
        q, k, v = jnp.split(qkv, 3, axis=-1)

        def to_heads(t):
            return t.reshape(b, n, HEADS, DIM_HEAD).transpose(0, 2, 1, 3)
        q, k, v = (to_heads(q), to_heads(k), to_heads(v))
        k = _inst_norm_lastdim(k)
        v = _inst_norm_lastdim(v)
        dots = jnp.einsum('bhnd,bhne->bhde', k, v)
        out = jnp.einsum('bhnd,bhde->bhne', q, dots) / n
        out = out.transpose(0, 2, 1, 3).reshape(b, n, HEADS * DIM_HEAD)
        return jnp.einsum('bnf,cf->bnc', out, Wout) + bout

    def _L0_ffn_ref(h, gate_w, gate_b, w1, b1, w2, b2):
        import math
        import jax, jax.numpy as jnp
        import numpy as np
        CAPACITY_FACTOR = 1.25
        B, L, D = h.shape
        E = gate_w.shape[1]
        T = B * L
        C = max(1, math.ceil(CAPACITY_FACTOR * T / E))
        x = h.reshape(T, D)
        logits = x @ gate_w + gate_b
        probs = jax.nn.softmax(logits, axis=-1)
        idx = jnp.argmax(probs, axis=-1)
        prb = jnp.take_along_axis(probs, idx[:, None], axis=1)[:, 0]
        one_hot = jax.nn.one_hot(idx, E, dtype=jnp.float32)
        pos = (jnp.cumsum(one_hot, axis=0) * one_hot).sum(-1).astype(jnp.int32) - 1
        kept = pos < C
        pos_safe = jnp.where(kept, pos, C)
        buf = jnp.zeros((E, C, D), dtype=h.dtype).at[idx, pos_safe].set(x, mode='drop')
        hmid = jax.nn.relu(jnp.einsum('ecd,edf->ecf', buf, w1) + b1[:, None, :])
        ybuf = jnp.einsum('ecf,efd->ecd', hmid, w2) + b2[:, None, :]
        pos_g = jnp.minimum(pos, C - 1)
        y_tok = ybuf[idx, pos_g] * (prb * kept)[:, None]
        y = y_tok.reshape(B, L, D)
        y = jnp.nan_to_num(y, nan=0.0, posinf=10000.0, neginf=-10000.0)
        return y
    xn = _layernorm(x, axis=-1)
    x = x + _L0_gnn_ref(xn, L0_gnn_W, L0_gnn_a_l, L0_gnn_a_r, src, dst) + _L0_mix_ref(xn[None], L0_mix_Wqkv, L0_mix_Wout, L0_mix_bout)[0]
    x = x + _L0_ffn_ref(_layernorm(x, axis=-1)[None], L0_ffn_gate_w, L0_ffn_gate_b, L0_ffn_w1, L0_ffn_b1, L0_ffn_w2, L0_ffn_b2)[0]
    return x

_drawn_inputs = setup_inputs


def setup_inputs(seed=0):
    import zlib

    import numpy as np

    out = dict(_drawn_inputs(seed))
    spreads = {'L0_ffn_gate_b': (0.0, 0.1), 'L0_ffn_b1': (0.0, 0.727), 'L0_ffn_b2': (0.0, 0.516)}
    factors = {'L0_mix_bout': 4.528}
    for name, (base, spread) in spreads.items():
        noise = np.random.default_rng([zlib.crc32(name.encode()), seed]).standard_normal(out[name].shape)
        drawn = base * np.exp(spread * noise) if base else spread * noise
        out[name] = jnp.asarray(drawn.astype(out[name].dtype))
    for name, factor in factors.items():
        out[name] = (out[name] * factor).astype(out[name].dtype)
    return out
```

```python
from contextlib import ExitStack

import concourse.bass as bass
from concourse import mybir

F32 = mybir.dt.float32
I32 = mybir.dt.int32
ALU = mybir.AluOpType
ACT = mybir.ActivationFunctionType
AX = mybir.AxisListType.X
RMAX = bass.bass_isa.ReduceOp.max
ds = bass.ds

P = 128
NODES, D, EDGES = 6250, 256, 200000
HEADS, HD = 4, 64
MH, INNER = 8, 512
EXPERTS, FF = 8, 1024
CAP = -(-5 * NODES // (4 * EXPERTS))
ALPHA, EPS = 0.2, 1e-5

NT = -(-NODES // P)
CT = 7
CH = NT // CT
LAST = NODES - (NT - 1) * P
KC = D // P

ROW = D + HEADS

DB = 13
KEY_ONE = 1 << 29
PAD_SRC = (1 << DB) - 1
LB = 11
COLS = 1 << LB
SHORT = EDGES // P
REST = EDGES - SHORT * P

GT, HT = 8, 4
GROUPS = -(-EDGES // (GT * P))
ET = GROUPS * GT
RING = 4


def setup_consts(nc, m):
    ctx = ExitStack()
    with ctx:
        made = ctx.enter_context(nc.semaphore("c_made"))
        block = ctx.enter_context(nc.Block())

        @block.gpsimd
        def _(pool):
            nc.gpsimd.memset(m.ident[:, :], 0.0).then_inc(made, 1)
            nc.gpsimd.memset(m.ones[:, :], 1.0)
            nc.gpsimd.memset(m.tri[:, :], 1.0).then_inc(made, 1)
            nc.gpsimd.memset(m.zeros[:, :], 0.0)
            nc.gpsimd.iota(m.lane[:, :], [[0, 1]], base=0, channel_multiplier=1)
            nc.gpsimd.iota(m.iota[:, :], [[1, P]], base=0, channel_multiplier=0,
                           allow_small_or_imprecise_dtypes=True)
            nc.gpsimd.iota(m.iota_row[:, :], [[1, GROUPS]], base=0, channel_multiplier=0,
                           allow_small_or_imprecise_dtypes=True)
            pool.wait_ge(made, 2)
            nc.gpsimd.affine_select(out=m.ident[:, :], in_=m.ident[:, :], compare_op=ALU.not_equal, fill=1.0,
                                    base=0, pattern=[[-1, P]], channel_multiplier=1)
            nc.gpsimd.affine_select(out=m.tri[:, :], in_=m.tri[:, :], compare_op=ALU.is_ge, fill=0.0,
                                    base=0, pattern=[[1, P]], channel_multiplier=-1)


def node_rows(nc, m, x, W, a_l, a_r, slots):
    ctx = ExitStack()
    with ctx:
        sem = lambda n: ctx.enter_context(nc.semaphore(n))
        sb = lambda n, s, d=F32: ctx.enter_context(nc.sbuf_tensor(n, s, d))
        x_in = [sem(f"n_x{g}") for g in range(CH)]
        w_in, a_in = sem("n_w"), sem("n_a")
        link_v, var_ok, std_ok = sem("n_link"), sem("n_var"), sem("n_std")
        xn_ok, xt_ok, xs_ok, saved = sem("n_xn"), sem("n_xt"), sem("n_xs"), sem("n_saved")
        h_ok, h_copied, cleared = sem("n_h"), sem("n_hc"), sem("n_clr")
        mulled, row_ok, row_out, zeroed = sem("n_mul"), sem("n_row"), sem("n_out"), sem("n_zero")
        hr_max, all_max = sem("n_hrmax"), sem("n_allmax")
        padded = sem("n_pad")
        w_sb = sb("n_wsb", [P, KC, D])
        a_sb = sb("n_asb", [P, 2, D])
        stats = sb("n_stats", [P, CT, 6])
        mv = sb("n_mv", [P, CT, 2])
        std = sb("n_stdsb", [P, CT])
        rstd = sb("n_rstd", [P, CT])
        xn = sb("n_xnsb", [P, CT, D])
        xs = sb("n_xssb", [P, CT, D])
        hc = sb("n_hcsb", [P, CT, D])
        mask = sb("n_mask", [P, CT, D], I32)
        row = sb("n_rowsb", [P, CT, ROW])
        prod = sb("n_prod", [P, CT, 2, D])
        zrow = sb("n_zrow", [P, 2048])
        peak = sb("n_peak", [P, HEADS])
        top = sb("n_top", [P, HEADS])
        psx, psh = m.ps[0:2], m.ps[2:4]
        zw = slots.shape[0] * D // P
        slots_flat = slots.rearrange("s d -> (s d)").rearrange("(p f) -> p f", p=P)
        nz = -(-zw // 2048)
        block = ctx.enter_context(nc.Block())

        @block.sync
        def _(sp):
            xt = x[0:(NT - 1) * P, :].rearrange("(t p) c -> p t c", p=P)
            sp.dma_start(w_sb[:, :, :], W.rearrange("(k p) f -> p k f", p=P)).then_inc(w_in, 16)
            sp.wait_ge(padded, 1)
            for g in range(CH):
                n = CT if g < CH - 1 else CT - 1
                dst = m.x_all[:, g * CT * D:(g * CT + n) * D].rearrange("p (t c) -> p t c", c=D)
                sp.dma_start(dst, xt[:, g * CT:g * CT + n, :]).then_inc(x_in[g], 16)
            sp.dma_start(m.x_all[0:LAST, (NT - 1) * D:NT * D], x[(NT - 1) * P:NODES, :]).then_inc(x_in[CH - 1], 16)
            sp.dma_start(a_sb[:, 0, :], a_l.rearrange("o h d -> o (h d)").to_broadcast([P, D])).then_inc(a_in, 16)
            sp.dma_start(a_sb[:, 1, :], a_r.rearrange("o h d -> o (h d)").to_broadcast([P, D])).then_inc(a_in, 16)
            sp.wait_ge(padded, 2)
            for k in range(nz):
                w = min(2048, zw - k * 2048)
                sp.dma_start(slots_flat[:, k * 2048:k * 2048 + w], zrow[:, 0:w]).then_inc(zeroed, 16)
            table = m.table.rearrange("(t p) c -> p t c", p=P)
            with sp.Fori(0, CH) as g:
                sp.wait_ge(row_ok, g + 1)
                sp.dma_start(table[:, ds(g * CT, CT), :], row[:, :, :]).then_inc(row_out, 16)
            sp.wait_ge(row_out, 16 * CH)
            sp.wait_ge(zeroed, 16 * nz)

        @block.vector
        def _(dve):
            n = [0]

            def link(ins):
                n[0] += 1
                ins.then_inc(link_v, 1)

            nc.vector.memset(m.x_all[:, (NT - 1) * D:NT * D], 0.0).then_inc(padded, 1)
            nc.vector.memset(zrow[:, :], 0.0).then_inc(padded, 1)
            dve.wait_ge(a_in, 32)
            LINKS = 7
            for q in range(CH):
                dve.wait_ge(x_in[q], 16 if q < CH - 1 else 32)
            with dve.Fori(0, CH) as g:
                base = g * LINKS
                for k in range(CT):
                    last = nc.vector.bn_stats(stats[:, k, :], m.x_all[:, ds((g * CT + k) * D, D)])
                last.then_inc(link_v, 1)
                dve.wait_ge(link_v, base + 1)
                dve.sem_inc(m.held, 1)
                for k in range(CT):
                    last = nc.vector.bn_aggr(mv[:, k, :], stats[:, k, :])
                last.then_inc(link_v, 1)
                dve.wait_ge(link_v, base + 2)
                nc.vector.tensor_scalar(rstd[:, :], mv[:, :, 1], EPS, None, ALU.add).then_inc(var_ok, 1)
                dve.wait_ge(std_ok, g + 1)
                nc.vector.reciprocal(rstd[:, :], std[:, :]).then_inc(link_v, 1)
                dve.wait_ge(link_v, base + 3)
                dve.wait_ge(xt_ok, g * CT)
                for k in range(CT):
                    nc.vector.tensor_scalar(xn[:, k, :], m.x_all[:, ds((g * CT + k) * D, D)], mv[:, k, 0:1],
                                            rstd[:, k:k + 1], ALU.subtract, ALU.mult).then_inc(xn_ok, 1)
                dve.wait_ge(h_copied, (g + 1) * CT)
                nc.vector.tensor_tensor(mask[:, :, :], hc[:, :, :], hc[:, :, :], ALU.is_equal).then_inc(link_v, 1)
                dve.wait_ge(link_v, base + 4)
                dve.wait_ge(cleared, g + 1)
                dve.sem_inc(m.held, 1)
                nc.vector.copy_predicated(row[:, :, 0:D], mask[:, :, :], hc[:, :, :]).then_inc(link_v, 1)
                dve.wait_ge(link_v, base + 5)
                nc.vector.tensor_tensor(prod[:, :, 0, :], row[:, :, 0:D],
                                        a_sb[:, 0:1, :].to_broadcast([P, CT, D]), ALU.mult)
                nc.vector.tensor_tensor(prod[:, :, 1, :], row[:, :, 0:D],
                                        a_sb[:, 1:2, :].to_broadcast([P, CT, D]), ALU.mult).then_inc(link_v, 1)
                dve.wait_ge(link_v, base + 6)
                logits = m.hlr[:, ds(g * CT * 8, CT * 8)].rearrange("p (t c) -> p t c", c=8)
                for s in range(2):
                    last = nc.vector.tensor_reduce(logits[:, :, 4 * s:4 * s + 4],
                                                   prod[:, :, s, :].rearrange("p t (h d) -> p t h d", h=HEADS),
                                                   AX, ALU.add)
                last.then_inc(link_v, 1)
                dve.wait_ge(link_v, base + 7)
                dve.sem_inc(m.held, 1)
                nc.vector.tensor_copy(row[:, :, D:ROW], logits[:, :, 4:8]).then_inc(row_ok, 1)
            hl = m.hlr[:, :].rearrange("p (t c) -> p t c", c=8)
            nc.vector.tensor_reduce(peak[:, :], hl[:, :, 4:8].rearrange("p t h -> p h t"), AX,
                                    ALU.max).then_inc(hr_max, 1)
            dve.wait_ge(all_max, 1)
            total = LINKS * CH
            nc.vector.tensor_tensor(hl[:, :, 4:8], hl[:, :, 0:4],
                                    top[:, :].unsqueeze(1).to_broadcast([P, NT, HEADS]), ALU.add).then_inc(link_v, 1)
            dve.wait_ge(link_v, total + 1)
            nc.vector.scalar_tensor_tensor(out=hl[:, :, 4:8], in0=hl[:, :, 4:8], scalar=ALPHA, in1=hl[:, :, 4:8],
                                           op0=ALU.mult, op1=ALU.max)

        @block.scalar
        def _(act):
            with act.Fori(0, CH) as g:
                act.wait_ge(var_ok, g + 1)
                nc.scalar.activation(std[:, :], rstd[:, :], ACT.Sqrt).then_inc(std_ok, 1)
                for k in range(CT):
                    act.wait_ge(xt_ok, g * CT + k + 1)
                    act.wait_ge(h_ok, g * CT)
                    act.wait_ge(saved, g)
                    nc.scalar.activation(xs[:, k, :], psx[k % 2][:, 0:D], ACT.Copy).then_inc(xs_ok, 1)
                    if k >= 1:
                        act.wait_ge(h_ok, g * CT + k)
                        nc.scalar.activation(hc[:, k - 1, :], psh[(k - 1) % 2][:, 0:D], ACT.Copy).then_inc(h_copied, 1)
                act.wait_ge(h_ok, g * CT + CT)
                nc.scalar.activation(hc[:, CT - 1, :], psh[(CT - 1) % 2][:, 0:D], ACT.Copy).then_inc(h_copied, 1)

        @block.tensor
        def _(pe):
            pe.wait_ge(w_in, 16)
            with pe.Fori(0, CH) as g:
                for k in range(CT + 1):
                    if k < CT:
                        pe.wait_ge(xn_ok, g * CT + k + 1)
                        pe.wait_ge(xs_ok, g * CT + max(k - 1, 0))
                        for c in range(KC):
                            last = nc.tensor.transpose(psx[k % 2][:, c * P:(c + 1) * P], xn[:, k, c * P:(c + 1) * P],
                                                       m.ident[:, :])
                        last.then_inc(xt_ok, 1)
                    if k >= 1:
                        pe.wait_ge(xs_ok, g * CT + k)
                        pe.wait_ge(h_copied, g * CT + max(k - 2, 0))
                        for c in range(KC):
                            last = nc.tensor.matmul(psh[(k - 1) % 2][:, 0:D], xs[:, k - 1, c * P:(c + 1) * P],
                                                    w_sb[:, c, :], start=c == 0, stop=c == KC - 1)
                        last.then_inc(h_ok, 1)

        @block.gpsimd
        def _(pool):
            with pool.Fori(0, CH) as g:
                pool.wait_ge(row_out, 16 * g)
                pool.sem_inc(m.held, 1)
                nc.gpsimd.memset(row[:, :, 0:D], 0.0).then_inc(cleared, 1)
                pool.wait_ge(xs_ok, (g + 1) * CT)
                nc.gpsimd.tensor_copy(m.xt_all[:, ds(g * CT * D, CT * D)],
                                      xs[:, :, :].rearrange("p t c -> p (t c)")).then_inc(saved, 1)
            pool.wait_ge(hr_max, 1)
            nc.gpsimd.partition_all_reduce(top[:, :], peak[:, :], P, RMAX).then_inc(all_max, 1)


def edge_sort(nc, m, src, dst):
    ctx = ExitStack()
    with ctx:
        sem = lambda n: ctx.enter_context(nc.semaphore(n))
        sb = lambda n, s, d=F32: ctx.enter_context(nc.sbuf_tensor(n, s, d))
        loaded, stage_done, turned = sem("s_load"), sem("s_stage"), sem("s_turn")
        keys = [sb("s_keys0", [P, COLS]), sb("s_keys1", [P, COLS])]
        src_sb, dst_sb = sb("s_src", [P, COLS], I32), sb("s_dst", [P, COLS], I32)
        bits = sb("s_bits", [P, 8], I32)
        sign = sb("s_sign", [P, 8])
        turn = sb("s_turns", [P, 8])
        code = sb("s_code", [P, ET], I32)
        last_src = sb("s_last", [P, 2])
        last_int = sb("s_lasti", [P, 2], I32)
        bound = sb("s_bound", [P, NT + 1])
        below = sb("s_below", [P, NT + 1, 2])
        belows = sb("s_belows", [P, NT + 1])
        lo_f = sb("s_lof", [P, NT + 1])
        group_no = sb("s_group", [1, GROUPS])
        begun = sb("s_begun", [1, GROUPS, NT - 1])
        uses = sb("s_uses", [1, GROUPS])
        turns = []
        marks = {}
        bank = 4 * P
        block = ctx.enter_context(nc.Block())

        @block.sync
        def _(sp):
            sp.wait_ge(stage_done, 2)
            for t, d in ((src_sb, src), (dst_sb, dst)):
                sp.dma_start(t[:, 0:SHORT], d[0:SHORT * P].rearrange("(p f) -> p f", p=P)).then_inc(loaded, 16)
                sp.dma_start(t[0:REST, SHORT:SHORT + 1],
                             d[SHORT * P:EDGES].rearrange("(p f) -> p f", f=1)).then_inc(loaded, 16)

        @block.vector
        def _(dve):
            done = [0]
            cur = [0]

            def then(ins):
                ins.then_inc(stage_done, 1)
                done[0] += 1
                dve.wait_ge(stage_done, done[0])

            def exchange(dist, mirror=False):
                a, b = keys[cur[0]], keys[1 - cur[0]]
                av = a[:, :].rearrange("p (h two l) -> p h two l", two=2, l=dist)
                bv = b[:, :].rearrange("p (h two l) -> p h two l", two=2, l=dist)
                lo, hi, out_lo, out_hi = av[:, :, 0, :], av[:, :, 1, :], bv[:, :, 0, :], bv[:, :, 1, :]
                if mirror:
                    hi, out_hi = hi[:, :, ::-1], out_hi[:, :, ::-1]
                nc.vector.tensor_tensor(out_lo, lo, hi, ALU.min)
                then(nc.vector.tensor_tensor(out_hi, lo, hi, ALU.max))
                cur[0] ^= 1

            def flip(k):
                a, b = keys[cur[0]], keys[1 - cur[0]]
                then(nc.vector.tensor_scalar(b[:, :], a[:, :], turn[:, k:k + 1], None, ALU.mult))
                cur[0] ^= 1

            def transposed():
                b = keys[1 - cur[0]]
                turns.append((done[0], cur[0]))
                for q in range(4):
                    dve.wait_ge(turned, 4 * (len(turns) - 1) + q + 1)
                    last = nc.vector.tensor_copy(b[:, bank * q:bank * (q + 1)], m.ps[q][:, :])
                then(last)
                cur[0] ^= 1

            then(nc.vector.memset(src_sb[:, :], PAD_SRC))
            then(nc.vector.memset(dst_sb[:, :], NODES))
            for k in range(8):
                last = nc.vector.tensor_scalar(bits[:, k:k + 1], m.lane[:, :], k, 1, ALU.logical_shift_right,
                                               ALU.bitwise_and)
            then(last)
            then(nc.vector.tensor_scalar(sign[:, :], bits[:, :], -2.0, 1.0, ALU.mult, ALU.add))
            nc.vector.tensor_copy(turn[:, 0:1], sign[:, 0:1])
            then(nc.vector.tensor_tensor(turn[:, 1:8], sign[:, 0:7], sign[:, 1:8], ALU.mult))
            dve.wait_ge(loaded, 64)
            then(nc.vector.tensor_scalar(src_sb[:, :], src_sb[:, :], DB, KEY_ONE, ALU.logical_shift_left,
                                         ALU.bitwise_or))
            then(nc.vector.tensor_tensor(keys[0][:, :].bitcast(I32), src_sb[:, :], dst_sb[:, :], ALU.bitwise_or))
            for k in range(1, LB):
                exchange(1 << (k - 1), mirror=True)
                for j in range(k - 2, -1, -1):
                    exchange(1 << j)
            flip(0)
            exchange(1 << (LB - 1), mirror=True)
            for j in range(LB - 2, -1, -1):
                exchange(1 << j)
            for k in range(1, 8):
                flip(k)
                transposed()
                for j in range(k - 1, -1, -1):
                    exchange(1 << j)
                transposed()
                for j in range(LB - 1, -1, -1):
                    exchange(1 << j)
            fin = keys[cur[0]]
            then(nc.vector.tensor_scalar(last_int[:, :], fin[:, GT * P - 1::GT * P].bitcast(I32), DB, PAD_SRC,
                                         ALU.logical_shift_right, ALU.bitwise_and))
            nc.vector.tensor_copy(last_src[:, :], last_int[:, :])
            then(nc.vector.tensor_scalar(bound[:, :], m.iota[:, 0:NT + 1], float(P), None, ALU.mult))
            then(nc.vector.tensor_tensor(below[:, :, :], last_src[:, :].unsqueeze(1).to_broadcast([P, NT + 1, 2]),
                                         bound[:, :].unsqueeze(2).to_broadcast([P, NT + 1, 2]), ALU.is_lt))
            then(nc.vector.tensor_reduce(belows[:, :], below[:, :, :], AX, ALU.add))
            marks["sum"] = done[0]
            turns.append((done[0], cur[0]))
            code_v = code[:, :].rearrange("q (r c) -> q c r", c=COLS // P)
            rows = ET * P // COLS
            for q in range(4):
                dve.wait_ge(turned, 4 * (len(turns) - 1) + q + 1)
                last = nc.vector.tensor_copy(code_v[:, 4 * q:4 * q + 4, :].bitcast(F32),
                                             m.ps[q][:, :].rearrange("q (c r) -> q c r", r=P)[:, :, 0:rows])
            then(last)
            nc.vector.tensor_scalar(m.dst_of[:, :], code[:, :], PAD_SRC, None, ALU.bitwise_and)
            then(nc.vector.tensor_scalar(code[:, :], code[:, :], DB, PAD_SRC, ALU.logical_shift_right,
                                         ALU.bitwise_and))
            nc.vector.tensor_copy(m.src_of[:, :], code[:, :])
            dve.wait_ge(turned, 4 * len(turns) + 1)
            then(nc.vector.tensor_copy(lo_f[:, :], m.ps[4][:, 0:NT + 1]))
            nc.vector.tensor_copy(m.first_group[:, :], lo_f[:, :])
            then(nc.vector.tensor_copy(group_no[:, :], m.iota_row[0:1, 0:GROUPS]))
            then(nc.vector.tensor_tensor(begun[:, :, :], lo_f[0:1, 1:NT].unsqueeze(1).to_broadcast([1, GROUPS, NT - 1]),
                                         group_no[:, :].unsqueeze(2).to_broadcast([1, GROUPS, NT - 1]), ALU.is_le))
            then(nc.vector.tensor_reduce(uses[:, :], begun[:, :, :], AX, ALU.add))
            then(nc.vector.tensor_tensor(uses[:, :], uses[:, :], group_no[:, :], ALU.add))
            then(nc.vector.tensor_scalar(uses[:, :], uses[:, :], 1.0, None, ALU.add))
            then(nc.vector.memset(m.needed[:, 0:RING], 0))
            nc.vector.tensor_copy(m.needed[:, RING:GROUPS], uses[:, 0:GROUPS - RING])

        @block.tensor
        def _(pe):
            for count, which in turns:
                pe.wait_ge(stage_done, count)
                for q in range(4):
                    for c in range(4):
                        at = bank * q + c * P
                        last = nc.tensor.transpose(m.ps[q][:, c * P:(c + 1) * P], keys[which][:, at:at + P],
                                                   m.ident[:, :])
                    last.then_inc(turned, 1)
            pe.wait_ge(stage_done, marks["sum"])
            nc.tensor.matmul(m.ps[4][:, 0:NT + 1], m.ones[:, :], belows[:, :], start=True,
                             stop=True).then_inc(turned, 1)


def attention_steps(nc, m, Wqkv):
    ctx = ExitStack()
    with ctx:
        sem = lambda n: ctx.enter_context(nc.semaphore(n))
        sb = lambda n, s, d=F32: ctx.enter_context(nc.sbuf_tensor(n, s, d))
        w_in, w_turned, w_copied, w_ready = sem("e_win"), sem("e_wturn"), sem("e_wcopy"), sem("e_wready")
        w_nat = sb("e_wnat", [P, 2 * INNER // P, D])
        w_kv = sb("e_wkv", [P, KC, 2 * INNER])
        w_mean = sb("e_wmean", [P, KC * 2 * MH])
        tile_base = sb("e_base", [P, NT])
        index_ok = sem("e_index")
        landed = [sem(f"e_land{r}") for r in range(RING)]
        arrived = sem("e_arrived")
        rows = sb("e_rows", [P, RING * GT * ROW])
        index = [sb(f"e_index{r}", [P, GT], I32) for r in range(RING)]
        hot_ok, turned_ok, hot_back, src_ok, raw_ok, exp_ok, msg_ok, summed = (
            [sem(f"e_{n}{h}") for h in range(2)]
            for n in ("hot", "turned", "back", "src", "raw", "exp", "msg", "sum"))
        link_s, link_t, rel_ok = sem("e_links"), sem("e_linkt"), sem("e_rel")
        rel = sb("e_relsb", [P, GT])
        hot = [sb(f"e_hotsb{h}", [P, HT, P]) for h in range(2)]
        hot_tr = [sb(f"e_hottr{h}", [P, HT, P]) for h in range(2)]
        raw = [sb(f"e_rawsb{h}", [P, HT, HEADS]) for h in range(2)]
        msg = [sb(f"e_msgsb{h}", [P, HT, ROW]) for h in range(2)]
        den = sb("e_den", [P, HEADS])
        agg = sb("e_agg", [P, D])
        opened, out_free = sem("e_open"), sem("e_outfree")
        xk_ok, kv_ok, sq_ok, var_ok, std_ok, ks_ok, dots_ok = (sem(f"e_{n}") for n in
                                                                ("xk", "kv", "sq", "var", "std", "ks", "dots"))
        link_a, v_ok = sem("e_linka"), sem("e_v")
        xk = sb("e_xksb", [P, D])
        sq = sb("e_sqsb", [P, 2 * INNER])
        v_sb = sb("e_vsb", [P, INNER])
        ks = sb("e_kssb", [P, INNER])
        var = sb("e_varsb", [P, 2 * MH])
        std = sb("e_stdsb", [P, 2 * MH])
        scale = sb("e_scalesb", [P, MH])
        ps_hot, ps_out, ps_kv, ps_dots = m.ps[0:2], m.ps[3], m.ps[4:6], m.ps[7]
        src_vals = [bank[:, 0:HT * 8].rearrange("p (t c) -> p t c", c=8) for bank in (m.ps[2], m.ps[6])]
        block = ctx.enter_context(nc.Block())

        @block.sync
        def _(sp):
            sp.dma_start(w_nat[:, :, :], Wqkv[INNER:3 * INNER, :].rearrange("(j p) c -> p j c", p=P)).then_inc(w_in, 16)
            with sp.Fori(0, GROUPS // RING) as n:
                for s in range(RING):
                    sp.wait_ge(landed[s], (n + 1) * (16 * GT))
                    sp.sem_inc(arrived, 1)

        @block.gpsimd
        def _(pool):
            with pool.Fori(0, GROUPS // RING) as n:
                for s in range(RING):
                    need = pool.value_load(m.needed[0:1, ds(n * RING + s, 1)], min_val=0, max_val=2 * GROUPS)
                    pool.wait_ge(msg_ok[1], need)
                    nc.gpsimd.tensor_copy(index[s][:, :],
                                          m.dst_of[:, ds((n * RING + s) * GT, GT)]).then_inc(index_ok, 1)
                    pool.wait_ge(index_ok, n * RING + (s + 1))
                    pool.sem_inc(m.held, 1)
                    for t in range(GT):
                        at = (s * GT + t) * ROW
                        nc.gpsimd.indirect_dma_start(
                            out=rows[:, at:at + ROW], out_offset=None, in_=m.table,
                            in_offset=bass.IndirectOffsetOnAxis(ap=index[s][:, t:t + 1], axis=0),
                        ).then_inc(landed[s], 16)

        def tile_range(eng, b):
            first = eng.value_load(m.first_group[0:1, ds(b, 1)], min_val=0, max_val=GROUPS - 1)
            last = eng.value_load(m.first_group[0:1, ds(b + 1, 1)], min_val=0, max_val=GROUPS - 1)
            return first, last

        @block.vector
        def _(dve):
            dve.wait_ge(w_copied, 4)
            wv = w_kv[:, :, :].rearrange("p k (h d) -> p (k h) d", d=HD)
            nc.vector.tensor_scalar(tile_base[:, :], m.iota[:, 0:NT], float(P), None, ALU.mult)
            nc.vector.tensor_reduce(w_mean[:, :], wv, AX, ALU.add).then_inc(w_ready, 1)
            dve.wait_ge(w_ready, 1)
            nc.vector.tensor_scalar(w_mean[:, :], w_mean[:, :], 1.0 / HD, None, ALU.mult).then_inc(w_ready, 1)
            dve.wait_ge(w_ready, 2)
            nc.vector.tensor_tensor(wv, wv, w_mean[:, :].unsqueeze(2).to_broadcast([P, KC * 2 * MH, HD]),
                                    ALU.subtract).then_inc(w_ready, 1)
            dve.wait_ge(w_ready, 3)
            with dve.Fori(0, NT) as b:
                first, last = tile_range(dve, b)
                with dve.Fori(first, last + 1) as i:
                    n = b + i
                    nc.vector.tensor_scalar(rel[:, :], m.src_of[:, ds(i * GT, GT)], tile_base[:, ds(b, 1)], None,
                                            ALU.subtract).then_inc(rel_ok, 1)
                    dve.wait_ge(rel_ok, n + 1)
                    for h in range(2):
                        dve.wait_ge(summed[h], n)
                        nc.vector.tensor_tensor(hot[h][:, :, :], m.iota[:, :].unsqueeze(1).to_broadcast([P, HT, P]),
                                                rel[:, h * HT:(h + 1) * HT].unsqueeze(2).to_broadcast([P, HT, P]),
                                                ALU.is_equal).then_inc(hot_ok[h], 1)
                    dve.wait_ge(arrived, i + 1)
                    slot = (i & (RING - 1)) * (GT * ROW)
                    part = [rows[:, ds(slot + h * (HT * ROW), HT * ROW)].rearrange("p (t c) -> p t c", c=ROW)
                            for h in range(2)]
                    for h in range(2):
                        dve.wait_ge(src_ok[h], n + 1)
                        dve.wait_ge(exp_ok[h], n)
                        nc.vector.tensor_tensor(raw[h][:, :, :], part[h][:, :, D:ROW], src_vals[h][:, :, 0:HEADS],
                                                ALU.add).then_inc(link_s, 1)
                        dve.wait_ge(link_s, n * 4 + 2 * h + 1)
                        nc.vector.scalar_tensor_tensor(out=raw[h][:, :, :], in0=raw[h][:, :, :], scalar=ALPHA,
                                                       in1=raw[h][:, :, :], op0=ALU.mult,
                                                       op1=ALU.max).then_inc(link_s, 1)
                        dve.wait_ge(link_s, n * 4 + 2 * h + 2)
                        nc.vector.tensor_tensor(raw[h][:, :, :], raw[h][:, :, :], src_vals[h][:, :, HEADS:2 * HEADS],
                                                ALU.subtract).then_inc(raw_ok[h], 1)
                    for h in range(2):
                        dve.wait_ge(exp_ok[h], n + 1)
                        for t in range(HT):
                            last_msg = nc.vector.tensor_tensor(
                                msg[h][:, t, 0:D].rearrange("p (h d) -> p h d", h=HEADS),
                                part[h][:, t, 0:D].rearrange("p (h d) -> p h d", h=HEADS),
                                msg[h][:, t, D:ROW].unsqueeze(2).to_broadcast([P, HEADS, HD]), ALU.mult)
                        last_msg.then_inc(msg_ok[h], 1)
                dve.wait_ge(sq_ok, b + 1)
                nc.vector.tensor_reduce(var[:, :], sq[:, :].rearrange("p (h d) -> p h d", d=HD), AX,
                                        ALU.add).then_inc(link_t, 1)
                dve.wait_ge(link_t, b * 6 + 1)
                nc.vector.tensor_scalar(var[:, :], var[:, :], 1.0 / HD, EPS, ALU.mult, ALU.add).then_inc(var_ok, 1)
                dve.wait_ge(std_ok, b + 1)
                nc.vector.reciprocal(std[:, :], std[:, :]).then_inc(link_t, 1)
                dve.wait_ge(link_t, b * 6 + 2)
                nc.vector.tensor_tensor(scale[:, :], std[:, 0:MH], std[:, MH:2 * MH], ALU.mult).then_inc(link_t, 1)
                dve.wait_ge(link_t, b * 6 + 3)
                dve.wait_ge(dots_ok, b)
                nc.vector.tensor_tensor(ks[:, :].rearrange("p (h d) -> p h d", d=HD),
                                        ps_kv[0][:, :].rearrange("p (h d) -> p h d", d=HD),
                                        scale[:, :].unsqueeze(2).to_broadcast([P, MH, HD]), ALU.mult).then_inc(ks_ok, 1)
                dve.wait_ge(opened, 2 * b + 2)
                nc.vector.tensor_scalar(den[:, :], ps_out[:, D:ROW], 1e-37, None, ALU.max).then_inc(link_t, 1)
                dve.wait_ge(link_t, b * 6 + 4)
                nc.vector.reciprocal(den[:, :], den[:, :]).then_inc(link_t, 1)
                dve.wait_ge(link_t, b * 6 + 5)
                nc.vector.tensor_tensor(agg[:, :].rearrange("p (h d) -> p h d", d=HD),
                                        ps_out[:, 0:D].rearrange("p (h d) -> p h d", d=HD),
                                        den[:, :].unsqueeze(2).to_broadcast([P, HEADS, HD]),
                                        ALU.mult).then_inc(out_free, 1)
                dve.wait_ge(out_free, b + 1)
                nc.vector.tensor_tensor(m.x_all[:, ds(b * D, D)], m.x_all[:, ds(b * D, D)], agg[:, :],
                                        ALU.add).then_inc(link_t, 1)
                dve.wait_ge(link_t, b * 6 + 6)

        @block.scalar
        def _(act):
            for q in range(4):
                act.wait_ge(w_turned, q + 1)
                nc.scalar.activation(w_kv[:, :, 2 * q * P:2 * (q + 1) * P],
                                     m.ps[q][:, :].rearrange("p (k f) -> p k f", k=KC), ACT.Copy).then_inc(w_copied, 1)
            with act.Fori(0, NT) as b:
                first, last = tile_range(act, b)
                act.wait_ge(kv_ok, b)
                nc.scalar.activation(xk[:, :], m.xt_all[:, ds(b * D, D)], ACT.Copy).then_inc(xk_ok, 1)
                with act.Fori(first, last + 1) as i:
                    n = b + i
                    for h in range(2):
                        act.wait_ge(turned_ok[h], n + 1)
                        act.wait_ge(src_ok[h], n)
                        nc.scalar.activation(hot_tr[h][:, :, :].rearrange("p t e -> p (t e)"), ps_hot[h][:, :],
                                             ACT.Copy).then_inc(hot_back[h], 1)
                    for h in range(2):
                        act.wait_ge(raw_ok[h], n + 1)
                        act.wait_ge(summed[h], n)
                        nc.scalar.activation(msg[h][:, :, D:ROW], raw[h][:, :, :], ACT.Exp).then_inc(exp_ok[h], 1)
                act.wait_ge(kv_ok, b + 1)
                act.wait_ge(var_ok, b)
                for s in range(2):
                    nc.scalar.activation(sq[:, s * INNER:(s + 1) * INNER], ps_kv[s][:, :],
                                         ACT.Square).then_inc(sq_ok if s else link_a, 1)
                act.wait_ge(dots_ok, b)
                nc.scalar.activation(v_sb[:, :], ps_kv[1][:, :], ACT.Copy).then_inc(v_ok, 1)
                act.wait_ge(var_ok, b + 1)
                nc.scalar.activation(std[:, :], var[:, :], ACT.Sqrt).then_inc(std_ok, 1)

        @block.tensor
        def _(pe):
            pe.wait_ge(w_in, 16)
            for q in range(4):
                for k in range(KC):
                    for f in range(2):
                        last_t = nc.tensor.transpose(m.ps[q][:, (2 * k + f) * P:(2 * k + f + 1) * P],
                                                     w_nat[:, 2 * q + f, k * P:(k + 1) * P], m.ident[:, :])
                last_t.then_inc(w_turned, 1)
            pe.wait_ge(w_ready, 3)
            nc.tensor.matmul(ps_dots[:, :], m.zeros[:, 0:P], m.zeros[:, 0:INNER], start=True, stop=False)
            with pe.Fori(0, NT) as b:
                first, last = tile_range(pe, b)
                pe.wait_ge(xk_ok, b + 1)
                pe.wait_ge(ks_ok, b)
                pe.wait_ge(v_ok, b)
                for s in range(2):
                    for k in range(KC):
                        kv = nc.tensor.matmul(ps_kv[s][:, :], xk[:, k * P:(k + 1) * P],
                                              w_kv[:, k, s * INNER:(s + 1) * INNER], start=k == 0, stop=k == KC - 1)
                kv.then_inc(kv_ok, 1)
                pe.wait_ge(out_free, b)
                nc.tensor.matmul(ps_out[:, 0:ROW], m.zeros[:, 0:P], m.zeros[:, 0:ROW], start=True,
                                 stop=False).then_inc(opened, 1)
                with pe.Fori(first, last + 1) as i:
                    n = b + i
                    for h in range(2):
                        pe.wait_ge(hot_ok[h], n + 1)
                        pe.wait_ge(hot_back[h], n)
                        for t in range(HT):
                            ins = nc.tensor.transpose(ps_hot[h][:, t * P:(t + 1) * P], hot[h][:, t, :], m.ident[:, :])
                        ins.then_inc(turned_ok[h], 1)
                    for h in range(2):
                        pe.wait_ge(hot_back[h], n + 1)
                        pe.wait_ge(raw_ok[h], n)
                        for t in range(HT):
                            ins = nc.tensor.matmul(src_vals[h][:, t, :], hot_tr[h][:, t, :], m.hlr[:, ds(b * 8, 8)],
                                                   start=True, stop=True)
                        ins.then_inc(src_ok[h], 1)
                    for h in range(2):
                        pe.wait_ge(msg_ok[h], n + 1)
                        for t in range(HT):
                            ins = nc.tensor.matmul(ps_out[:, 0:ROW], hot[h][:, t, :], msg[h][:, t, :], start=False,
                                                   stop=False)
                        ins.then_inc(summed[h], 1)
                nc.tensor.matmul(ps_out[:, 0:ROW], m.zeros[:, 0:P], m.zeros[:, 0:ROW], start=False,
                                 stop=True).then_inc(opened, 1)
                pe.wait_ge(ks_ok, b + 1)
                pe.wait_ge(v_ok, b + 1)
                for j in range(INNER // P):
                    ins = nc.tensor.matmul(ps_dots[:, j * P:(j + 1) * P], v_sb[:, j * P:(j + 1) * P],
                                           ks[:, j * P:(j + 1) * P], start=False, stop=False)
                ins.then_inc(dots_ok, 1)
            nc.tensor.matmul(ps_dots[:, :], m.zeros[:, 0:P], m.zeros[:, 0:INNER], start=False, stop=True)


def mix_and_route(nc, m, Wqkv, Wout, bout, gate_w, gate_b, slots):
    ctx = ExitStack()
    with ctx:
        sem = lambda n: ctx.enter_context(nc.semaphore(n))
        sb = lambda n, s, d=F32: ctx.enter_context(nc.sbuf_tensor(n, s, d))
        w_in, w_ok = sem("m_win"), sem("m_wok")
        step = sem("m_step")
        wq = sb("m_wq", [P, INNER // P, D])
        wo = sb("m_wo", [P, KC, INNER])
        wo_t = sb("m_wot", [P, INNER // P, D])
        dots = sb("m_dots", [P, INNER // P, P])
        dw = sb("m_dw", [P, INNER // P, D])
        mixer = sb("m_mixer", [P, KC, D])
        b_row = sb("m_brow", [1, D])
        g_w = sb("m_gw", [P, KC, EXPERTS])
        g_row = sb("m_grow", [1, EXPERTS])
        xs_ok, mix_ok, added, var_ok, std_ok = sem("m_xs"), sem("m_mix"), sem("m_added"), sem("m_var"), sem("m_std")
        link_v, xn_ok, xt_ok, xts_ok, lg_ok, lg_read, saved = (sem(f"m_{n}") for n in
                                                                ("link", "xn", "xt", "xts", "lg", "lgr", "saved"))
        xs = sb("m_xssb", [P, CT, D])
        xn = sb("m_xnsb", [P, CT, D])
        xts = sb("m_xtsb", [P, CT, D])
        stats = sb("m_stats", [P, CT, 6])
        mv = sb("m_mv", [P, CT, 2])
        var = sb("m_varsb", [P, CT])
        std = sb("m_stdsb", [P, CT])
        rstd = sb("m_rstd", [P, CT])
        logits = sb("m_logits", [P, NT * EXPERTS])
        lg = logits[:, :].rearrange("p (t e) -> p t e", e=EXPERTS)
        big = lambda n: sb(n, [P, NT, EXPERTS])
        pick, wide, excl, ones_t = big("m_pick"), big("m_wide"), big("m_excl"), sb("m_onest", [P, NT])
        total = big("m_total")
        small = lambda n: sb(n, [P, NT])
        peak, first, prob, pos, kept, here, base, far = (small(f"m_{n}") for n in
                                                         ("peak", "first", "prob", "pos", "kept", "here", "base", "far"))
        order = sb("m_order", [P, EXPERTS])
        real = sb("m_real", [P, 1])
        to_slot = sb("m_toslot", [P, NT], I32)
        gate, exp_ok, count_ok, routed = sem("m_gate"), sem("m_exp"), sem("m_count"), sem("m_routed")
        idx = sb("m_idx", [P, CT], I32)
        idx_ok, src_ok, sent = sem("m_idx"), sem("m_src"), sem("m_sent")
        block = ctx.enter_context(nc.Block())

        @block.sync
        def _(sp):
            sp.dma_start(wq[:, :, :], Wqkv[0:INNER, :].rearrange("(j p) c -> p j c", p=P)).then_inc(w_in, 16)
            sp.dma_start(wo[:, :, :], Wout.rearrange("(k p) f -> p k f", p=P)).then_inc(w_in, 16)
            sp.dma_start(b_row[:, :], bout.rearrange("(a n) -> a n", a=1)).then_inc(w_in, 16)
            sp.dma_start(g_w[:, :, :], gate_w.rearrange("(k p) e -> p k e", p=P)).then_inc(w_in, 16)
            sp.dma_start(g_row[:, :], gate_b.rearrange("(a n) -> a n", a=1)).then_inc(w_in, 16)

        @block.tensor
        def _(pe):
            pe.wait_ge(w_in, 80)
            for j in range(INNER // P):
                for k in range(KC):
                    last = nc.tensor.transpose(m.ps[j // 2][:, (j % 2) * D + k * P:(j % 2) * D + (k + 1) * P],
                                               wo[:, k, j * P:(j + 1) * P], m.ident[:, :])
            last.then_inc(w_ok, 1)
            pe.wait_ge(step, 2)
            for j in range(INNER // P):
                last = nc.tensor.matmul(m.ps[2 + j // 2][:, (j % 2) * D:(j % 2 + 1) * D], dots[:, j, :], wo_t[:, j, :],
                                        start=True, stop=True)
            last.then_inc(w_ok, 1)
            pe.wait_ge(step, 3)
            for k in range(KC):
                for j in range(INNER // P):
                    last = nc.tensor.matmul(m.ps[4][:, k * D:(k + 1) * D], wq[:, j, k * P:(k + 1) * P], dw[:, j, :],
                                            start=j == 0, stop=j == INNER // P - 1)
            last.then_inc(w_ok, 1)
            pe.wait_ge(step, 4)
            with pe.Fori(0, CH) as g:
                pe.wait_ge(xs_ok, g + 1)
                for t in range(CT):
                    pe.wait_ge(added, g * CT + max(t - 1, 0))
                    for k in range(KC):
                        nc.tensor.matmul(m.ps[t % 2][:, 0:D], xs[:, t, k * P:(k + 1) * P], mixer[:, k, :],
                                         start=k == 0, stop=False)
                    nc.tensor.matmul(m.ps[t % 2][:, 0:D], m.ones[0:1, :], b_row[0:1, :], start=False,
                                     stop=True).then_inc(mix_ok, 1)
                for t in range(CT + 1):
                    if t < CT:
                        pe.wait_ge(xn_ok, g * CT + t + 1)
                        pe.wait_ge(xts_ok, g * CT + max(t - 1, 0))
                        for k in range(KC):
                            last = nc.tensor.transpose(m.ps[2 + t % 2][:, k * P:(k + 1) * P],
                                                       xn[:, t, k * P:(k + 1) * P], m.ident[:, :])
                        last.then_inc(xt_ok, 1)
                    if t >= 1:
                        q = t - 1
                        pe.wait_ge(xts_ok, g * CT + t)
                        pe.wait_ge(lg_read, g * CT + max(q - 1, 0))
                        for k in range(KC):
                            nc.tensor.matmul(m.ps[4 + q % 2][:, 0:EXPERTS], xts[:, q, k * P:(k + 1) * P], g_w[:, k, :],
                                             start=k == 0, stop=False)
                        nc.tensor.matmul(m.ps[4 + q % 2][:, 0:EXPERTS], m.ones[0:1, :], g_row[0:1, :], start=False,
                                         stop=True).then_inc(lg_ok, 1)
            pe.wait_ge(routed, 1)
            nc.tensor.matmul(m.ps[6][:, 0:NT * EXPERTS], m.tri[:, :], pick[:, :, :].rearrange("p t e -> p (t e)"),
                             start=True, stop=True)
            nc.tensor.matmul(m.ps[7][:, 0:NT * EXPERTS], m.ones[:, :], pick[:, :, :].rearrange("p t e -> p (t e)"),
                             start=True, stop=True).then_inc(count_ok, 1)

        @block.scalar
        def _(act):
            act.wait_ge(w_ok, 1)
            for j in range(2):
                last = nc.scalar.activation(wo_t[:, 2 * j:2 * j + 2, :].rearrange("p j d -> p (j d)"), m.ps[j][:, :],
                                            ACT.Copy)
            last.then_inc(step, 1)
            act.wait_ge(w_ok, 2)
            for j in range(2):
                last = nc.scalar.activation(dw[:, 2 * j:2 * j + 2, :].rearrange("p j d -> p (j d)"), m.ps[2 + j][:, :],
                                            ACT.Copy)
            last.then_inc(step, 1)
            act.wait_ge(w_ok, 3)
            nc.scalar.activation(mixer[:, :, :].rearrange("p k d -> p (k d)"), m.ps[4][:, :], ACT.Copy,
                                 scale=1.0 / NODES).then_inc(step, 1)
            with act.Fori(0, CH) as g:
                act.wait_ge(var_ok, g + 1)
                nc.scalar.activation(std[:, :], var[:, :], ACT.Sqrt).then_inc(std_ok, 1)
                for t in range(CT + 1):
                    if t < CT:
                        act.wait_ge(xt_ok, g * CT + t + 1)
                        act.wait_ge(lg_ok, g * CT)
                        nc.scalar.activation(xts[:, t, :], m.ps[2 + t % 2][:, 0:D], ACT.Copy).then_inc(xts_ok, 1)
                    if t >= 1:
                        act.wait_ge(lg_ok, g * CT + t)
                        nc.scalar.activation(logits[:, ds((g * CT + (t - 1)) * EXPERTS, EXPERTS)],
                                             m.ps[4 + (t - 1) % 2][:, 0:EXPERTS], ACT.Copy).then_inc(lg_read, 1)
            act.wait_ge(gate, 5)
            nc.scalar.activation(wide[:, :, :], wide[:, :, :], ACT.Exp).then_inc(exp_ok, 1)
            with act.Fori(0, CH) as g:
                act.wait_ge(sent, g * (16 * CT))
                act.wait_ge(saved, CH)
                nc.scalar.activation(xs[:, :, :].rearrange("p t d -> p (t d)"), m.xt_all[:, ds(g * CT * D, CT * D)],
                                     ACT.Copy).then_inc(src_ok, 1)

        @block.vector
        def _(dve):
            nc.vector.memset(dots[:, :, :], 0.0).then_inc(link_v, 1)
            dve.wait_ge(link_v, 1)
            pairs = m.ps[7][:, :].rearrange("p (j e) -> p j e", e=P)
            nc.vector.tensor_copy(dots[0:HD, :, 0:HD], pairs[0:HD, :, 0:HD])
            nc.vector.tensor_copy(dots[HD:P, :, HD:P], pairs[HD:P, :, HD:P]).then_inc(step, 1)
            LINKS = 3
            with dve.Fori(0, CH) as g:
                for t in range(CT):
                    dve.wait_ge(mix_ok, g * CT + t + 1)
                    at = ds((g * CT + t) * D, D)
                    nc.vector.tensor_tensor(m.x_all[:, at], m.x_all[:, at], m.ps[t % 2][:, 0:D],
                                            ALU.add).then_inc(added, 1)
                dve.wait_ge(added, (g + 1) * CT)
                dve.sem_inc(m.held, 1)
                for t in range(CT):
                    last = nc.vector.bn_stats(stats[:, t, :], m.x_all[:, ds((g * CT + t) * D, D)])
                last.then_inc(link_v, 1)
                dve.wait_ge(link_v, g * LINKS + 2)
                dve.sem_inc(m.held, 1)
                for t in range(CT):
                    last = nc.vector.bn_aggr(mv[:, t, :], stats[:, t, :])
                last.then_inc(link_v, 1)
                dve.wait_ge(link_v, g * LINKS + 3)
                nc.vector.tensor_scalar(var[:, :], mv[:, :, 1], EPS, None, ALU.add).then_inc(var_ok, 1)
                dve.wait_ge(std_ok, g + 1)
                nc.vector.reciprocal(rstd[:, :], std[:, :]).then_inc(link_v, 1)
                dve.wait_ge(link_v, g * LINKS + 4)
                dve.wait_ge(xt_ok, g * CT)
                dve.wait_ge(saved, g)
                for t in range(CT):
                    nc.vector.tensor_scalar(xn[:, t, :], m.x_all[:, ds((g * CT + t) * D, D)], mv[:, t, 0:1],
                                            rstd[:, t:t + 1], ALU.subtract, ALU.mult).then_inc(xn_ok, 1)
            done = [0]

            def then(ins):
                ins.then_inc(gate, 1)
                done[0] += 1
                dve.wait_ge(gate, done[0])

            wide3 = lambda a: a[:, :].unsqueeze(2).to_broadcast([P, NT, EXPERTS])
            dve.wait_ge(lg_read, NT)
            nc.vector.tensor_scalar(order[:, :], m.iota[:, 0:EXPERTS], -1.0, float(EXPERTS), ALU.mult, ALU.add)
            nc.vector.memset(ones_t[:, :], 1.0)
            nc.vector.tensor_scalar(real[:, :], m.lane[:, :], float(LAST), None, ALU.is_lt)
            then(nc.vector.tensor_reduce(peak[:, :], lg, AX, ALU.max))
            then(nc.vector.tensor_tensor(pick[:, :, :], lg, wide3(peak), ALU.is_equal))
            then(nc.vector.tensor_tensor(pick[:, :, :], pick[:, :, :],
                                         order[:, :].unsqueeze(1).to_broadcast([P, NT, EXPERTS]), ALU.mult))
            then(nc.vector.tensor_reduce(first[:, :], pick[:, :, :], AX, ALU.max))
            then(nc.vector.tensor_tensor(wide[:, :, :], lg, wide3(peak), ALU.subtract))
            then(nc.vector.tensor_tensor(pick[:, :, :], order[:, :].unsqueeze(1).to_broadcast([P, NT, EXPERTS]),
                                         wide3(first), ALU.is_equal))
            nc.vector.tensor_scalar(pick[:, NT - 1, :], pick[:, NT - 1, :], real[:, 0:1], None,
                                    ALU.mult).then_inc(routed, 1)
            dve.wait_ge(routed, 1)
            dve.wait_ge(exp_ok, 1)
            then(nc.vector.tensor_reduce(prob[:, :], wide[:, :, :], AX, ALU.add))
            nc.vector.reciprocal(prob[:, :], prob[:, :])
            nc.vector.tensor_reduce(here[:, :], pick[:, :, :], AX, ALU.add)
            dve.wait_ge(count_ok, 1)
            then(nc.vector.tensor_copy(total[:, :, :].rearrange("p t e -> p (t e)"), m.ps[7][:, 0:NT * EXPERTS]))
            for e in range(EXPERTS):
                last = nc.vector.tensor_tensor_scan(excl[:, :, e], ones_t[:, :], total[:, :, e], 0.0, ALU.mult, ALU.add)
            then(last)
            then(nc.vector.tensor_tensor(excl[:, :, :], excl[:, :, :], total[:, :, :], ALU.subtract))
            then(nc.vector.tensor_tensor(excl[:, :, :].rearrange("p t e -> p (t e)"),
                                         excl[:, :, :].rearrange("p t e -> p (t e)"), m.ps[6][:, 0:NT * EXPERTS],
                                         ALU.add))
            then(nc.vector.tensor_tensor(excl[:, :, :], excl[:, :, :], pick[:, :, :], ALU.mult))
            then(nc.vector.tensor_reduce(pos[:, :], excl[:, :, :], AX, ALU.add))
            then(nc.vector.tensor_scalar(pos[:, :], pos[:, :], -1.0, None, ALU.add))
            then(nc.vector.tensor_scalar(kept[:, :], pos[:, :], float(CAP), None, ALU.is_lt))
            then(nc.vector.tensor_tensor(kept[:, :], kept[:, :], here[:, :], ALU.mult))
            nc.vector.tensor_tensor(m.weight[:, :], prob[:, :], kept[:, :], ALU.mult)
            then(nc.vector.tensor_scalar(base[:, :], first[:, :], float(-CAP), float(CAP * EXPERTS), ALU.mult, ALU.add))
            then(nc.vector.tensor_scalar(far[:, :], kept[:, :], -1e6, 1e6, ALU.mult, ALU.add))
            then(nc.vector.tensor_tensor(far[:, :], far[:, :], base[:, :], ALU.add))
            then(nc.vector.tensor_tensor(far[:, :], far[:, :], pos[:, :], ALU.add))
            nc.vector.tensor_copy(to_slot[:, :], far[:, :])
            then(nc.vector.tensor_scalar(pos[:, :], pos[:, :], float(CAP - 1), 0.0, ALU.min, ALU.max))
            then(nc.vector.tensor_tensor(pos[:, :], pos[:, :], base[:, :], ALU.add))
            nc.vector.tensor_copy(m.from_slot[:, :], pos[:, :]).then_inc(routed, 1)

        @block.gpsimd
        def _(pool):
            with pool.Fori(0, CH) as g:
                pool.wait_ge(mix_ok, g * CT)
                pool.sem_inc(m.held, 1)
                nc.gpsimd.tensor_copy(xs[:, :, :].rearrange("p t d -> p (t d)"),
                                      m.xt_all[:, ds(g * CT * D, CT * D)]).then_inc(xs_ok, 1)
                pool.wait_ge(xn_ok, (g + 1) * CT)
                pool.sem_inc(m.held, 1)
                nc.gpsimd.tensor_copy(m.xt_all[:, ds(g * CT * D, CT * D)],
                                      xn[:, :, :].rearrange("p t d -> p (t d)")).then_inc(saved, 1)
            pool.wait_ge(routed, 2)
            with pool.Fori(0, CH) as g:
                pool.wait_ge(sent, g * (16 * CT))
                pool.sem_inc(m.held, 1)
                nc.gpsimd.tensor_copy(idx[:, :], to_slot[:, ds(g * CT, CT)]).then_inc(idx_ok, 1)
                pool.wait_ge(idx_ok, g + 1)
                pool.wait_ge(src_ok, g + 1)
                pool.sem_inc(m.held, 1)
                for t in range(CT):
                    nc.gpsimd.indirect_dma_start(
                        out=slots, out_offset=bass.IndirectOffsetOnAxis(ap=idx[:, t:t + 1], axis=0),
                        in_=xs[:, t, :], in_offset=None, bounds_check=EXPERTS * CAP - 1,
                        oob_is_err=False).then_inc(sent, 16)
            pool.wait_ge(sent, 16 * NT)


def experts(nc, m, slots, w1, b1, w2, b2, results):
    ctx = ExitStack()
    with ctx:
        sem = lambda n: ctx.enter_context(nc.semaphore(n))
        sb = lambda n, s, d=F32: ctx.enter_context(nc.sbuf_tensor(n, s, d))
        ST = -(-CAP // P)
        FULL = CAP // P
        TAIL = CAP - FULL * P
        FT = FF // P
        size = lambda j: P if j < FULL else TAIL
        halves = [(0, 512), (512, CAP - 512)]
        b_in, b_turned, b_ok = sem("f_bin"), sem("f_bturn"), sem("f_bok")
        loaded = [sem(f"f_load{q}") for q in range(2)]
        stored = [sem(f"f_store{q}") for q in range(2)]
        turned, turned_ok, mid, mid_ok, y_ok, y_out = (sem(f"f_{n}") for n in
                                                       ("turn", "turnok", "mid", "midok", "y", "yout"))
        b1_nat = sb("f_b1n", [EXPERTS * FT, P])
        b1_t = sb("f_b1t", [P, EXPERTS * FT])
        b2_row = sb("f_b2", [1, EXPERTS * D])
        w1_sb = [sb(f"f_w1{q}", [P, KC, FF]) for q in range(2)]
        w2_sb = [sb(f"f_w2{q}", [P, FT, D]) for q in range(2)]
        rows = [sb(f"f_rows{q}", [P, ST, D]) for q in range(2)]
        rows_t = [sb(f"f_rowst{q}", [P, KC, CAP]) for q in range(2)]
        hidden = sb("f_hidden", [P, FT, CAP])
        y_sb = [sb(f"f_y{q}", [P, ST, D]) for q in range(2)]
        block = ctx.enter_context(nc.Block())

        @block.sync
        def _(sp):
            sp.dma_start(b1_nat[:, :], b1.rearrange("e (f p) -> (e f) p", p=P)).then_inc(b_in, 16)
            sp.dma_start(b2_row[:, :], b2.rearrange("e d -> (e d)").rearrange("(a n) -> a n", a=1)).then_inc(b_in, 16)

            def store(e, q):
                sp.wait_ge(y_out, (e + 1) * ST)
                sp.dma_start(results[ds(e * CAP, FULL * P), :].rearrange("(j p) d -> p j d", p=P),
                             y_sb[q][:, 0:FULL, :]).then_inc(stored[q], 16)
                sp.dma_start(results[ds(e * CAP + FULL * P, TAIL), :],
                             y_sb[q][0:TAIL, FULL, :]).then_inc(stored[q], 16)

            with sp.Fori(0, EXPERTS // 2) as pair:
                for q in range(2):
                    e = pair * 2 + q
                    sp.wait_ge(y_ok, pair * (2 * ST))
                    sp.dma_start(w1_sb[q][:, :, :], w1[ds(e, 1), :, :].rearrange("e (k p) f -> p (e k) f", p=P)
                                 ).then_inc(loaded[q], 16)
                    sp.dma_start(w2_sb[q][:, :, :], w2[ds(e, 1), :, :].rearrange("e (f p) d -> p (e f) d", p=P)
                                 ).then_inc(loaded[q], 16)
                    sp.dma_start(rows[q][:, 0:FULL, :], slots[ds(e * CAP, FULL * P), :].rearrange(
                        "(j p) d -> p j d", p=P)).then_inc(loaded[q], 16)
                    sp.dma_start(rows[q][0:TAIL, FULL, :], slots[ds(e * CAP + FULL * P, TAIL), :]).then_inc(loaded[q], 16)
                for q in range(2):
                    store(pair * 2 + q, q)
            for q in range(2):
                sp.wait_ge(stored[q], 32 * (EXPERTS // 2))

        @block.tensor
        def _(pe):
            pe.wait_ge(b_in, 32)
            nc.tensor.transpose(m.ps[0][:, 0:EXPERTS * FT], b1_nat[:, :],
                                m.ident[0:EXPERTS * FT, 0:EXPERTS * FT]).then_inc(b_turned, 1)
            pe.wait_ge(b_ok, 1)
            with pe.Fori(0, EXPERTS // 2) as pair:
                for q in range(2):
                    e = pair * 2 + q
                    pe.wait_ge(loaded[q], (pair + 1) * 64)
                    for j in range(ST):
                        pe.wait_ge(turned_ok, e * ST + max(j - 1, 0))
                        n = size(j)
                        for k in range(KC):
                            last = nc.tensor.transpose(m.ps[j % 2][:, k * P:k * P + n],
                                                       rows[q][0:n, j, k * P:(k + 1) * P], m.ident[0:n, 0:n])
                        last.then_inc(turned, 1)
                    pe.wait_ge(turned_ok, (e + 1) * ST)
                    for f in range(FT):
                        for s, (at, w) in enumerate(halves):
                            n = 2 * f + s
                            pe.wait_ge(mid_ok, e * (2 * FT) + max(n - 3, 0))
                            for k in range(KC):
                                last = nc.tensor.matmul(m.ps[2 + n % 4][:, 0:w], w1_sb[q][:, k, f * P:(f + 1) * P],
                                                        rows_t[q][:, k, at:at + w], start=k == 0, stop=k == KC - 1)
                            last.then_inc(mid, 1)
                    pe.wait_ge(mid_ok, (e + 1) * (2 * FT))
                    for j in range(ST):
                        n = size(j)
                        pe.wait_ge(y_out, e * ST + max(j - 1, 0))
                        for f in range(FT):
                            nc.tensor.matmul(m.ps[6 + j % 2][0:n, 0:D], hidden[:, f, j * P:j * P + n],
                                             w2_sb[q][:, f, :], start=f == 0, stop=False)
                        nc.tensor.matmul(m.ps[6 + j % 2][0:n, 0:D], m.ones[0:1, 0:n], b2_row[0:1, ds(e * D, D)],
                                         start=False, stop=True).then_inc(y_ok, 1)

        @block.scalar
        def _(act):
            act.wait_ge(b_turned, 1)
            nc.scalar.activation(b1_t[:, :], m.ps[0][:, 0:EXPERTS * FT], ACT.Copy).then_inc(b_ok, 1)
            act.wait_ge(b_ok, 1)
            with act.Fori(0, EXPERTS // 2) as pair:
                for q in range(2):
                    e = pair * 2 + q
                    act.wait_ge(y_ok, e * ST)
                    for f in range(FT):
                        for s, (at, w) in enumerate(halves):
                            n = 2 * f + s
                            act.wait_ge(mid, e * (2 * FT) + (n + 1))
                            act.sem_inc(m.held, 1)
                            nc.scalar.activation(hidden[:, f, at:at + w], m.ps[2 + n % 4][:, 0:w], ACT.Relu,
                                                 bias=b1_t[:, ds(e * FT + f, 1)]).then_inc(mid_ok, 1)

        @block.vector
        def _(dve):
            with dve.Fori(0, EXPERTS // 2) as pair:
                for q in range(2):
                    e = pair * 2 + q
                    for j in range(ST):
                        n = size(j)
                        dve.wait_ge(turned, e * ST + (j + 1))
                        nc.vector.tensor_copy(rows_t[q][:, :, j * P:j * P + n],
                                              m.ps[j % 2][:, 0:KC * P].rearrange("p (k s) -> p k s", k=KC)[:, :, 0:n]
                                              ).then_inc(turned_ok, 1)
                    dve.wait_ge(stored[q], pair * 32)
                    for j in range(ST):
                        n = size(j)
                        dve.wait_ge(y_ok, e * ST + (j + 1))
                        dve.sem_inc(m.held, 1)
                        nc.vector.tensor_copy(y_sb[q][0:n, j, :], m.ps[6 + j % 2][0:n, 0:D]).then_inc(y_out, 1)


def combine(nc, m, results, out):
    ctx = ExitStack()
    with ctx:
        sem = lambda n: ctx.enter_context(nc.semaphore(n))
        sb = lambda n, s, d=F32: ctx.enter_context(nc.sbuf_tensor(n, s, d))
        FMAX = 3.4028234e38
        landed = [sem(f"o_land{t}") for t in range(CT)]
        free, idx_ok, link_v, cleared, left = sem("o_free"), sem("o_idx"), sem("o_link"), sem("o_clr"), sem("o_left")
        added = sem("o_added")
        idx = sb("o_idxsb", [P, CT], I32)
        y = sb("o_y", [P, CT, D])
        safe = sb("o_safe", [P, 2, D])
        inf = sb("o_inf", [P, 2, D])
        fin = sb("o_fin", [P, D], I32)
        block = ctx.enter_context(nc.Block())

        @block.gpsimd
        def _(pool):
            with pool.Fori(0, CH) as g:
                pool.wait_ge(added, g * CT)
                pool.sem_inc(m.held, 1)
                nc.gpsimd.tensor_copy(idx[:, :], m.from_slot[:, ds(g * CT, CT)]).then_inc(idx_ok, 1)
                pool.wait_ge(idx_ok, g + 1)
                pool.sem_inc(m.held, 1)
                for t in range(CT):
                    nc.gpsimd.indirect_dma_start(
                        out=y[:, t, :], out_offset=None, in_=results,
                        in_offset=bass.IndirectOffsetOnAxis(ap=idx[:, t:t + 1], axis=0)).then_inc(landed[t], 16)

        @block.vector
        def _(dve):
            LINKS = 5
            with dve.Fori(0, CH) as g:
                for t in range(CT):
                    n = g * CT + t
                    dve.wait_ge(landed[t], (g + 1) * 16)
                    dve.wait_ge(added, n)
                    nc.vector.memset(safe[:, 0, :], 0.0)
                    nc.vector.tensor_scalar(y[:, t, :], y[:, t, :], m.weight[:, ds(n, 1)], None,
                                            ALU.mult).then_inc(link_v, 1)
                    dve.wait_ge(link_v, n * LINKS + 1)
                    nc.vector.tensor_scalar(fin[:, :], y[:, t, :], 0.0, 0.0, ALU.mult, ALU.is_equal)
                    nc.vector.tensor_scalar(inf[:, 0, :], y[:, t, :], FMAX, 1e4, ALU.is_gt, ALU.mult)
                    nc.vector.tensor_scalar(inf[:, 1, :], y[:, t, :], -FMAX, -1e4, ALU.is_lt,
                                            ALU.mult).then_inc(link_v, 1)
                    dve.wait_ge(link_v, n * LINKS + 2)
                    dve.sem_inc(m.held, 1)
                    nc.vector.copy_predicated(safe[:, 0, :], fin[:, :], y[:, t, :])
                    nc.vector.tensor_tensor(inf[:, 0, :], inf[:, 0, :], inf[:, 1, :], ALU.add).then_inc(link_v, 1)
                    dve.wait_ge(link_v, n * LINKS + 3)
                    nc.vector.tensor_tensor(safe[:, 0, :], safe[:, 0, :], inf[:, 0, :], ALU.add).then_inc(link_v, 1)
                    dve.wait_ge(link_v, n * LINKS + 4)
                    nc.vector.tensor_tensor(m.x_all[:, ds(n * D, D)], m.x_all[:, ds(n * D, D)], safe[:, 0, :],
                                            ALU.add).then_inc(added, 1)
                    nc.vector.engine_nop().then_inc(link_v, 1)

        @block.sync
        def _(sp):
            rows = out[0:(NT - 1) * P, :].rearrange("(t p) c -> p t c", p=P)
            for g in range(CH):
                n = CT if g < CH - 1 else CT - 1
                sp.wait_ge(added, (g + 1) * CT)
                sp.dma_start(rows[:, g * CT:g * CT + n, :],
                             m.x_all[:, g * CT * D:(g * CT + n) * D].rearrange("p (t c) -> p t c", c=D)
                             ).then_inc(left, 16)
            sp.dma_start(out[(NT - 1) * P:NODES, :], m.x_all[0:LAST, (NT - 1) * D:NT * D]).then_inc(left, 16)
            sp.wait_ge(left, 16 * (CH + 1))


class Memory:

    def __init__(self, nc, ctx):
        def sb(n, s, d=F32):
            return ctx.enter_context(nc.sbuf_tensor(n, s, d))

        self.ident = sb("ident", [P, P])
        self.ones = sb("ones", [P, P])
        self.tri = sb("tri", [P, P])
        self.zeros = sb("zeros", [P, INNER])
        self.lane = sb("lane", [P, 1], I32)
        self.iota = sb("iota", [P, P])
        self.iota_row = sb("iota_row", [1, GROUPS])
        self.x_all = sb("x_all", [P, NT * D])
        self.hlr = sb("hlr", [P, NT * 2 * HEADS])
        self.first_group = sb("first_group", [P, NT + 1], I32)
        self.needed = sb("needed", [1, GROUPS], I32)
        self.weight = sb("weight", [P, NT])
        self.from_slot = sb("from_slot", [P, NT], I32)
        self.ps = [ctx.enter_context(nc.psum_tensor(f"ps{i}", [P, 512], F32)) for i in range(8)]
        self.held = ctx.enter_context(nc.semaphore("held"))


def gps_layer(nc, x, src, dst, W, a_l, a_r, Wqkv, Wout, bout, gate_w, gate_b, w1, b1, w2, b2, out):
    table = nc.dram_tensor("node_table", [NT * P, ROW], F32).ap()
    slots = nc.dram_tensor("expert_slots", [EXPERTS * CAP, D], F32).ap()
    results = nc.dram_tensor("expert_results", [EXPERTS * CAP, D], F32).ap()
    ctx = ExitStack()
    with ctx:
        m = Memory(nc, ctx)
        m.table = table
        setup_consts(nc, m)
        with nc.sbuf_tensor("xt_all", [P, NT * D], F32) as m.xt_all:
            with nc.sbuf_tensor("src_of", [P, ET], F32) as m.src_of, nc.sbuf_tensor("dst_of", [P, ET], I32) as m.dst_of:
                node_rows(nc, m, x, W, a_l, a_r, slots)
                edge_sort(nc, m, src, dst)
                attention_steps(nc, m, Wqkv)
            mix_and_route(nc, m, Wqkv, Wout, bout, gate_w, gate_b, slots)
        experts(nc, m, slots, w1, b1, w2, b2, results)
        combine(nc, m, results, out)


_INS = ["x", "src", "dst", "L0_gnn_W", "L0_gnn_a_l", "L0_gnn_a_r", "L0_mix_Wqkv", "L0_mix_Wout", "L0_mix_bout",
        "L0_ffn_gate_w", "L0_ffn_gate_b", "L0_ffn_w1", "L0_ffn_b1", "L0_ffn_w2", "L0_ffn_b2"]


def kernel(**inputs):
    import numpy as _np
    import concourse.bacc as _bacc
    from concourse import mybir as _mybir
    from concourse.bass_utils import run_bass_kernel_spmd as _run

    nc = _bacc.Bacc("TRN2", target_bir_lowering=False, num_devices=1)
    arrays, args = {}, []
    for name in _INS:
        a = _np.ascontiguousarray(inputs[name])
        arrays[f"in_{name}"] = a
        args.append(nc.dram_tensor(f"in_{name}", a.shape, _mybir.dt.from_np(a.dtype), kind="ExternalInput").ap())
    out = nc.dram_tensor("out_x", (NODES, D), F32, kind="ExternalOutput").ap()
    gps_layer(nc, *args, out)
    r = _run(nc, [arrays], core_ids=[0])
    return r.results[0]["out_x"]
```

```python
from contextlib import ExitStack

import concourse.bass as bass
from concourse import mybir

F32 = mybir.dt.float32
I32 = mybir.dt.int32
BF16 = mybir.dt.bfloat16
ALU = mybir.AluOpType
ACT = mybir.ActivationFunctionType
AX = mybir.AxisListType.X
RMAX = bass.bass_isa.ReduceOp.max
ds = bass.ds

P = 128
NODES, D, EDGES = 6250, 256, 200000
HEADS, HD = 4, 64
MH, INNER = 8, 512
EXPERTS, FF = 8, 1024
CAP = -(-5 * NODES // (4 * EXPERTS))
ALPHA, EPS = 0.2, 1e-5

NT = -(-NODES // P)
CT = 7
CH = NT // CT
LAST = NODES - (NT - 1) * P
KC = D // P

ROW = D + HEADS

DB = 13
KEY_ONE = 1 << 29
PAD_SRC = (1 << DB) - 1
LB = 11
COLS = 1 << LB
SHORT = EDGES // P
REST = EDGES - SHORT * P

GT, HT = 8, 4
GROUPS = -(-EDGES // (GT * P))
ET = GROUPS * GT
RING = 4

PASS = 4
HOTS = 4
STEPS = -(-(EDGES // (GT * P) + NT) // PASS) * PASS
AHEAD = STEPS + HOTS - NT - GROUPS
PARTS = 3
BETWEEN = 2
KVT = NT + 1
PRIME = 16


def setup_consts(nc, m):
    ctx = ExitStack()
    with ctx:
        made = ctx.enter_context(nc.semaphore("c_made"))
        block = ctx.enter_context(nc.Block())

        @block.gpsimd
        def _(pool):
            nc.gpsimd.memset(m.ident[:, :], 0.0).then_inc(made, 1)
            nc.gpsimd.memset(m.ones[:, :], 1.0)
            nc.gpsimd.memset(m.tri[:, :], 1.0).then_inc(made, 1)
            nc.gpsimd.memset(m.zeros[:, :], 0.0)
            nc.gpsimd.iota(m.lane[:, :], [[0, 1]], base=0, channel_multiplier=1)
            nc.gpsimd.iota(m.iota[:, :], [[1, P]], base=0, channel_multiplier=0,
                           allow_small_or_imprecise_dtypes=True)
            nc.gpsimd.iota(m.iota_row[:, :], [[1, STEPS + HOTS]], base=0, channel_multiplier=0,
                           allow_small_or_imprecise_dtypes=True)
            pool.wait_ge(made, 2)
            nc.gpsimd.affine_select(out=m.ident[:, :], in_=m.ident[:, :], compare_op=ALU.not_equal, fill=1.0,
                                    base=0, pattern=[[-1, P]], channel_multiplier=1)
            nc.gpsimd.affine_select(out=m.tri[:, :], in_=m.tri[:, :], compare_op=ALU.is_ge, fill=0.0,
                                    base=0, pattern=[[1, P]], channel_multiplier=-1)


def node_rows(nc, m, x, W, a_l, a_r, slots):
    ctx = ExitStack()
    with ctx:
        sem = lambda n: ctx.enter_context(nc.semaphore(n))
        sb = lambda n, s, d=F32: ctx.enter_context(nc.sbuf_tensor(n, s, d))
        x_in = [sem(f"n_x{g}") for g in range(CH)]
        w_in, a_in = sem("n_w"), sem("n_a")
        link_v, var_ok, std_ok = sem("n_link"), sem("n_var"), sem("n_std")
        xn_ok, xt_ok, xs_ok, saved = sem("n_xn"), sem("n_xt"), sem("n_xs"), sem("n_saved")
        h_ok, h_copied, cleared = sem("n_h"), sem("n_hc"), sem("n_clr")
        mulled, row_ok, row_out, zeroed = sem("n_mul"), sem("n_row"), sem("n_out"), sem("n_zero")
        hr_max, all_max = sem("n_hrmax"), sem("n_allmax")
        padded = sem("n_pad")
        w_sb = sb("n_wsb", [P, KC, D])
        x_all = m.acc[:, 0:NT * D]
        a_sb = sb("n_asb", [P, 2, D])
        stats = sb("n_stats", [P, CT, 6])
        mv = sb("n_mv", [P, CT, 2])
        std = sb("n_stdsb", [P, CT])
        rstd = sb("n_rstd", [P, CT])
        xn = sb("n_xnsb", [P, CT, D])
        xs = sb("n_xssb", [P, CT, D])
        hc = sb("n_hcsb", [P, CT, D])
        mask = sb("n_mask", [P, CT, D], I32)
        row = sb("n_rowsb", [P, CT, ROW])
        prod = sb("n_prod", [P, CT, 2, D])
        zrow = sb("n_zrow", [P, 2048])
        peak = sb("n_peak", [P, HEADS])
        top = sb("n_top", [P, HEADS])
        psx, psh = m.ps[0:2], m.ps[2:4]
        zw = slots.shape[0] * D // P
        slots_flat = slots.rearrange("s d -> (s d)").rearrange("(p f) -> p f", p=P)
        nz = -(-zw // 2048)
        block = ctx.enter_context(nc.Block())

        @block.sync
        def _(sp):
            xt = x[0:(NT - 1) * P, :].rearrange("(t p) c -> p t c", p=P)
            sp.dma_start(w_sb[:, :, :], W.rearrange("(k p) f -> p k f", p=P)).then_inc(w_in, 16)
            sp.wait_ge(padded, 1)
            for g in range(CH):
                n = CT if g < CH - 1 else CT - 1
                dst = x_all[:, g * CT * D:(g * CT + n) * D].rearrange("p (t c) -> p t c", c=D)
                sp.dma_start(dst, xt[:, g * CT:g * CT + n, :]).then_inc(x_in[g], 16)
            sp.dma_start(x_all[0:LAST, (NT - 1) * D:NT * D], x[(NT - 1) * P:NODES, :]).then_inc(x_in[CH - 1], 16)
            sp.dma_start(a_sb[:, 0, :], a_l.rearrange("o h d -> o (h d)").to_broadcast([P, D])).then_inc(a_in, 16)
            sp.dma_start(a_sb[:, 1, :], a_r.rearrange("o h d -> o (h d)").to_broadcast([P, D])).then_inc(a_in, 16)
            sp.wait_ge(padded, 2)
            for k in range(nz):
                w = min(2048, zw - k * 2048)
                sp.dma_start(slots_flat[:, k * 2048:k * 2048 + w], zrow[:, 0:w]).then_inc(zeroed, 16)
            table = m.table.rearrange("(t p) c -> p t c", p=P)
            with sp.Fori(0, CH) as g:
                sp.wait_ge(row_ok, g + 1)
                sp.dma_start(table[:, ds(g * CT, CT), :], row[:, :, :]).then_inc(row_out, 16)
            sp.wait_ge(row_out, 16 * CH)
            sp.wait_ge(zeroed, 16 * nz)

        @block.vector
        def _(dve):
            n = [0]

            def link(ins):
                n[0] += 1
                ins.then_inc(link_v, 1)

            nc.vector.memset(x_all[:, (NT - 1) * D:NT * D], 0.0).then_inc(padded, 1)
            nc.vector.memset(m.hlr[:, NT * 8:(NT + 1) * 8], 0.0)
            nc.vector.memset(m.xt_all[:, NT * D:(NT + 2) * D], 0.0)
            nc.vector.memset(zrow[:, :], 0.0).then_inc(padded, 1)
            dve.wait_ge(a_in, 32)
            LINKS = 7
            for q in range(CH):
                dve.wait_ge(x_in[q], 16 if q < CH - 1 else 32)
            with dve.Fori(0, CH) as g:
                base = g * LINKS
                for k in range(CT):
                    last = nc.vector.bn_stats(stats[:, k, :], x_all[:, ds((g * CT + k) * D, D)])
                last.then_inc(link_v, 1)
                dve.wait_ge(link_v, base + 1)
                dve.sem_inc(m.held, 1)
                for k in range(CT):
                    last = nc.vector.bn_aggr(mv[:, k, :], stats[:, k, :])
                last.then_inc(link_v, 1)
                dve.wait_ge(link_v, base + 2)
                nc.vector.tensor_scalar(rstd[:, :], mv[:, :, 1], EPS, None, ALU.add).then_inc(var_ok, 1)
                dve.wait_ge(std_ok, g + 1)
                nc.vector.reciprocal(rstd[:, :], std[:, :]).then_inc(link_v, 1)
                dve.wait_ge(link_v, base + 3)
                dve.wait_ge(xt_ok, g * CT)
                for k in range(CT):
                    nc.vector.tensor_scalar(xn[:, k, :], x_all[:, ds((g * CT + k) * D, D)], mv[:, k, 0:1],
                                            rstd[:, k:k + 1], ALU.subtract, ALU.mult).then_inc(xn_ok, 1)
                dve.wait_ge(h_copied, (g + 1) * CT)
                nc.vector.tensor_tensor(mask[:, :, :], hc[:, :, :], hc[:, :, :], ALU.is_equal).then_inc(link_v, 1)
                dve.wait_ge(link_v, base + 4)
                dve.wait_ge(cleared, g + 1)
                dve.sem_inc(m.held, 1)
                nc.vector.copy_predicated(row[:, :, 0:D], mask[:, :, :], hc[:, :, :]).then_inc(link_v, 1)
                dve.wait_ge(link_v, base + 5)
                nc.vector.tensor_tensor(prod[:, :, 0, :], row[:, :, 0:D],
                                        a_sb[:, 0:1, :].to_broadcast([P, CT, D]), ALU.mult)
                nc.vector.tensor_tensor(prod[:, :, 1, :], row[:, :, 0:D],
                                        a_sb[:, 1:2, :].to_broadcast([P, CT, D]), ALU.mult).then_inc(link_v, 1)
                dve.wait_ge(link_v, base + 6)
                logits = m.hlr[:, ds(g * CT * 8, CT * 8)].rearrange("p (t c) -> p t c", c=8)
                for s in range(2):
                    last = nc.vector.tensor_reduce(logits[:, :, 4 * s:4 * s + 4],
                                                   prod[:, :, s, :].rearrange("p t (h d) -> p t h d", h=HEADS),
                                                   AX, ALU.add)
                last.then_inc(link_v, 1)
                dve.wait_ge(link_v, base + 7)
                dve.sem_inc(m.held, 1)
                nc.vector.tensor_copy(row[:, :, D:ROW], logits[:, :, 4:8]).then_inc(row_ok, 1)
            hl = m.hlr[:, 0:NT * 8].rearrange("p (t c) -> p t c", c=8)
            nc.vector.tensor_reduce(peak[:, :], hl[:, :, 4:8].rearrange("p t h -> p h t"), AX,
                                    ALU.max).then_inc(hr_max, 1)
            dve.wait_ge(all_max, 1)
            total = LINKS * CH
            nc.vector.tensor_tensor(hl[:, :, 4:8], hl[:, :, 0:4],
                                    top[:, :].unsqueeze(1).to_broadcast([P, NT, HEADS]), ALU.add).then_inc(link_v, 1)
            dve.wait_ge(link_v, total + 1)
            nc.vector.scalar_tensor_tensor(out=hl[:, :, 4:8], in0=hl[:, :, 4:8], scalar=ALPHA, in1=hl[:, :, 4:8],
                                           op0=ALU.mult, op1=ALU.max).then_inc(link_v, 1)
            dve.wait_ge(link_v, total + 2)
            parts = m.src_parts[:, :].rearrange("p (v s) -> p v s", s=PARTS)
            for s in range(PARTS):
                nc.vector.tensor_copy(parts[:, :, s], m.hlr[:, :]).then_inc(link_v, 1)
                dve.wait_ge(link_v, total + 3 + 2 * s)
                if s < PARTS - 1:
                    nc.vector.tensor_tensor(m.hlr[:, :], m.hlr[:, :], parts[:, :, s], ALU.subtract).then_inc(link_v, 1)
                    dve.wait_ge(link_v, total + 4 + 2 * s)

        @block.scalar
        def _(act):
            with act.Fori(0, CH) as g:
                act.wait_ge(var_ok, g + 1)
                nc.scalar.activation(std[:, :], rstd[:, :], ACT.Sqrt).then_inc(std_ok, 1)
                for k in range(CT):
                    act.wait_ge(xt_ok, g * CT + k + 1)
                    act.wait_ge(h_ok, g * CT)
                    act.wait_ge(saved, g)
                    nc.scalar.activation(xs[:, k, :], psx[k % 2][:, 0:D], ACT.Copy).then_inc(xs_ok, 1)
                    if k >= 1:
                        act.wait_ge(h_ok, g * CT + k)
                        nc.scalar.activation(hc[:, k - 1, :], psh[(k - 1) % 2][:, 0:D], ACT.Copy).then_inc(h_copied, 1)
                act.wait_ge(h_ok, g * CT + CT)
                nc.scalar.activation(hc[:, CT - 1, :], psh[(CT - 1) % 2][:, 0:D], ACT.Copy).then_inc(h_copied, 1)

        @block.tensor
        def _(pe):
            pe.wait_ge(w_in, 16)
            with pe.Fori(0, CH) as g:
                for k in range(CT + 1):
                    if k < CT:
                        pe.wait_ge(xn_ok, g * CT + k + 1)
                        pe.wait_ge(xs_ok, g * CT + max(k - 1, 0))
                        for c in range(KC):
                            last = nc.tensor.transpose(psx[k % 2][:, c * P:(c + 1) * P], xn[:, k, c * P:(c + 1) * P],
                                                       m.ident[:, :])
                        last.then_inc(xt_ok, 1)
                    if k >= 1:
                        pe.wait_ge(xs_ok, g * CT + k)
                        pe.wait_ge(h_copied, g * CT + max(k - 2, 0))
                        for c in range(KC):
                            last = nc.tensor.matmul(psh[(k - 1) % 2][:, 0:D], xs[:, k - 1, c * P:(c + 1) * P],
                                                    w_sb[:, c, :], start=c == 0, stop=c == KC - 1)
                        last.then_inc(h_ok, 1)

        @block.gpsimd
        def _(pool):
            with pool.Fori(0, CH) as g:
                pool.wait_ge(row_out, 16 * g)
                pool.sem_inc(m.held, 1)
                nc.gpsimd.memset(row[:, :, 0:D], 0.0).then_inc(cleared, 1)
                pool.wait_ge(xs_ok, (g + 1) * CT)
                nc.gpsimd.tensor_copy(m.xt_all[:, ds(g * CT * D, CT * D)],
                                      xs[:, :, :].rearrange("p t c -> p (t c)")).then_inc(saved, 1)
            pool.wait_ge(hr_max, 1)
            nc.gpsimd.partition_all_reduce(top[:, :], peak[:, :], P, RMAX).then_inc(all_max, 1)


def edge_sort(nc, m, src, dst, Wqkv):
    ctx = ExitStack()
    with ctx:
        sem = lambda n: ctx.enter_context(nc.semaphore(n))
        sb = lambda n, s, d=F32: ctx.enter_context(nc.sbuf_tensor(n, s, d))
        loaded, stage_done, turned = sem("s_load"), sem("s_stage"), sem("s_turn")
        keys = [sb("s_keys0", [P, COLS]), sb("s_keys1", [P, COLS])]
        src_sb, dst_sb = sb("s_src", [P, COLS], I32), sb("s_dst", [P, COLS], I32)
        bits = sb("s_bits", [P, 8], I32)
        sign = sb("s_sign", [P, 8])
        turn = sb("s_turns", [P, 8])
        code = sb("s_code", [P, ET], I32)
        last_src = sb("s_last", [P, 2])
        last_int = sb("s_lasti", [P, 2], I32)
        bound = sb("s_bound", [P, NT + 1])
        below = sb("s_below", [P, NT + 1, 2])
        belows = sb("s_belows", [P, NT + 1])
        lo_f = sb("s_lof", [P, NT + 1])
        item = sb("s_item", [P, 2])
        first_step = sb("s_fstep", [P, NT + 1])
        begun = sb("s_begun", [P, 2, 2, NT])
        tiles_begun = sb("s_tbegun", [P, 4])
        group_no = sb("s_group", [1, GROUPS - RING])
        w_in, w_turned, w_copied, w_ready = sem("k_win"), sem("k_wturn"), sem("k_wcopy"), sem("k_wready")
        w_nat = sb("k_wnat", [P, 2 * INNER // P, D])
        w_kv = sb("k_wkv", [P, KC, 2 * INNER])
        w_mean = sb("k_wmean", [P, KC * 2 * MH])
        xk_ok, kv_ok, v_read, k_read, scale_ok, ks_ok, dots_ok = (
            sem(f"k_{n}") for n in ("xk", "kv", "vread", "kread", "scale", "ks", "dots"))
        xk = [sb(f"k_xk{q}", [P, D]) for q in range(2)]
        k_sb = [sb(f"k_k{q}", [P, INNER]) for q in range(2)]
        v_sb = [sb(f"k_v{q}", [P, INNER]) for q in range(2)]
        ks = [sb(f"k_ks{q}", [P, INNER]) for q in range(2)]
        sq = [sb(f"k_sq{q}", [P, 2 * INNER]) for q in range(2)]
        var = [sb(f"k_var{q}", [P, 2 * MH]) for q in range(2)]
        scale = sb("k_scalesb", [P, 2 * MH])
        power = sb("k_power", [P, 2 * MH])
        ps_k, ps_v, ps_dots = m.ps[4:6], m.ps[6], m.ps[7]
        heads = lambda a: a.rearrange("p (h d) -> p h d", d=HD)

        def done_kv(n, per=1):
            return n * per + (PRIME + per)

        turns = []
        marks = {}
        bank = 4 * P
        block = ctx.enter_context(nc.Block())

        @block.gpsimd
        def _(pool):
            pool.sem_inc(scale_ok, PRIME)
            pool.sem_inc(ks_ok, PRIME)
            nc.gpsimd.memset(power[:, :], -0.5).then_inc(scale_ok, 1)
            pool.wait_ge(scale_ok, PRIME + 1)
            with pool.Fori(0, KVT // 2) as g:
                for q in range(2):
                    n = g * 2 + q
                    pool.wait_ge(k_read, done_kv(n))
                    pool.wait_ge(ks_ok, done_kv(n - 1))
                    pool.sem_inc(m.held, 1)
                    link = n * 3 + (PRIME + 2)
                    nc.gpsimd.tensor_scalar(var[q][:, :], var[q][:, :], 1.0 / HD, EPS, ALU.mult,
                                            ALU.add).then_inc(scale_ok, 1)
                    pool.wait_ge(scale_ok, link)
                    nc.gpsimd.tensor_tensor(scale[:, :], var[q][:, :], power[:, :], ALU.pow).then_inc(scale_ok, 1)
                    pool.wait_ge(scale_ok, link + 1)
                    nc.gpsimd.tensor_tensor(scale[:, 0:MH], scale[:, 0:MH], scale[:, MH:2 * MH],
                                            ALU.mult).then_inc(scale_ok, 1)
                    pool.wait_ge(scale_ok, link + 2)
                    pool.wait_ge(dots_ok, done_kv(n - 2))
                    nc.gpsimd.tensor_tensor(heads(ks[q][:, :]), heads(k_sb[q][:, :]),
                                            scale[:, 0:MH].unsqueeze(2).to_broadcast([P, MH, HD]),
                                            ALU.mult).then_inc(ks_ok, 1)
            nc.gpsimd.memset(m.acc[:, :], 0.0)

        @block.scalar
        def _(act):
            for s in (xk_ok, v_read, k_read):
                act.sem_inc(s, PRIME)
            for q in range(4):
                act.wait_ge(w_turned, q + 1)
                nc.scalar.activation(w_kv[:, :, 2 * q * P:2 * (q + 1) * P],
                                     m.ps[q][:, :].rearrange("p (k f) -> p k f", k=KC), ACT.Copy).then_inc(w_copied, 1)
            nc.scalar.activation(xk[0][:, :], m.xt_all[:, 0:D], ACT.Copy).then_inc(xk_ok, 1)
            with act.Fori(0, KVT // 2) as g:
                for q in range(2):
                    n = g * 2 + q
                    act.wait_ge(kv_ok, done_kv(n - 1, 2))
                    act.sem_inc(m.held, 1)
                    nc.scalar.activation(xk[1 - q][:, :], m.xt_all[:, ds((n + 1) * D, D)], ACT.Copy).then_inc(xk_ok, 1)
                    act.wait_ge(dots_ok, done_kv(n - 2))
                    for part, (src_ps, dst_sb, off, read) in enumerate(((ps_v, v_sb[q], 1, v_read),
                                                                        (ps_k[q], k_sb[q], 0, k_read))):
                        act.wait_ge(kv_ok, n * 2 + (PRIME + 1 + part))
                        nc.scalar.activation(dst_sb[:, :], src_ps[:, :], ACT.Copy)
                        for h in range(MH):
                            at = slice(off * INNER + h * HD, off * INNER + (h + 1) * HD)
                            last = nc.scalar.activation(sq[q][:, at], src_ps[:, h * HD:(h + 1) * HD], ACT.Square,
                                                        accum_out=var[q][:, off * MH + h:off * MH + h + 1])
                        last.then_inc(read, 1)

        @block.sync
        def _(sp):
            sp.dma_start(w_nat[:, :, :], Wqkv[INNER:3 * INNER, :].rearrange("(j p) c -> p j c", p=P)).then_inc(w_in, 16)
            sp.wait_ge(stage_done, 2)
            for t, d in ((src_sb, src), (dst_sb, dst)):
                sp.dma_start(t[:, 0:SHORT], d[0:SHORT * P].rearrange("(p f) -> p f", p=P)).then_inc(loaded, 16)
                sp.dma_start(t[0:REST, SHORT:SHORT + 1],
                             d[SHORT * P:EDGES].rearrange("(p f) -> p f", f=1)).then_inc(loaded, 16)

        @block.vector
        def _(dve):
            done = [0]
            cur = [0]

            def then(ins):
                ins.then_inc(stage_done, 1)
                done[0] += 1
                dve.wait_ge(stage_done, done[0])

            def exchange(dist, mirror=False):
                a, b = keys[cur[0]], keys[1 - cur[0]]
                av = a[:, :].rearrange("p (h two l) -> p h two l", two=2, l=dist)
                bv = b[:, :].rearrange("p (h two l) -> p h two l", two=2, l=dist)
                lo, hi, out_lo, out_hi = av[:, :, 0, :], av[:, :, 1, :], bv[:, :, 0, :], bv[:, :, 1, :]
                if mirror:
                    hi, out_hi = hi[:, :, ::-1], out_hi[:, :, ::-1]
                nc.vector.tensor_tensor(out_lo, lo, hi, ALU.min)
                then(nc.vector.tensor_tensor(out_hi, lo, hi, ALU.max))
                cur[0] ^= 1

            def flip(k):
                a, b = keys[cur[0]], keys[1 - cur[0]]
                then(nc.vector.tensor_scalar(b[:, :], a[:, :], turn[:, k:k + 1], None, ALU.mult))
                cur[0] ^= 1

            def transposed():
                b = keys[1 - cur[0]]
                turns.append((done[0], cur[0]))
                for q in range(4):
                    dve.wait_ge(turned, 4 * (len(turns) - 1) + q + 1)
                    last = nc.vector.tensor_copy(b[:, bank * q:bank * (q + 1)], m.ps[q][:, :])
                then(last)
                cur[0] ^= 1

            dve.wait_ge(w_copied, 4)
            wv = w_kv[:, :, :].rearrange("p k (h d) -> p (k h) d", d=HD)
            nc.vector.tensor_reduce(w_mean[:, :], wv, AX, ALU.add).then_inc(w_ready, 1)
            dve.wait_ge(w_ready, 1)
            nc.vector.tensor_scalar(w_mean[:, :], w_mean[:, :], 1.0 / HD, None, ALU.mult).then_inc(w_ready, 1)
            dve.wait_ge(w_ready, 2)
            nc.vector.tensor_tensor(wv, wv, w_mean[:, :].unsqueeze(2).to_broadcast([P, KC * 2 * MH, HD]),
                                    ALU.subtract).then_inc(w_ready, 1)
            then(nc.vector.memset(src_sb[:, :], PAD_SRC))
            then(nc.vector.memset(dst_sb[:, :], NODES))
            for k in range(8):
                last = nc.vector.tensor_scalar(bits[:, k:k + 1], m.lane[:, :], k, 1, ALU.logical_shift_right,
                                               ALU.bitwise_and)
            then(last)
            then(nc.vector.tensor_scalar(sign[:, :], bits[:, :], -2.0, 1.0, ALU.mult, ALU.add))
            nc.vector.tensor_copy(turn[:, 0:1], sign[:, 0:1])
            then(nc.vector.tensor_tensor(turn[:, 1:8], sign[:, 0:7], sign[:, 1:8], ALU.mult))
            dve.wait_ge(loaded, 64)
            then(nc.vector.tensor_scalar(src_sb[:, :], src_sb[:, :], DB, KEY_ONE, ALU.logical_shift_left,
                                         ALU.bitwise_or))
            then(nc.vector.tensor_tensor(keys[0][:, :].bitcast(I32), src_sb[:, :], dst_sb[:, :], ALU.bitwise_or))
            for k in range(1, LB):
                exchange(1 << (k - 1), mirror=True)
                for j in range(k - 2, -1, -1):
                    exchange(1 << j)
            flip(0)
            exchange(1 << (LB - 1), mirror=True)
            for j in range(LB - 2, -1, -1):
                exchange(1 << j)
            for k in range(1, 8):
                flip(k)
                transposed()
                for j in range(k - 1, -1, -1):
                    exchange(1 << j)
                transposed()
                for j in range(LB - 1, -1, -1):
                    exchange(1 << j)
            fin = keys[cur[0]]
            then(nc.vector.tensor_scalar(last_int[:, :], fin[:, GT * P - 1::GT * P].bitcast(I32), DB, PAD_SRC,
                                         ALU.logical_shift_right, ALU.bitwise_and))
            nc.vector.tensor_copy(last_src[:, :], last_int[:, :])
            then(nc.vector.tensor_scalar(bound[:, :], m.iota[:, 0:NT + 1], float(P), None, ALU.mult))
            then(nc.vector.tensor_tensor(below[:, :, :], last_src[:, :].unsqueeze(1).to_broadcast([P, NT + 1, 2]),
                                         bound[:, :].unsqueeze(2).to_broadcast([P, NT + 1, 2]), ALU.is_lt))
            then(nc.vector.tensor_reduce(belows[:, :], below[:, :, :], AX, ALU.add))
            marks["sum"] = done[0]
            turns.append((done[0], cur[0]))
            code_v = code[:, :].rearrange("q (r c) -> q c r", c=COLS // P)
            rows = ET * P // COLS
            for q in range(4):
                dve.wait_ge(turned, 4 * (len(turns) - 1) + q + 1)
                last = nc.vector.tensor_copy(code_v[:, 4 * q:4 * q + 4, :].bitcast(F32),
                                             m.ps[q][:, :].rearrange("q (c r) -> q c r", r=P)[:, :, 0:rows])
            then(last)
            nc.vector.tensor_scalar(m.dst_of[:, :], code[:, :], PAD_SRC, None, ALU.bitwise_and)
            then(nc.vector.tensor_scalar(code[:, :], code[:, :], DB, PAD_SRC, ALU.logical_shift_right,
                                         ALU.bitwise_and))
            nc.vector.tensor_copy(m.src_of[:, 0:ET], code[:, :])
            nc.vector.memset(m.src_of[:, ET:ET + (AHEAD + 1) * GT], float(PAD_SRC))
            dve.wait_ge(turned, 4 * len(turns) + 1)
            then(nc.vector.tensor_copy(lo_f[:, :], m.ps[4][:, 0:NT + 1]))
            nc.vector.tensor_copy(item[:, 0:1], m.lane[:, :])
            nc.vector.tensor_scalar(item[:, 1:2], m.lane[:, :], float(P), None, ALU.add)
            then(nc.vector.tensor_tensor(first_step[:, :], lo_f[:, :], m.iota[:, 0:NT + 1], ALU.add))
            for what, (begins, until) in enumerate(((lo_f, NT), (first_step, NT + 1))):
                last = nc.vector.tensor_tensor(begun[:, what, :, 0:until - 1],
                                               begins[:, 1:until].unsqueeze(1).to_broadcast([P, 2, until - 1]),
                                               item[:, :].unsqueeze(2).to_broadcast([P, 2, until - 1]), ALU.is_le)
            then(last)
            nc.vector.tensor_reduce(tiles_begun[:, 0:2], begun[:, 0, :, 0:NT - 1], AX, ALU.add)
            then(nc.vector.tensor_reduce(tiles_begun[:, 2:4], begun[:, 1, :, 0:NT], AX, ALU.add))
            marks["rows"] = done[0]
            dve.wait_ge(turned, 4 * len(turns) + 2)
            nc.vector.memset(m.tile_at[:, 0:1], NT)
            begun_row = m.ps[5][0:1, 2 * P:2 * P + STEPS + HOTS]
            nc.vector.tensor_copy(m.tile_at[:, 1:STEPS + HOTS + 1], begun_row)
            nc.vector.memset(m.group_at[:, 0:1], 0)
            nc.vector.tensor_tensor(m.group_at[:, 1:STEPS + HOTS + 1], m.iota_row[:, 0:STEPS + HOTS], begun_row,
                                    ALU.subtract)
            nc.vector.memset(m.needed[:, 0:RING], 0)
            then(nc.vector.tensor_copy(group_no[:, :], m.iota_row[0:1, 1:GROUPS - RING + 1]))
            nc.vector.tensor_tensor(m.needed[:, RING:GROUPS], group_no[:, :], m.ps[5][0:1, 0:GROUPS - RING], ALU.add)

        @block.tensor
        def _(pe):
            pe.sem_inc(kv_ok, PRIME)
            pe.sem_inc(dots_ok, PRIME)
            pe.wait_ge(w_in, 16)
            for q in range(4):
                for k in range(KC):
                    for f in range(2):
                        last = nc.tensor.transpose(m.ps[q][:, (2 * k + f) * P:(2 * k + f + 1) * P],
                                                   w_nat[:, 2 * q + f, k * P:(k + 1) * P], m.ident[:, :])
                last.then_inc(w_turned, 1)
            nc.tensor.matmul(ps_dots[:, :], m.zeros[:, 0:P], m.zeros[:, 0:INNER], start=True, stop=False)
            pe.wait_ge(w_ready, 3)

            def dots(n, q):
                pe.wait_ge(ks_ok, done_kv(n))
                for j in range(INNER // P):
                    ins = nc.tensor.matmul(ps_dots[:, j * P:(j + 1) * P], v_sb[q][:, j * P:(j + 1) * P],
                                           ks[q][:, j * P:(j + 1) * P], start=False, stop=False)
                ins.then_inc(dots_ok, 1)

            def k_and_v(n, q):
                pe.wait_ge(xk_ok, done_kv(n))
                for bank, column, read in ((ps_v, INNER, v_read), (ps_k[q], 0, k_read)):
                    pe.wait_ge(read, done_kv(n - 1 if bank is ps_v else n - 2))
                    for k in range(KC):
                        ins = nc.tensor.matmul(bank[:, :], xk[q][:, k * P:(k + 1) * P],
                                               w_kv[:, k, column:column + INNER], start=k == 0, stop=k == KC - 1)
                    ins.then_inc(kv_ok, 1)

            def pairs(first, until):
                with pe.Fori(first, until) as g:
                    for q in range(2):
                        k_and_v(g * 2 + (q + 1), 1 - q)
                        dots(g * 2 + q, q)

            k_and_v(0, 0)
            all_pairs = KVT // 2
            until = all_pairs - 6 * BETWEEN
            pairs(0, until)
            for at, (count, which) in enumerate(turns):
                pe.wait_ge(stage_done, count)
                for q in range(4):
                    for c in range(4):
                        off = bank * q + c * P
                        last = nc.tensor.transpose(m.ps[q][:, c * P:(c + 1) * P], keys[which][:, off:off + P],
                                                   m.ident[:, :])
                    last.then_inc(turned, 1)
                if at % 2 == 1 and until < all_pairs:
                    pairs(until, until + BETWEEN)
                    until += BETWEEN
            nc.tensor.matmul(ps_dots[:, :], m.zeros[:, 0:P], m.zeros[:, 0:INNER], start=False, stop=True)
            pe.wait_ge(stage_done, marks["sum"])
            pe.wait_ge(k_read, done_kv(KVT - 1))
            nc.tensor.matmul(m.ps[4][:, 0:NT + 1], m.ones[:, :], belows[:, :], start=True,
                             stop=True).then_inc(turned, 1)
            pe.wait_ge(stage_done, marks["rows"])
            for c in range(4):
                last = nc.tensor.matmul(m.ps[5][0:1, c * P:(c + 1) * P], tiles_begun[:, c:c + 1], m.ident[:, :],
                                        start=True, stop=True)
            last.then_inc(turned, 1)


def attention_steps(nc, m):
    ctx = ExitStack()
    with ctx:
        sem = lambda n: ctx.enter_context(nc.semaphore(n))
        sb = lambda n, s, d=F32: ctx.enter_context(nc.sbuf_tensor(n, s, d))
        tile_base = sb("e_base", [P, NT + 1])
        index_ok = sem("e_index")
        landed = [sem(f"e_land{r}") for r in range(RING)]
        arrived = sem("e_arrived")
        rows = sb("e_rows", [P, RING * GT * ROW])
        index = [sb(f"e_index{r}", [P, GT], I32) for r in range(RING)]
        rel_ok, hot_ok, turned_ok, back_ok, src_ok = (sem(f"e_{n}") for n in ("rel", "hot", "turned", "back", "src"))
        link_s, raw_ok, exp_ok, msg_ok, summed, taken = (sem(f"e_{n}") for n in
                                                         ("link", "raw", "exp", "msg", "sum", "taken"))
        rel = sb("e_relsb", [P, GT])
        hot = sb("e_hotsb", [P, HOTS, GT * P])
        hot_tr = sb("e_hottr", [P, GT * P], BF16)
        vals = sb("e_vals", [P, GT, 2 * HEADS])
        raw = sb("e_rawsb", [P, GT, HEADS])
        msg = sb("e_msgsb", [P, 2, GT, ROW])
        ps_hot, ps_src, ps_out = m.ps[0:2], m.ps[2], m.ps[3:5]
        by_value = ps_src[:, 0:GT * 2 * HEADS * PARTS].rearrange("p (t c s) -> p t c s", c=2 * HEADS, s=PARTS)
        block = ctx.enter_context(nc.Block())

        def done(n, per=1):
            return n * per + (PRIME + per)

        @block.sync
        def _(sp):
            with sp.Fori(0, GROUPS // RING) as n:
                for s in range(RING):
                    sp.wait_ge(landed[s], (n + 1) * (16 * GT))
                    sp.sem_inc(arrived, 1)
            sp.sem_inc(arrived, AHEAD)

        @block.gpsimd
        def _(pool):
            with pool.Fori(0, GROUPS // RING) as n:
                for s in range(RING):
                    need = pool.value_load(m.needed[0:1, ds(n * RING + s, 1)], min_val=0, max_val=STEPS)
                    pool.wait_ge(msg_ok, need * 2 + PRIME)
                    nc.gpsimd.tensor_copy(index[s][:, :],
                                          m.dst_of[:, ds((n * RING + s) * GT, GT)]).then_inc(index_ok, 1)
                    pool.wait_ge(index_ok, n * RING + (s + 1))
                    pool.sem_inc(m.held, 1)
                    for t in range(GT):
                        at = (s * GT + t) * ROW
                        nc.gpsimd.indirect_dma_start(
                            out=rows[:, at:at + ROW], out_offset=None, in_=m.table,
                            in_offset=bass.IndirectOffsetOnAxis(ap=index[s][:, t:t + 1], axis=0),
                        ).then_inc(landed[s], 16)

        @block.vector
        def _(dve):
            for s in (rel_ok, hot_ok, link_s, raw_ok, msg_ok, taken):
                dve.sem_inc(s, PRIME)
            nc.vector.tensor_scalar(tile_base[:, :], m.iota[:, 0:NT + 1], float(P), None, ALU.mult).then_inc(rel_ok, 1)
            dve.wait_ge(rel_ok, PRIME + 1)

            def tile_of(n):
                return dve.value_load(m.tile_at[0:1, ds(n + 1, 1)], min_val=0, max_val=NT)

            def group_of(n):
                return dve.value_load(m.group_at[0:1, ds(n + 1, 1)], min_val=0, max_val=GROUPS + AHEAD)

            def one_hot(n, b, buf):
                dve.wait_ge(hot_ok, done(n - 1))
                nc.vector.tensor_scalar(rel[:, :], m.src_of[:, ds(group_of(n) * GT, GT)], tile_base[:, ds(b, 1)], None,
                                        ALU.subtract).then_inc(rel_ok, 1)
                dve.wait_ge(rel_ok, done(n) + 1)
                dve.wait_ge(summed, done(n - HOTS))
                nc.vector.tensor_tensor(hot[:, buf, :].rearrange("p (t e) -> p t e", e=P),
                                        m.iota[:, :].unsqueeze(1).to_broadcast([P, GT, P]),
                                        rel[:, :].unsqueeze(2).to_broadcast([P, GT, P]),
                                        ALU.is_equal).then_inc(hot_ok, 1)

            def logits(n, part):
                dve.wait_ge(src_ok, done(n))
                dve.wait_ge(exp_ok, done(n - 1))
                nc.vector.tensor_reduce(vals[:, :, :], by_value, AX, ALU.add).then_inc(link_s, 1)
                dve.wait_ge(link_s, n * 3 + (PRIME + 1))
                nc.vector.tensor_tensor(raw[:, :, :], part[:, :, D:ROW], vals[:, :, 0:HEADS], ALU.add).then_inc(link_s, 1)
                dve.wait_ge(link_s, n * 3 + (PRIME + 2))
                nc.vector.scalar_tensor_tensor(out=raw[:, :, :], in0=raw[:, :, :], scalar=ALPHA, in1=raw[:, :, :],
                                               op0=ALU.mult, op1=ALU.max).then_inc(link_s, 1)
                dve.wait_ge(link_s, n * 3 + (PRIME + 3))
                nc.vector.tensor_tensor(raw[:, :, :], raw[:, :, :], vals[:, :, HEADS:2 * HEADS],
                                        ALU.subtract).then_inc(raw_ok, 1)

            def rows_of(n):
                i = group_of(n)
                dve.wait_ge(arrived, i + 1)
                slot = (i & (RING - 1)) * (GT * ROW)
                return rows[:, ds(slot, GT * ROW)].rearrange("p (t c) -> p t c", c=ROW)

            def messages(n, part, buf):
                dve.wait_ge(exp_ok, done(n))
                for h in range(2):
                    t = slice(h * HT, (h + 1) * HT)
                    nc.vector.tensor_tensor(msg[:, buf, t, 0:D].rearrange("p t (h d) -> p t h d", h=HEADS),
                                            part[:, t, 0:D].rearrange("p t (h d) -> p t h d", h=HEADS),
                                            msg[:, buf, t, D:ROW].unsqueeze(3).to_broadcast([P, HT, HEADS, HD]),
                                            ALU.mult).then_inc(msg_ok, 1)

            def take(n, b, buf):
                dve.wait_ge(summed, done(n))
                dve.wait_ge(taken, done(n - 1))
                nc.vector.tensor_tensor(m.acc[:, ds(b * ROW, ROW)], m.acc[:, ds(b * ROW, ROW)], ps_out[buf][:, 0:ROW],
                                        ALU.add).then_inc(taken, 1)

            b = [dve.value_load(m.tile_at[0:1, n + 1:n + 2], min_val=0, max_val=NT) for n in range(HOTS - 1)]
            for n in range(HOTS - 1):
                one_hot(n, b[n], n)
            part = rows_of(0)
            logits(0, part)
            messages(0, part, 0)
            with dve.Fori(0, STEPS // PASS) as g:
                for k in range(PASS):
                    n = g * PASS + k
                    part = rows_of(n + 1)
                    logits(n + 1, part)
                    take(n - 1, tile_of(n - 1), (k + 1) % 2)
                    one_hot(n + 3, tile_of(n + 3), (k + 3) % HOTS)
                    messages(n + 1, part, (k + 1) % 2)
            take(STEPS - 1, dve.value_load(m.tile_at[0:1, STEPS:STEPS + 1], min_val=0, max_val=NT), (STEPS - 1) % 2)

        @block.scalar
        def _(act):
            for s in (back_ok, exp_ok):
                act.sem_inc(s, PRIME)

            def back(n):
                act.wait_ge(src_ok, done(n - 1))
                for h in range(2):
                    act.wait_ge(turned_ok, n * 2 + (PRIME + h + 1))
                    nc.scalar.activation(hot_tr[:, h * HT * P:(h + 1) * HT * P], ps_hot[h][:, :],
                                         ACT.Copy).then_inc(back_ok, 1)

            def exponentials(n, buf):
                act.wait_ge(raw_ok, done(n))
                act.wait_ge(summed, done(n - 2))
                nc.scalar.activation(msg[:, buf, :, D:ROW], raw[:, :, :], ACT.Exp).then_inc(exp_ok, 1)

            back(0)
            back(1)
            exponentials(0, 0)
            with act.Fori(0, STEPS // PASS) as g:
                for k in range(PASS):
                    n = g * PASS + k
                    exponentials(n + 1, (k + 1) % 2)
                    back(n + 2)

        @block.tensor
        def _(pe):
            for s in (turned_ok, src_ok, summed):
                pe.sem_inc(s, PRIME - 1 if s is summed else PRIME)
            nc.tensor.matmul(ps_out[1][:, 0:ROW], m.zeros[:, 0:P], m.zeros[:, 0:ROW], start=True,
                             stop=True).then_inc(summed, 1)

            def tile_of(n):
                return pe.value_load(m.tile_at[0:1, ds(n + 1, 1)], min_val=0, max_val=NT)

            def turn(n, buf):
                pe.wait_ge(hot_ok, done(n))
                pe.wait_ge(back_ok, done(n - 1, 2))
                for h in range(2):
                    for t in range(HT):
                        at = (h * HT + t) * P
                        ins = nc.tensor.transpose(ps_hot[h][:, t * P:(t + 1) * P], hot[:, buf, at:at + P],
                                                  m.ident[:, :])
                    ins.then_inc(turned_ok, 1)

            def look_up(n, b):
                pe.wait_ge(back_ok, done(n, 2))
                pe.wait_ge(raw_ok, done(n - 1))
                w = 2 * HEADS * PARTS
                for t in range(GT):
                    ins = nc.tensor.matmul(ps_src[:, t * w:(t + 1) * w], hot_tr[:, t * P:(t + 1) * P],
                                           m.src_parts[:, ds(b * w, w)], start=True, stop=True)
                ins.then_inc(src_ok, 1)

            def sums(n, hot_buf, buf):
                pe.wait_ge(taken, done(n - 2))
                for h in range(2):
                    pe.wait_ge(msg_ok, n * 2 + (PRIME + h + 1))
                    for t in range(h * HT, (h + 1) * HT):
                        ins = nc.tensor.matmul(ps_out[buf][:, 0:ROW], hot[:, hot_buf, t * P:(t + 1) * P],
                                               msg[:, buf, t, :], start=t == 0, stop=t == GT - 1)
                ins.then_inc(summed, 1)

            turn(0, 0)
            look_up(0, pe.value_load(m.tile_at[0:1, 1:2], min_val=0, max_val=NT))
            turn(1, 1)
            with pe.Fori(0, STEPS // PASS) as g:
                for k in range(PASS):
                    n = g * PASS + k
                    look_up(n + 1, tile_of(n + 1))
                    turn(n + 2, (k + 2) % HOTS)
                    sums(n, k, k % 2)


def mix_and_route(nc, m, x, Wqkv, Wout, bout, gate_w, gate_b, slots):
    ctx = ExitStack()
    with ctx:
        sem = lambda n: ctx.enter_context(nc.semaphore(n))
        sb = lambda n, s, d=F32: ctx.enter_context(nc.sbuf_tensor(n, s, d))
        w_in, w_ok = sem("m_win"), sem("m_wok")
        step = sem("m_step")
        wq = sb("m_wq", [P, INNER // P, D])
        wo = sb("m_wo", [P, KC, INNER])
        wo_t = sb("m_wot", [P, INNER // P, D])
        dots = sb("m_dots", [P, INNER // P, P])
        dw = sb("m_dw", [P, INNER // P, D])
        mixer = sb("m_mixer", [P, KC, D])
        b_row = sb("m_brow", [1, D])
        g_w = sb("m_gw", [P, KC, EXPERTS])
        g_row = sb("m_grow", [1, EXPERTS])
        xs_ok, mix_ok, added, var_ok, std_ok = sem("m_xs"), sem("m_mix"), sem("m_added"), sem("m_var"), sem("m_std")
        link_v, xn_ok, xt_ok, xts_ok, lg_ok, lg_read, saved = (sem(f"m_{n}") for n in
                                                                ("link", "xn", "xt", "xts", "lg", "lgr", "saved"))
        xs = sb("m_xssb", [P, CT, D])
        xn = sb("m_xnsb", [P, CT, D])
        xts = sb("m_xtsb", [P, CT, D])
        x_in, x_used, link_d, x_last = sem("m_xin"), sem("m_xused"), sem("m_linkd"), sem("m_xlast")
        x_sb = sb("m_xsb", [P, CT, D])
        den = sb("m_den", [P, CT, HEADS])
        stats = sb("m_stats", [P, CT, 6])
        mv = sb("m_mv", [P, CT, 2])
        var = sb("m_varsb", [P, CT])
        std = sb("m_stdsb", [P, CT])
        rstd = sb("m_rstd", [P, CT])
        logits = sb("m_logits", [P, NT * EXPERTS])
        lg = logits[:, :].rearrange("p (t e) -> p t e", e=EXPERTS)
        big = lambda n: sb(n, [P, NT, EXPERTS])
        pick, wide, excl, ones_t = big("m_pick"), big("m_wide"), big("m_excl"), sb("m_onest", [P, NT])
        total = big("m_total")
        small = lambda n: sb(n, [P, NT])
        peak, first, prob, pos, kept, here, base, far = (small(f"m_{n}") for n in
                                                         ("peak", "first", "prob", "pos", "kept", "here", "base", "far"))
        order = sb("m_order", [P, EXPERTS])
        real = sb("m_real", [P, 1])
        to_slot = sb("m_toslot", [P, NT], I32)
        gate, exp_ok, count_ok, routed = sem("m_gate"), sem("m_exp"), sem("m_count"), sem("m_routed")
        idx = sb("m_idx", [P, CT], I32)
        idx_ok, src_ok, sent = sem("m_idx"), sem("m_src"), sem("m_sent")
        block = ctx.enter_context(nc.Block())

        @block.sync
        def _(sp):
            sp.dma_start(wq[:, :, :], Wqkv[0:INNER, :].rearrange("(j p) c -> p j c", p=P)).then_inc(w_in, 16)
            sp.dma_start(wo[:, :, :], Wout.rearrange("(k p) f -> p k f", p=P)).then_inc(w_in, 16)
            sp.dma_start(b_row[:, :], bout.rearrange("(a n) -> a n", a=1)).then_inc(w_in, 16)
            sp.dma_start(g_w[:, :, :], gate_w.rearrange("(k p) e -> p k e", p=P)).then_inc(w_in, 16)
            sp.dma_start(g_row[:, :], gate_b.rearrange("(a n) -> a n", a=1)).then_inc(w_in, 16)
            x_rows = x[0:(NT - 1) * P, :].rearrange("(t p) c -> p t c", p=P)
            with sp.Fori(0, CH - 1) as g:
                sp.wait_ge(x_used, g)
                sp.dma_start(x_sb[:, :, :], x_rows[:, ds(g * CT, CT), :]).then_inc(x_in, 16)
            sp.wait_ge(x_used, CH - 1)
            sp.dma_start(x_sb[:, 0:CT - 1, :], x_rows[:, (CH - 1) * CT:NT - 1, :]).then_inc(x_last, 16)
            sp.dma_start(x_sb[0:LAST, CT - 1, :], x[(NT - 1) * P:NODES, :]).then_inc(x_last, 16)
            sp.wait_ge(x_last, 32)
            sp.sem_inc(x_in, 16)

        @block.tensor
        def _(pe):
            pe.wait_ge(w_in, 80)
            for j in range(INNER // P):
                for k in range(KC):
                    last = nc.tensor.transpose(m.ps[j // 2][:, (j % 2) * D + k * P:(j % 2) * D + (k + 1) * P],
                                               wo[:, k, j * P:(j + 1) * P], m.ident[:, :])
            last.then_inc(w_ok, 1)
            pe.wait_ge(step, 2)
            for j in range(INNER // P):
                last = nc.tensor.matmul(m.ps[2 + j // 2][:, (j % 2) * D:(j % 2 + 1) * D], dots[:, j, :], wo_t[:, j, :],
                                        start=True, stop=True)
            last.then_inc(w_ok, 1)
            pe.wait_ge(step, 3)
            for k in range(KC):
                for j in range(INNER // P):
                    last = nc.tensor.matmul(m.ps[4][:, k * D:(k + 1) * D], wq[:, j, k * P:(k + 1) * P], dw[:, j, :],
                                            start=j == 0, stop=j == INNER // P - 1)
            last.then_inc(w_ok, 1)
            pe.wait_ge(step, 4)
            with pe.Fori(0, CH) as g:
                pe.wait_ge(xs_ok, g + 1)
                for t in range(CT):
                    pe.wait_ge(added, g * CT + max(t - 1, 0))
                    for k in range(KC):
                        nc.tensor.matmul(m.ps[t % 2][:, 0:D], xs[:, t, k * P:(k + 1) * P], mixer[:, k, :],
                                         start=k == 0, stop=False)
                    nc.tensor.matmul(m.ps[t % 2][:, 0:D], m.ones[0:1, :], b_row[0:1, :], start=False,
                                     stop=True).then_inc(mix_ok, 1)
                for t in range(CT + 1):
                    if t < CT:
                        pe.wait_ge(xn_ok, g * CT + t + 1)
                        pe.wait_ge(xts_ok, g * CT + max(t - 1, 0))
                        for k in range(KC):
                            last = nc.tensor.transpose(m.ps[2 + t % 2][:, k * P:(k + 1) * P],
                                                       xn[:, t, k * P:(k + 1) * P], m.ident[:, :])
                        last.then_inc(xt_ok, 1)
                    if t >= 1:
                        q = t - 1
                        pe.wait_ge(xts_ok, g * CT + t)
                        pe.wait_ge(lg_read, g * CT + max(q - 1, 0))
                        for k in range(KC):
                            nc.tensor.matmul(m.ps[4 + q % 2][:, 0:EXPERTS], xts[:, q, k * P:(k + 1) * P], g_w[:, k, :],
                                             start=k == 0, stop=False)
                        nc.tensor.matmul(m.ps[4 + q % 2][:, 0:EXPERTS], m.ones[0:1, :], g_row[0:1, :], start=False,
                                         stop=True).then_inc(lg_ok, 1)
            pe.wait_ge(routed, 1)
            nc.tensor.matmul(m.ps[6][:, 0:NT * EXPERTS], m.tri[:, :], pick[:, :, :].rearrange("p t e -> p (t e)"),
                             start=True, stop=True)
            nc.tensor.matmul(m.ps[7][:, 0:NT * EXPERTS], m.ones[:, :], pick[:, :, :].rearrange("p t e -> p (t e)"),
                             start=True, stop=True).then_inc(count_ok, 1)

        @block.scalar
        def _(act):
            act.wait_ge(w_ok, 1)
            for j in range(2):
                last = nc.scalar.activation(wo_t[:, 2 * j:2 * j + 2, :].rearrange("p j d -> p (j d)"), m.ps[j][:, :],
                                            ACT.Copy)
            last.then_inc(step, 1)
            act.wait_ge(w_ok, 2)
            for j in range(2):
                last = nc.scalar.activation(dw[:, 2 * j:2 * j + 2, :].rearrange("p j d -> p (j d)"), m.ps[2 + j][:, :],
                                            ACT.Copy)
            last.then_inc(step, 1)
            act.wait_ge(w_ok, 3)
            nc.scalar.activation(mixer[:, :, :].rearrange("p k d -> p (k d)"), m.ps[4][:, :], ACT.Copy,
                                 scale=1.0 / NODES).then_inc(step, 1)
            with act.Fori(0, CH) as g:
                act.wait_ge(var_ok, g + 1)
                nc.scalar.activation(std[:, :], var[:, :], ACT.Sqrt).then_inc(std_ok, 1)
                for t in range(CT + 1):
                    if t < CT:
                        act.wait_ge(xt_ok, g * CT + t + 1)
                        act.wait_ge(lg_ok, g * CT)
                        nc.scalar.activation(xts[:, t, :], m.ps[2 + t % 2][:, 0:D], ACT.Copy).then_inc(xts_ok, 1)
                    if t >= 1:
                        act.wait_ge(lg_ok, g * CT + t)
                        nc.scalar.activation(logits[:, ds((g * CT + (t - 1)) * EXPERTS, EXPERTS)],
                                             m.ps[4 + (t - 1) % 2][:, 0:EXPERTS], ACT.Copy).then_inc(lg_read, 1)
            act.wait_ge(gate, 5)
            nc.scalar.activation(wide[:, :, :], wide[:, :, :], ACT.Exp).then_inc(exp_ok, 1)
            with act.Fori(0, CH) as g:
                act.wait_ge(sent, g * (16 * CT))
                act.wait_ge(saved, CH)
                nc.scalar.activation(xs[:, :, :].rearrange("p t d -> p (t d)"), m.xt_all[:, ds(g * CT * D, CT * D)],
                                     ACT.Copy).then_inc(src_ok, 1)

        @block.vector
        def _(dve):
            nc.vector.memset(dots[:, :, :], 0.0).then_inc(link_v, 1)
            dve.wait_ge(link_v, 1)
            pairs = m.ps[7][:, :].rearrange("p (j e) -> p j e", e=P)
            nc.vector.tensor_copy(dots[0:HD, :, 0:HD], pairs[0:HD, :, 0:HD])
            nc.vector.tensor_copy(dots[HD:P, :, HD:P], pairs[HD:P, :, HD:P]).then_inc(step, 1)
            LINKS = 3
            with dve.Fori(0, CH) as g:
                acc = m.acc[:, ds(g * CT * ROW, CT * ROW)].rearrange("p (t c) -> p t c", c=ROW)
                nc.vector.tensor_scalar(den[:, :, :], acc[:, :, D:ROW], 1e-37, None, ALU.max).then_inc(link_d, 1)
                dve.wait_ge(link_d, g * 3 + 1)
                nc.vector.reciprocal(den[:, :, :], den[:, :, :]).then_inc(link_d, 1)
                dve.wait_ge(link_d, g * 3 + 2)
                nc.vector.tensor_tensor(acc[:, :, 0:D].rearrange("p t (h d) -> p t h d", h=HEADS),
                                        acc[:, :, 0:D].rearrange("p t (h d) -> p t h d", h=HEADS),
                                        den[:, :, :].unsqueeze(3).to_broadcast([P, CT, HEADS, HD]),
                                        ALU.mult).then_inc(link_d, 1)
                dve.wait_ge(x_in, g * 16 + 16)
                dve.wait_ge(link_d, g * 3 + 3)
                nc.vector.tensor_tensor(acc[:, :, 0:D], acc[:, :, 0:D], x_sb[:, :, :], ALU.add).then_inc(x_used, 1)
                dve.wait_ge(x_used, g + 1)
                for t in range(CT):
                    dve.wait_ge(mix_ok, g * CT + t + 1)
                    at = ds((g * CT + t) * ROW, D)
                    nc.vector.tensor_tensor(m.acc[:, at], m.acc[:, at], m.ps[t % 2][:, 0:D],
                                            ALU.add).then_inc(added, 1)
                dve.wait_ge(added, (g + 1) * CT)
                dve.sem_inc(m.held, 1)
                for t in range(CT):
                    last = nc.vector.bn_stats(stats[:, t, :], m.acc[:, ds((g * CT + t) * ROW, D)])
                last.then_inc(link_v, 1)
                dve.wait_ge(link_v, g * LINKS + 2)
                dve.sem_inc(m.held, 1)
                for t in range(CT):
                    last = nc.vector.bn_aggr(mv[:, t, :], stats[:, t, :])
                last.then_inc(link_v, 1)
                dve.wait_ge(link_v, g * LINKS + 3)
                nc.vector.tensor_scalar(var[:, :], mv[:, :, 1], EPS, None, ALU.add).then_inc(var_ok, 1)
                dve.wait_ge(std_ok, g + 1)
                nc.vector.reciprocal(rstd[:, :], std[:, :]).then_inc(link_v, 1)
                dve.wait_ge(link_v, g * LINKS + 4)
                dve.wait_ge(xt_ok, g * CT)
                dve.wait_ge(saved, g)
                for t in range(CT):
                    nc.vector.tensor_scalar(xn[:, t, :], m.acc[:, ds((g * CT + t) * ROW, D)], mv[:, t, 0:1],
                                            rstd[:, t:t + 1], ALU.subtract, ALU.mult).then_inc(xn_ok, 1)
            done = [0]

            def then(ins):
                ins.then_inc(gate, 1)
                done[0] += 1
                dve.wait_ge(gate, done[0])

            wide3 = lambda a: a[:, :].unsqueeze(2).to_broadcast([P, NT, EXPERTS])
            dve.wait_ge(lg_read, NT)
            nc.vector.tensor_scalar(order[:, :], m.iota[:, 0:EXPERTS], -1.0, float(EXPERTS), ALU.mult, ALU.add)
            nc.vector.memset(ones_t[:, :], 1.0)
            nc.vector.tensor_scalar(real[:, :], m.lane[:, :], float(LAST), None, ALU.is_lt)
            then(nc.vector.tensor_reduce(peak[:, :], lg, AX, ALU.max))
            then(nc.vector.tensor_tensor(pick[:, :, :], lg, wide3(peak), ALU.is_equal))
            then(nc.vector.tensor_tensor(pick[:, :, :], pick[:, :, :],
                                         order[:, :].unsqueeze(1).to_broadcast([P, NT, EXPERTS]), ALU.mult))
            then(nc.vector.tensor_reduce(first[:, :], pick[:, :, :], AX, ALU.max))
            then(nc.vector.tensor_tensor(wide[:, :, :], lg, wide3(peak), ALU.subtract))
            then(nc.vector.tensor_tensor(pick[:, :, :], order[:, :].unsqueeze(1).to_broadcast([P, NT, EXPERTS]),
                                         wide3(first), ALU.is_equal))
            nc.vector.tensor_scalar(pick[:, NT - 1, :], pick[:, NT - 1, :], real[:, 0:1], None,
                                    ALU.mult).then_inc(routed, 1)
            dve.wait_ge(routed, 1)
            dve.wait_ge(exp_ok, 1)
            then(nc.vector.tensor_reduce(prob[:, :], wide[:, :, :], AX, ALU.add))
            nc.vector.reciprocal(prob[:, :], prob[:, :])
            nc.vector.tensor_reduce(here[:, :], pick[:, :, :], AX, ALU.add)
            dve.wait_ge(count_ok, 1)
            then(nc.vector.tensor_copy(total[:, :, :].rearrange("p t e -> p (t e)"), m.ps[7][:, 0:NT * EXPERTS]))
            for e in range(EXPERTS):
                last = nc.vector.tensor_tensor_scan(excl[:, :, e], ones_t[:, :], total[:, :, e], 0.0, ALU.mult, ALU.add)
            then(last)
            then(nc.vector.tensor_tensor(excl[:, :, :], excl[:, :, :], total[:, :, :], ALU.subtract))
            then(nc.vector.tensor_tensor(excl[:, :, :].rearrange("p t e -> p (t e)"),
                                         excl[:, :, :].rearrange("p t e -> p (t e)"), m.ps[6][:, 0:NT * EXPERTS],
                                         ALU.add))
            then(nc.vector.tensor_tensor(excl[:, :, :], excl[:, :, :], pick[:, :, :], ALU.mult))
            then(nc.vector.tensor_reduce(pos[:, :], excl[:, :, :], AX, ALU.add))
            then(nc.vector.tensor_scalar(pos[:, :], pos[:, :], -1.0, None, ALU.add))
            then(nc.vector.tensor_scalar(kept[:, :], pos[:, :], float(CAP), None, ALU.is_lt))
            then(nc.vector.tensor_tensor(kept[:, :], kept[:, :], here[:, :], ALU.mult))
            nc.vector.tensor_tensor(m.weight[:, :], prob[:, :], kept[:, :], ALU.mult)
            then(nc.vector.tensor_scalar(base[:, :], first[:, :], float(-CAP), float(CAP * EXPERTS), ALU.mult, ALU.add))
            then(nc.vector.tensor_scalar(far[:, :], kept[:, :], -1e6, 1e6, ALU.mult, ALU.add))
            then(nc.vector.tensor_tensor(far[:, :], far[:, :], base[:, :], ALU.add))
            then(nc.vector.tensor_tensor(far[:, :], far[:, :], pos[:, :], ALU.add))
            nc.vector.tensor_copy(to_slot[:, :], far[:, :])
            then(nc.vector.tensor_scalar(pos[:, :], pos[:, :], float(CAP - 1), 0.0, ALU.min, ALU.max))
            then(nc.vector.tensor_tensor(pos[:, :], pos[:, :], base[:, :], ALU.add))
            nc.vector.tensor_copy(m.from_slot[:, :], pos[:, :]).then_inc(routed, 1)

        @block.gpsimd
        def _(pool):
            with pool.Fori(0, CH) as g:
                pool.wait_ge(mix_ok, g * CT)
                pool.sem_inc(m.held, 1)
                nc.gpsimd.tensor_copy(xs[:, :, :].rearrange("p t d -> p (t d)"),
                                      m.xt_all[:, ds(g * CT * D, CT * D)]).then_inc(xs_ok, 1)
                pool.wait_ge(xn_ok, (g + 1) * CT)
                pool.sem_inc(m.held, 1)
                nc.gpsimd.tensor_copy(m.xt_all[:, ds(g * CT * D, CT * D)],
                                      xn[:, :, :].rearrange("p t d -> p (t d)")).then_inc(saved, 1)
            pool.wait_ge(routed, 2)
            with pool.Fori(0, CH) as g:
                pool.wait_ge(sent, g * (16 * CT))
                pool.sem_inc(m.held, 1)
                nc.gpsimd.tensor_copy(idx[:, :], to_slot[:, ds(g * CT, CT)]).then_inc(idx_ok, 1)
                pool.wait_ge(idx_ok, g + 1)
                pool.wait_ge(src_ok, g + 1)
                pool.sem_inc(m.held, 1)
                for t in range(CT):
                    nc.gpsimd.indirect_dma_start(
                        out=slots, out_offset=bass.IndirectOffsetOnAxis(ap=idx[:, t:t + 1], axis=0),
                        in_=xs[:, t, :], in_offset=None, bounds_check=EXPERTS * CAP - 1,
                        oob_is_err=False).then_inc(sent, 16)
            pool.wait_ge(sent, 16 * NT)


def experts(nc, m, slots, w1, b1, w2, b2, results):
    ctx = ExitStack()
    with ctx:
        sem = lambda n: ctx.enter_context(nc.semaphore(n))
        sb = lambda n, s, d=F32: ctx.enter_context(nc.sbuf_tensor(n, s, d))
        ST = -(-CAP // P)
        FULL = CAP // P
        TAIL = CAP - FULL * P
        FT = FF // P
        size = lambda j: P if j < FULL else TAIL
        halves = [(0, 512), (512, CAP - 512)]
        b_in, b_turned, b_ok = sem("f_bin"), sem("f_bturn"), sem("f_bok")
        loaded = [sem(f"f_load{q}") for q in range(2)]
        stored = [sem(f"f_store{q}") for q in range(2)]
        turned, turned_ok, mid, mid_ok, y_ok, y_out = (sem(f"f_{n}") for n in
                                                       ("turn", "turnok", "mid", "midok", "y", "yout"))
        b1_nat = sb("f_b1n", [EXPERTS * FT, P])
        b1_t = sb("f_b1t", [P, EXPERTS * FT])
        b2_row = sb("f_b2", [1, EXPERTS * D])
        w1_sb = [sb(f"f_w1{q}", [P, KC, FF]) for q in range(2)]
        w2_sb = [sb(f"f_w2{q}", [P, FT, D]) for q in range(2)]
        rows = [sb(f"f_rows{q}", [P, ST, D]) for q in range(2)]
        rows_t = [sb(f"f_rowst{q}", [P, KC, CAP]) for q in range(2)]
        hidden = sb("f_hidden", [P, FT, CAP])
        y_sb = [sb(f"f_y{q}", [P, ST, D]) for q in range(2)]
        block = ctx.enter_context(nc.Block())

        @block.sync
        def _(sp):
            sp.dma_start(b1_nat[:, :], b1.rearrange("e (f p) -> (e f) p", p=P)).then_inc(b_in, 16)
            sp.dma_start(b2_row[:, :], b2.rearrange("e d -> (e d)").rearrange("(a n) -> a n", a=1)).then_inc(b_in, 16)

            def store(e, q):
                sp.wait_ge(y_out, (e + 1) * ST)
                sp.dma_start(results[ds(e * CAP, FULL * P), :].rearrange("(j p) d -> p j d", p=P),
                             y_sb[q][:, 0:FULL, :]).then_inc(stored[q], 16)
                sp.dma_start(results[ds(e * CAP + FULL * P, TAIL), :],
                             y_sb[q][0:TAIL, FULL, :]).then_inc(stored[q], 16)

            with sp.Fori(0, EXPERTS // 2) as pair:
                for q in range(2):
                    e = pair * 2 + q
                    sp.wait_ge(y_ok, pair * (2 * ST))
                    sp.dma_start(w1_sb[q][:, :, :], w1[ds(e, 1), :, :].rearrange("e (k p) f -> p (e k) f", p=P)
                                 ).then_inc(loaded[q], 16)
                    sp.dma_start(w2_sb[q][:, :, :], w2[ds(e, 1), :, :].rearrange("e (f p) d -> p (e f) d", p=P)
                                 ).then_inc(loaded[q], 16)
                    sp.dma_start(rows[q][:, 0:FULL, :], slots[ds(e * CAP, FULL * P), :].rearrange(
                        "(j p) d -> p j d", p=P)).then_inc(loaded[q], 16)
                    sp.dma_start(rows[q][0:TAIL, FULL, :], slots[ds(e * CAP + FULL * P, TAIL), :]).then_inc(loaded[q], 16)
                for q in range(2):
                    store(pair * 2 + q, q)
            for q in range(2):
                sp.wait_ge(stored[q], 32 * (EXPERTS // 2))

        @block.tensor
        def _(pe):
            pe.wait_ge(b_in, 32)
            nc.tensor.transpose(m.ps[0][:, 0:EXPERTS * FT], b1_nat[:, :],
                                m.ident[0:EXPERTS * FT, 0:EXPERTS * FT]).then_inc(b_turned, 1)
            pe.wait_ge(b_ok, 1)
            with pe.Fori(0, EXPERTS // 2) as pair:
                for q in range(2):
                    e = pair * 2 + q
                    pe.wait_ge(loaded[q], (pair + 1) * 64)
                    for j in range(ST):
                        pe.wait_ge(turned_ok, e * ST + max(j - 1, 0))
                        n = size(j)
                        for k in range(KC):
                            last = nc.tensor.transpose(m.ps[j % 2][:, k * P:k * P + n],
                                                       rows[q][0:n, j, k * P:(k + 1) * P], m.ident[0:n, 0:n])
                        last.then_inc(turned, 1)
                    pe.wait_ge(turned_ok, (e + 1) * ST)
                    for f in range(FT):
                        for s, (at, w) in enumerate(halves):
                            n = 2 * f + s
                            pe.wait_ge(mid_ok, e * (2 * FT) + max(n - 3, 0))
                            for k in range(KC):
                                last = nc.tensor.matmul(m.ps[2 + n % 4][:, 0:w], w1_sb[q][:, k, f * P:(f + 1) * P],
                                                        rows_t[q][:, k, at:at + w], start=k == 0, stop=k == KC - 1)
                            last.then_inc(mid, 1)
                    pe.wait_ge(mid_ok, (e + 1) * (2 * FT))
                    for j in range(ST):
                        n = size(j)
                        pe.wait_ge(y_out, e * ST + max(j - 1, 0))
                        for f in range(FT):
                            nc.tensor.matmul(m.ps[6 + j % 2][0:n, 0:D], hidden[:, f, j * P:j * P + n],
                                             w2_sb[q][:, f, :], start=f == 0, stop=False)
                        nc.tensor.matmul(m.ps[6 + j % 2][0:n, 0:D], m.ones[0:1, 0:n], b2_row[0:1, ds(e * D, D)],
                                         start=False, stop=True).then_inc(y_ok, 1)

        @block.scalar
        def _(act):
            act.wait_ge(b_turned, 1)
            nc.scalar.activation(b1_t[:, :], m.ps[0][:, 0:EXPERTS * FT], ACT.Copy).then_inc(b_ok, 1)
            act.wait_ge(b_ok, 1)
            with act.Fori(0, EXPERTS // 2) as pair:
                for q in range(2):
                    e = pair * 2 + q
                    act.wait_ge(y_ok, e * ST)
                    for f in range(FT):
                        for s, (at, w) in enumerate(halves):
                            n = 2 * f + s
                            act.wait_ge(mid, e * (2 * FT) + (n + 1))
                            act.sem_inc(m.held, 1)
                            nc.scalar.activation(hidden[:, f, at:at + w], m.ps[2 + n % 4][:, 0:w], ACT.Relu,
                                                 bias=b1_t[:, ds(e * FT + f, 1)]).then_inc(mid_ok, 1)

        @block.vector
        def _(dve):
            with dve.Fori(0, EXPERTS // 2) as pair:
                for q in range(2):
                    e = pair * 2 + q
                    for j in range(ST):
                        n = size(j)
                        dve.wait_ge(turned, e * ST + (j + 1))
                        nc.vector.tensor_copy(rows_t[q][:, :, j * P:j * P + n],
                                              m.ps[j % 2][:, 0:KC * P].rearrange("p (k s) -> p k s", k=KC)[:, :, 0:n]
                                              ).then_inc(turned_ok, 1)
                    dve.wait_ge(stored[q], pair * 32)
                    for j in range(ST):
                        n = size(j)
                        dve.wait_ge(y_ok, e * ST + (j + 1))
                        dve.sem_inc(m.held, 1)
                        nc.vector.tensor_copy(y_sb[q][0:n, j, :], m.ps[6 + j % 2][0:n, 0:D]).then_inc(y_out, 1)


def combine(nc, m, results, out):
    ctx = ExitStack()
    with ctx:
        sem = lambda n: ctx.enter_context(nc.semaphore(n))
        sb = lambda n, s, d=F32: ctx.enter_context(nc.sbuf_tensor(n, s, d))
        FMAX = 3.4028234e38
        landed = [sem(f"o_land{t}") for t in range(CT)]
        free, idx_ok, link_v, cleared, left = sem("o_free"), sem("o_idx"), sem("o_link"), sem("o_clr"), sem("o_left")
        added = sem("o_added")
        idx = sb("o_idxsb", [P, CT], I32)
        y = sb("o_y", [P, CT, D])
        safe = sb("o_safe", [P, 2, D])
        inf = sb("o_inf", [P, 2, D])
        fin = sb("o_fin", [P, D], I32)
        block = ctx.enter_context(nc.Block())

        @block.gpsimd
        def _(pool):
            with pool.Fori(0, CH) as g:
                pool.wait_ge(added, g * CT)
                pool.sem_inc(m.held, 1)
                nc.gpsimd.tensor_copy(idx[:, :], m.from_slot[:, ds(g * CT, CT)]).then_inc(idx_ok, 1)
                pool.wait_ge(idx_ok, g + 1)
                pool.sem_inc(m.held, 1)
                for t in range(CT):
                    nc.gpsimd.indirect_dma_start(
                        out=y[:, t, :], out_offset=None, in_=results,
                        in_offset=bass.IndirectOffsetOnAxis(ap=idx[:, t:t + 1], axis=0)).then_inc(landed[t], 16)

        @block.vector
        def _(dve):
            LINKS = 5
            with dve.Fori(0, CH) as g:
                for t in range(CT):
                    n = g * CT + t
                    dve.wait_ge(landed[t], (g + 1) * 16)
                    dve.wait_ge(added, n)
                    nc.vector.memset(safe[:, 0, :], 0.0)
                    nc.vector.tensor_scalar(y[:, t, :], y[:, t, :], m.weight[:, ds(n, 1)], None,
                                            ALU.mult).then_inc(link_v, 1)
                    dve.wait_ge(link_v, n * LINKS + 1)
                    nc.vector.tensor_scalar(fin[:, :], y[:, t, :], 0.0, 0.0, ALU.mult, ALU.is_equal)
                    nc.vector.tensor_scalar(inf[:, 0, :], y[:, t, :], FMAX, 1e4, ALU.is_gt, ALU.mult)
                    nc.vector.tensor_scalar(inf[:, 1, :], y[:, t, :], -FMAX, -1e4, ALU.is_lt,
                                            ALU.mult).then_inc(link_v, 1)
                    dve.wait_ge(link_v, n * LINKS + 2)
                    dve.sem_inc(m.held, 1)
                    nc.vector.copy_predicated(safe[:, 0, :], fin[:, :], y[:, t, :])
                    nc.vector.tensor_tensor(inf[:, 0, :], inf[:, 0, :], inf[:, 1, :], ALU.add).then_inc(link_v, 1)
                    dve.wait_ge(link_v, n * LINKS + 3)
                    nc.vector.tensor_tensor(safe[:, 0, :], safe[:, 0, :], inf[:, 0, :], ALU.add).then_inc(link_v, 1)
                    dve.wait_ge(link_v, n * LINKS + 4)
                    nc.vector.tensor_tensor(m.acc[:, ds(n * ROW, D)], m.acc[:, ds(n * ROW, D)], safe[:, 0, :],
                                            ALU.add).then_inc(added, 1)
                    nc.vector.engine_nop().then_inc(link_v, 1)

        @block.sync
        def _(sp):
            rows = out[0:(NT - 1) * P, :].rearrange("(t p) c -> p t c", p=P)
            for g in range(CH):
                n = CT if g < CH - 1 else CT - 1
                sp.wait_ge(added, (g + 1) * CT)
                sp.dma_start(rows[:, g * CT:g * CT + n, :],
                             m.x_sum[:, g * CT:g * CT + n, 0:D]
                             ).then_inc(left, 16)
            sp.dma_start(out[(NT - 1) * P:NODES, :], m.x_sum[0:LAST, NT - 1, 0:D]).then_inc(left, 16)
            sp.wait_ge(left, 16 * (CH + 1))


class Memory:

    def __init__(self, nc, ctx):
        def sb(n, s, d=F32):
            return ctx.enter_context(nc.sbuf_tensor(n, s, d))

        self.ident = sb("ident", [P, P])
        self.ones = sb("ones", [P, P])
        self.tri = sb("tri", [P, P])
        self.zeros = sb("zeros", [P, INNER])
        self.lane = sb("lane", [P, 1], I32)
        self.iota = sb("iota", [P, P])
        self.iota_row = sb("iota_row", [1, STEPS + HOTS])
        self.acc = sb("acc", [P, (NT + 1) * ROW])
        self.x_sum = self.acc[:, 0:NT * ROW].rearrange("p (t c) -> p t c", c=ROW)
        self.hlr = sb("hlr", [P, (NT + 1) * 2 * HEADS])
        self.src_parts = sb("src_parts", [P, (NT + 1) * 2 * HEADS * PARTS], BF16)
        self.group_at = sb("group_at", [1, STEPS + HOTS + 1], I32)
        self.tile_at = sb("tile_at", [1, STEPS + HOTS + 1], I32)
        self.needed = sb("needed", [1, GROUPS], I32)
        self.weight = sb("weight", [P, NT])
        self.from_slot = sb("from_slot", [P, NT], I32)
        self.ps = [ctx.enter_context(nc.psum_tensor(f"ps{i}", [P, 512], F32)) for i in range(8)]
        self.held = ctx.enter_context(nc.semaphore("held"))


def gps_layer(nc, x, src, dst, W, a_l, a_r, Wqkv, Wout, bout, gate_w, gate_b, w1, b1, w2, b2, out):
    table = nc.dram_tensor("node_table", [NT * P, ROW], F32).ap()
    slots = nc.dram_tensor("expert_slots", [EXPERTS * CAP, D], F32).ap()
    results = nc.dram_tensor("expert_results", [EXPERTS * CAP, D], F32).ap()
    ctx = ExitStack()
    with ctx:
        m = Memory(nc, ctx)
        m.table = table
        setup_consts(nc, m)
        with nc.sbuf_tensor("xt_all", [P, (NT + 2) * D], F32) as m.xt_all:
            node_rows(nc, m, x, W, a_l, a_r, slots)
            with nc.sbuf_tensor("src_of", [P, ET + (AHEAD + 1) * GT], F32) as m.src_of, \
                    nc.sbuf_tensor("dst_of", [P, ET], I32) as m.dst_of:
                edge_sort(nc, m, src, dst, Wqkv)
                attention_steps(nc, m)
            mix_and_route(nc, m, x, Wqkv, Wout, bout, gate_w, gate_b, slots)
        experts(nc, m, slots, w1, b1, w2, b2, results)
        combine(nc, m, results, out)


_INS = ["x", "src", "dst", "L0_gnn_W", "L0_gnn_a_l", "L0_gnn_a_r", "L0_mix_Wqkv", "L0_mix_Wout", "L0_mix_bout",
        "L0_ffn_gate_w", "L0_ffn_gate_b", "L0_ffn_w1", "L0_ffn_b1", "L0_ffn_w2", "L0_ffn_b2"]


def kernel(**inputs):
    import numpy as _np
    import concourse.bacc as _bacc
    from concourse import mybir as _mybir
    from concourse.bass_utils import run_bass_kernel_spmd as _run

    nc = _bacc.Bacc("TRN2", target_bir_lowering=False, num_devices=1)
    arrays, args = {}, []
    for name in _INS:
        a = _np.ascontiguousarray(inputs[name])
        arrays[f"in_{name}"] = a
        args.append(nc.dram_tensor(f"in_{name}", a.shape, _mybir.dt.from_np(a.dtype), kind="ExternalInput").ap())
    out = nc.dram_tensor("out_x", (NODES, D), F32, kind="ExternalOutput").ap()
    gps_layer(nc, *args, out)
    r = _run(nc, [arrays], core_ids=[0])
    return r.results[0]["out_x"]
```

```python
from contextlib import ExitStack

import concourse.bass as bass
from concourse import mybir

F32 = mybir.dt.float32
I32 = mybir.dt.int32
BF16 = mybir.dt.bfloat16
ALU = mybir.AluOpType
ACT = mybir.ActivationFunctionType
AX = mybir.AxisListType.X
RMAX = bass.bass_isa.ReduceOp.max
ds = bass.ds

P = 128
NODES, D, EDGES = 6250, 256, 200000
HEADS, HD = 4, 64
MH, INNER = 8, 512
EXPERTS, FF = 8, 1024
CAP = -(-5 * NODES // (4 * EXPERTS))
ALPHA, EPS = 0.2, 1e-5

NT = -(-NODES // P)
CT = 7
CH = NT // CT
LAST = NODES - (NT - 1) * P
KC = D // P

ROW = D + HEADS

DB = 13
KEY_ONE = 1 << 29
PAD_SRC = (1 << DB) - 1
LB = 11
COLS = 1 << LB
SHORT = EDGES // P
REST = EDGES - SHORT * P

GT, HT = 8, 4
GROUPS = -(-EDGES // (GT * P))
ET = GROUPS * GT
GB = (GT * P).bit_length() - 1
RING = 4

PASS = 4
HOTS = 4
STEPS = -(-(EDGES // (GT * P) + NT) // PASS) * PASS
AHEAD = STEPS + HOTS - NT - GROUPS
TB = 6
TILE_BEFORE, TILE_NEXT, TILE_AHEAD, GROUP_NEXT = 0, TB, 2 * TB, 3 * TB

PARTS = 3
KVT = NT + 1
KV_FIRST, KV_AFTER = 15, {1: 3, 3: 3, 5: 3, 7: 1}
MIXER_AFTER, MIX_AFTER = 7, {8: 3, 9: 8, 10: 4, 11: 7, 12: 3}
assert KV_FIRST + sum(KV_AFTER.values()) == sum(MIX_AFTER.values()) == KVT // 2

PRIME = 16


def setup_consts(nc, m):
    ctx = ExitStack()
    with ctx:
        made = ctx.enter_context(nc.semaphore("c_made"))
        block = ctx.enter_context(nc.Block())

        @block.gpsimd
        def _(pool):
            nc.gpsimd.memset(m.ident[:, :], 0.0).then_inc(made, 1)
            nc.gpsimd.memset(m.ones[:, :], 1.0)
            nc.gpsimd.memset(m.tri[:, :], 1.0).then_inc(made, 1)
            nc.gpsimd.memset(m.zeros[:, :], 0.0)
            nc.gpsimd.iota(m.lane[:, :], [[0, 1]], base=0, channel_multiplier=1)
            nc.gpsimd.iota(m.iota[:, :], [[1, P]], base=0, channel_multiplier=0,
                           allow_small_or_imprecise_dtypes=True)
            nc.gpsimd.iota(m.iota_row[:, :], [[1, STEPS + HOTS]], base=0, channel_multiplier=0,
                           allow_small_or_imprecise_dtypes=True)
            pool.wait_ge(made, 2)
            nc.gpsimd.affine_select(out=m.ident[:, :], in_=m.ident[:, :], compare_op=ALU.not_equal, fill=1.0,
                                    base=0, pattern=[[-1, P]], channel_multiplier=1)
            nc.gpsimd.affine_select(out=m.tri[:, :], in_=m.tri[:, :], compare_op=ALU.is_ge, fill=0.0,
                                    base=0, pattern=[[1, P]], channel_multiplier=-1)


def chunks(eng, step):
    with eng.Fori(0, CH // 2) as pair:
        for q in range(2):
            step(pair * 2 + q, q, True)
    step(CH - 1, 0, False)


def node_rows(nc, m, x, W, a_l, a_r, slots, src, dst, Wqkv):
    ctx = ExitStack()
    with ctx:
        sem = lambda n: ctx.enter_context(nc.semaphore(n))
        sb = lambda n, s, d=F32: ctx.enter_context(nc.sbuf_tensor(n, s, d))
        x_in = [sem(f"n_x{g}") for g in range(CH)]
        x_ready, w_in, a_in, padded, zeroed = sem("n_xready"), sem("n_w"), sem("n_a"), sem("n_pad"), sem("n_zero")
        filled, loaded = sem("n_fill"), sem("n_load")
        measured, var_ok, std_ok = sem("n_meas"), sem("n_var"), sem("n_std")
        xn_ok, xt_ok, xs_ok, timed, saved = (sem(f"n_{n}") for n in ("xn", "xt", "xs", "timed", "saved"))
        h_ok, h_copied, cleared = sem("n_h"), sem("n_hc"), sem("n_clr")
        link_v, row_ok, row_out = sem("n_link"), sem("n_row"), [sem(f"n_out{q}") for q in range(2)]
        hr_max, all_max = sem("n_hrmax"), sem("n_allmax")
        w_sb = sb("n_wsb", [P, KC, D])
        x_all = m.x_all
        a_sb = sb("n_asb", [P, 2, D])
        stats = sb("n_stats", [P, CT, 6])
        mv = sb("n_mv", [P, CT, 2])
        var, std, rstd = (sb(f"n_{n}sb", [P, CT]) for n in ("var", "std", "rstd"))
        xn = sb("n_xnsb", [P, CT, D])
        xs = sb("n_xssb", [P, CT, D])
        hc = sb("n_hcsb", [P, CT, D])
        mask = sb("n_mask", [P, CT, D], I32)
        row = [sb(f"n_row{q}", [P, CT, ROW]) for q in range(2)]
        prod = (m.keys[0][:, 0:CT * D].rearrange("p (t c) -> p t c", c=D), mask[:, :, :].bitcast(F32))
        peak = sb("n_peak", [P, HEADS])
        top = sb("n_top", [P, HEADS])
        psx, psh = m.ps[0:2], m.ps[2:4]
        zw = slots.shape[0] * D // P
        slots_flat = slots.rearrange("s d -> (s d)").rearrange("(p f) -> p f", p=P)
        MEASURES, NORMS, LINKS = 2, CT + 1, 4
        block = ctx.enter_context(nc.Block())

        def done(g, per=1):
            return g * per + (PRIME + per)

        @block.sync
        def _(sp):
            for q in range(2):
                sp.sem_inc(row_out[q], PRIME)
            xt = x[0:(NT - 1) * P, :].rearrange("(t p) c -> p t c", p=P)
            sp.dma_start(w_sb[:, :, :], W.rearrange("(k p) f -> p k f", p=P)).then_inc(w_in, 16)
            for g in range(CH):
                n = CT if g < CH - 1 else CT - 1
                part = x_all[:, g * CT * D:(g * CT + n) * D].rearrange("p (t c) -> p t c", c=D)
                sp.dma_start(part, xt[:, g * CT:g * CT + n, :]).then_inc(x_in[g], 16)
                if g == 0:
                    for s, a in enumerate((a_l, a_r)):
                        sp.dma_start(a_sb[:, s, :],
                                     a.rearrange("o h d -> o (h d)").to_broadcast([P, D])).then_inc(a_in, 16)
            sp.wait_ge(filled, 1)
            for t, d in ((m.src_sb, src), (m.dst_sb, dst)):
                sp.dma_start(t[:, 0:SHORT], d[0:SHORT * P].rearrange("(p f) -> p f", p=P)).then_inc(loaded, 16)
                sp.dma_start(t[0:REST, SHORT:SHORT + 1],
                             d[SHORT * P:EDGES].rearrange("(p f) -> p f", f=1)).then_inc(loaded, 16)
            sp.dma_start(m.w_nat[:, :, :],
                         Wqkv[INNER:3 * INNER, :].rearrange("(j p) c -> p j c", p=P)).then_inc(loaded, 16)
            sp.wait_ge(padded, 1)
            sp.dma_start(x_all[0:LAST, (NT - 1) * D:NT * D], x[(NT - 1) * P:NODES, :]).then_inc(x_in[CH - 1], 16)
            sp.sem_inc(x_ready, PRIME)
            for g in range(CH):
                sp.wait_ge(x_in[g], 16 if g < CH - 1 else 32)
                sp.sem_inc(x_ready, 1)
            zc = zw // INNER * INNER
            sp.dma_start(slots_flat[:, 0:zc].rearrange("p (a b) -> p a b", b=INNER),
                         m.zeros[:, :].unsqueeze(1).to_broadcast([P, zc // INNER, INNER])).then_inc(zeroed, 16)
            sp.dma_start(slots_flat[:, zc:zw], m.zeros[:, 0:zw - zc]).then_inc(zeroed, 16)
            table = m.table.rearrange("(t p) c -> p t c", p=P)

            def store(g, q, more):
                sp.wait_ge(row_ok, done(g))
                sp.dma_start(table[:, ds(g * CT, CT), :], row[q][:, :, :]).then_inc(row_out[q], 16)

            chunks(sp, store)
            for q in range(2):
                sp.wait_ge(row_out[q], PRIME + 16 * ((CH + 1 - q) // 2))
            sp.wait_ge(zeroed, 32)
            sp.wait_ge(loaded, 80)

        @block.vector
        def _(dve):
            for s in (measured, var_ok, xn_ok, link_v, row_ok):
                dve.sem_inc(s, PRIME)
            nc.vector.memset(x_all[:, (NT - 1) * D:(NT + 1) * D], 0.0).then_inc(padded, 1)
            nc.vector.memset(m.hlr[:, NT * 8:(NT + 1) * 8], 0.0)
            nc.vector.memset(m.xt_all[:, NT * D:(NT + 2) * D], 0.0)

            def measure(g):
                dve.wait_ge(x_ready, done(g))
                dve.sem_inc(m.held, 1)
                for k in range(CT):
                    last = nc.vector.bn_stats(stats[:, k, :], x_all[:, ds((g * CT + k) * D, D)])
                last.then_inc(measured, 1)
                dve.wait_ge(measured, g * MEASURES + (PRIME + 1))
                dve.sem_inc(m.held, 1)
                for k in range(CT):
                    last = nc.vector.bn_aggr(mv[:, k, :], stats[:, k, :])
                last.then_inc(measured, 1)
                dve.wait_ge(measured, g * MEASURES + (PRIME + 2))
                nc.vector.tensor_scalar(var[:, :], mv[:, :, 1], EPS, None, ALU.add).then_inc(var_ok, 1)

            def norm(g):
                dve.wait_ge(std_ok, done(g))
                nc.vector.reciprocal(rstd[:, :], std[:, :]).then_inc(xn_ok, 1)
                dve.wait_ge(xn_ok, g * NORMS + (PRIME + 1))
                dve.wait_ge(xt_ok, g * CT + PRIME)
                for k in range(CT):
                    nc.vector.tensor_scalar(xn[:, k, :], x_all[:, ds((g * CT + k) * D, D)], mv[:, k, 0:1],
                                            rstd[:, k:k + 1], ALU.subtract, ALU.mult).then_inc(xn_ok, 1)

            def chunk(g, q, more):
                if more:
                    measure(g + 1)
                dve.wait_ge(h_copied, done(g, CT))
                nc.vector.tensor_tensor(mask[:, :, :], hc[:, :, :], hc[:, :, :], ALU.is_equal).then_inc(link_v, 1)
                dve.wait_ge(link_v, g * LINKS + (PRIME + 1))
                dve.wait_ge(cleared, done(g))
                dve.sem_inc(m.held, 1)
                nc.vector.copy_predicated(row[q][:, :, 0:D], mask[:, :, :], hc[:, :, :]).then_inc(link_v, 1)
                if more:
                    norm(g + 1)
                dve.wait_ge(link_v, g * LINKS + (PRIME + 2))
                nc.vector.tensor_tensor(prod[1], row[q][:, :, 0:D], a_sb[:, 1:2, :].to_broadcast([P, CT, D]),
                                        ALU.mult).then_inc(link_v, 1)
                dve.wait_ge(link_v, g * LINKS + (PRIME + 3))
                dve.wait_ge(timed, done(g))
                logits = m.hlr[:, ds(g * CT * 8, CT * 8)].rearrange("p (t c) -> p t c", c=8)
                for s in range(2):
                    last = nc.vector.tensor_reduce(logits[:, :, 4 * s:4 * s + 4],
                                                   prod[s].rearrange("p t (h d) -> p t h d", h=HEADS),
                                                   AX, ALU.add)
                last.then_inc(link_v, 1)
                dve.wait_ge(link_v, g * LINKS + (PRIME + 4))
                dve.sem_inc(m.held, 1)
                nc.vector.tensor_copy(row[q][:, :, D:ROW], logits[:, :, 4:8]).then_inc(row_ok, 1)

            measure(0)
            norm(0)
            dve.wait_ge(a_in, 32)
            chunks(dve, chunk)
            hl = m.hlr[:, 0:NT * 8].rearrange("p (t c) -> p t c", c=8)
            nc.vector.tensor_reduce(peak[:, :], hl[:, :, 4:8].rearrange("p t h -> p h t"), AX,
                                    ALU.max).then_inc(hr_max, 1)
            dve.wait_ge(all_max, 1)
            total = LINKS * CH + PRIME
            nc.vector.tensor_tensor(hl[:, :, 4:8], hl[:, :, 0:4],
                                    top[:, :].unsqueeze(1).to_broadcast([P, NT, HEADS]), ALU.add).then_inc(link_v, 1)
            dve.wait_ge(link_v, total + 1)
            nc.vector.scalar_tensor_tensor(out=hl[:, :, 4:8], in0=hl[:, :, 4:8], scalar=ALPHA, in1=hl[:, :, 4:8],
                                           op0=ALU.mult, op1=ALU.max).then_inc(link_v, 1)
            dve.wait_ge(link_v, total + 2)
            parts = m.src_parts[:, :].rearrange("p (v s) -> p v s", s=PARTS)
            for s in range(PARTS):
                nc.vector.tensor_copy(parts[:, :, s], m.hlr[:, :]).then_inc(link_v, 1)
                dve.wait_ge(link_v, total + 3 + 2 * s)
                if s < PARTS - 1:
                    nc.vector.tensor_tensor(m.hlr[:, :], m.hlr[:, :], parts[:, :, s], ALU.subtract).then_inc(link_v, 1)
                    dve.wait_ge(link_v, total + 4 + 2 * s)

        @block.scalar
        def _(act):
            for s in (std_ok, xs_ok, h_copied, saved):
                act.sem_inc(s, PRIME)

            def deviations(g):
                act.wait_ge(var_ok, done(g))
                nc.scalar.activation(std[:, :], var[:, :], ACT.Sqrt).then_inc(std_ok, 1)

            def take_h(k, g):
                act.wait_ge(h_ok, g * CT + (PRIME + k + 1))
                nc.scalar.activation(hc[:, k, :], psh[k % 2][:, 0:D], ACT.Copy).then_inc(h_copied, 1)

            def chunk(g, q, more):
                for k in range(CT):
                    act.wait_ge(xt_ok, g * CT + (PRIME + k + 1))
                    act.wait_ge(h_ok, g * CT + PRIME)
                    act.wait_ge(saved, done(g - 1))
                    nc.scalar.activation(xs[:, k, :], psx[k % 2][:, 0:D], ACT.Copy).then_inc(xs_ok, 1)
                    if k >= 1:
                        take_h(k - 1, g)
                take_h(CT - 1, g)
                if more:
                    deviations(g + 1)
                act.wait_ge(xs_ok, done(g, CT))
                act.sem_inc(m.held, 1)
                nc.scalar.activation(m.xt_all[:, ds(g * CT * D, CT * D)], xs[:, :, :].rearrange("p t c -> p (t c)"),
                                     ACT.Copy).then_inc(saved, 1)

            deviations(0)
            chunks(act, chunk)

        @block.tensor
        def _(pe):
            for s in (xt_ok, h_ok):
                pe.sem_inc(s, PRIME)
            pe.wait_ge(w_in, 16)

            def chunk(g, q, more):
                for k in range(CT + 1):
                    if k < CT:
                        pe.wait_ge(xn_ok, g * NORMS + (PRIME + k + 2))
                        pe.wait_ge(xs_ok, g * CT + (PRIME + k - 1))
                        for c in range(KC):
                            last = nc.tensor.transpose(psx[k % 2][:, c * P:(c + 1) * P], xn[:, k, c * P:(c + 1) * P],
                                                       m.ident[:, :])
                        last.then_inc(xt_ok, 1)
                    if k >= 1:
                        pe.wait_ge(xs_ok, g * CT + (PRIME + k))
                        pe.wait_ge(h_copied, g * CT + (PRIME + k - 2))
                        for c in range(KC):
                            last = nc.tensor.matmul(psh[(k - 1) % 2][:, 0:D], xs[:, k - 1, c * P:(c + 1) * P],
                                                    w_sb[:, c, :], start=c == 0, stop=c == KC - 1)
                        last.then_inc(h_ok, 1)

            chunks(pe, chunk)

        @block.gpsimd
        def _(pool):
            for s in (timed, cleared):
                pool.sem_inc(s, PRIME)

            def chunk(g, q, more):
                pool.wait_ge(row_out[q], (g >> 1) * 16 + PRIME)
                pool.sem_inc(m.held, 1)
                nc.gpsimd.memset(row[q][:, :, 0:D], 0.0).then_inc(cleared, 1)
                pool.wait_ge(link_v, g * LINKS + (PRIME + 2))
                pool.sem_inc(m.held, 1)
                nc.gpsimd.tensor_tensor(prod[0], row[q][:, :, 0:D], a_sb[:, 0:1, :].to_broadcast([P, CT, D]),
                                        ALU.mult).then_inc(timed, 1)

            nc.gpsimd.memset(m.src_sb, PAD_SRC)
            nc.gpsimd.memset(m.dst_sb[:, :], NODES).then_inc(filled, 1)
            pool.wait_ge(a_in, 32)
            chunks(pool, chunk)
            pool.wait_ge(hr_max, 1)
            nc.gpsimd.partition_all_reduce(top[:, :], peak[:, :], P, RMAX).then_inc(all_max, 1)


def edge_sort(nc, m, Wqkv, Wout, bout):
    ctx = ExitStack()
    with ctx:
        sem = lambda n: ctx.enter_context(nc.semaphore(n))
        sb = lambda n, s, d=F32: ctx.enter_context(nc.sbuf_tensor(n, s, d))
        stage_done, turned = sem("s_stage"), sem("s_turn")
        keys, src_sb, dst_sb, w_nat = m.keys, m.src_sb, m.dst_sb, m.w_nat
        bits = sb("s_bits", [P, 8], I32)
        sign = sb("s_sign", [P, 8])
        turn = sb("s_turns", [P, 8])
        code = sb("s_code", [P, ET], I32)
        last_src = sb("s_last", [P, 2])
        last_int = sb("s_lasti", [P, 2], I32)
        bound = sb("s_bound", [P, NT + 1])
        below = sb("s_below", [P, NT + 1, 2])
        belows = sb("s_belows", [P, NT + 1])
        lo_f = sb("s_lof", [P, NT + 1])
        item = sb("s_item", [P, 2])
        first_step = sb("s_fstep", [P, NT + 1])
        begun = sb("s_begun", [P, 2, 2, NT])
        tiles_begun = sb("s_tbegun", [P, 4])
        group_no = sb("s_group", [1, GROUPS - RING])
        field = sb("s_field", [1, STEPS], I32)
        w_turned, w_copied, w_ready = sem("k_wturn"), sem("k_wcopy"), sem("k_wready")
        w_kv = sb("k_wkv", [P, KC, 2 * INNER])
        w_mean = sb("k_wmean", [P, KC * 2 * MH])
        xk_ok, kv_ok, v_read, k_read, scale_ok, ks_ok, dots_ok = (
            sem(f"k_{n}") for n in ("xk", "kv", "vread", "kread", "scale", "ks", "dots"))
        xk = [sb(f"k_xk{q}", [P, D]) for q in range(2)]
        k_sb = [sb(f"k_k{q}", [P, INNER]) for q in range(2)]
        v_sb = [sb(f"k_v{q}", [P, INNER]) for q in range(2)]
        ks = [sb(f"k_ks{q}", [P, INNER]) for q in range(2)]
        sq = [sb(f"k_sq{q}", [P, 2 * INNER]) for q in range(2)]
        var = [sb(f"k_var{q}", [P, 2 * MH]) for q in range(2)]
        scale = sb("k_scalesb", [P, 2 * MH])
        power = sb("k_power", [P, 2 * MH])
        ps_k, ps_v, ps_dots = m.ps[4:6], m.ps[6], m.ps[7]
        m_in, m_made, m_taken, cleared = sem("k_min"), sem("k_mmade"), sem("k_mtaken"), sem("k_clr")
        xs_ok, mixed, based = sem("k_xs"), sem("k_mixed"), sem("k_based")
        PAIRS = INNER // P
        wq = w_nat[:, 0:PAIRS, :]
        wo = w_nat[:, PAIRS:2 * PAIRS, :].rearrange("p (k a) d -> p k (a d)", k=KC)
        wo_t = w_kv[:, 0, :].rearrange("p (j d) -> p j d", d=D)
        dw = w_kv[:, 1, :].rearrange("p (j d) -> p j d", d=D)
        dots_sb = sq[0][:, 0:INNER].rearrange("p (j e) -> p j e", e=P)
        mixer = sq[0][:, INNER:INNER + KC * D].rearrange("p (k d) -> p k d", d=D)
        b_row = sb("k_brow", [1, D])
        heads = lambda a: a.rearrange("p (h d) -> p h d", d=HD)

        def done_kv(n, per=1):
            return n * per + (PRIME + per)

        turns = []
        marks = {}
        bank = 4 * P
        block = ctx.enter_context(nc.Block())

        @block.gpsimd
        def _(pool):
            pool.sem_inc(scale_ok, PRIME)
            pool.sem_inc(ks_ok, PRIME)
            nc.gpsimd.memset(ks[1][:, :], 0.0)
            nc.gpsimd.memset(v_sb[1][:, :], 0.0).then_inc(cleared, 1)
            nc.gpsimd.memset(power[:, :], -0.5).then_inc(scale_ok, 1)
            pool.wait_ge(scale_ok, PRIME + 1)
            with pool.Fori(0, KVT // 2) as g:
                for q in range(2):
                    n = g * 2 + q
                    pool.wait_ge(k_read, done_kv(n))
                    pool.wait_ge(ks_ok, done_kv(n - 1))
                    pool.sem_inc(m.held, 1)
                    link = n * 3 + (PRIME + 2)
                    nc.gpsimd.tensor_scalar(var[q][:, :], var[q][:, :], 1.0 / HD, EPS, ALU.mult,
                                            ALU.add).then_inc(scale_ok, 1)
                    pool.wait_ge(scale_ok, link)
                    nc.gpsimd.tensor_tensor(scale[:, :], var[q][:, :], power[:, :], ALU.pow).then_inc(scale_ok, 1)
                    pool.wait_ge(scale_ok, link + 1)
                    nc.gpsimd.tensor_tensor(scale[:, 0:MH], scale[:, 0:MH], scale[:, MH:2 * MH],
                                            ALU.mult).then_inc(scale_ok, 1)
                    pool.wait_ge(scale_ok, link + 2)
                    pool.wait_ge(dots_ok, done_kv(n - 2))
                    nc.gpsimd.tensor_tensor(heads(ks[q][:, :]), heads(k_sb[q][:, :]),
                                            scale[:, 0:MH].unsqueeze(2).to_broadcast([P, MH, HD]),
                                            ALU.mult).then_inc(ks_ok, 1)
            pool.wait_ge(k_read, done_kv(KVT - 1))
            nc.gpsimd.memset(dots_sb, 0.0).then_inc(cleared, 1)
            pool.wait_ge(mixed, done_kv(KVT - 1))
            nc.gpsimd.memset(m.acc[:, :], 0.0)

        @block.scalar
        def _(act):
            for s in (xk_ok, v_read, k_read):
                act.sem_inc(s, PRIME)
            for q in range(4):
                act.wait_ge(w_turned, q + 1)
                nc.scalar.activation(w_kv[:, :, 2 * q * P:2 * (q + 1) * P],
                                     m.ps[q][:, :].rearrange("p (k f) -> p k f", k=KC), ACT.Copy).then_inc(w_copied, 1)
            nc.scalar.activation(xk[0][:, :], m.xt_all[:, 0:D], ACT.Copy).then_inc(xk_ok, 1)
            with act.Fori(0, KVT // 2) as g:
                for q in range(2):
                    n = g * 2 + q
                    act.wait_ge(kv_ok, done_kv(n - 1, 2))
                    act.sem_inc(m.held, 1)
                    nc.scalar.activation(xk[1 - q][:, :], m.xt_all[:, ds((n + 1) * D, D)], ACT.Copy).then_inc(xk_ok, 1)
                    act.wait_ge(dots_ok, done_kv(n - 2))
                    for part, (src_ps, dst_sb, off, read) in enumerate(((ps_v, v_sb[q], 1, v_read),
                                                                        (ps_k[q], k_sb[q], 0, k_read))):
                        act.wait_ge(kv_ok, n * 2 + (PRIME + 1 + part))
                        nc.scalar.activation(dst_sb[:, :], src_ps[:, :], ACT.Copy)
                        for h in range(MH):
                            at = slice(off * INNER + h * HD, off * INNER + (h + 1) * HD)
                            last = nc.scalar.activation(sq[q][:, at], src_ps[:, h * HD:(h + 1) * HD], ACT.Square,
                                                        accum_out=var[q][:, off * MH + h:off * MH + h + 1])
                        last.then_inc(read, 1)
            act.wait_ge(cleared, 2)
            act.wait_ge(m_made, 1)
            blocks = ps_dots[:, :].rearrange("p (j e) -> p j e", e=P)
            nc.scalar.activation(dots_sb[0:HD, :, 0:HD], blocks[0:HD, :, 0:HD], ACT.Copy)
            nc.scalar.activation(dots_sb[HD:P, :, HD:P], blocks[HD:P, :, HD:P], ACT.Copy)
            for made, into in enumerate((wo_t, dw)):
                act.wait_ge(m_made, made + 1)
                for j in range(2):
                    last = nc.scalar.activation(into[:, 2 * j:2 * j + 2, :].rearrange("p j d -> p (j d)"),
                                                m.ps[4 + j][:, :], ACT.Copy)
                last.then_inc(m_taken, 1)
            act.wait_ge(m_made, 3)
            nc.scalar.activation(mixer.rearrange("p k d -> p (k d)"), m.ps[6][:, :], ACT.Copy,
                                 scale=1.0 / NODES).then_inc(m_taken, 1)
            for s in (xs_ok, based):
                act.sem_inc(s, PRIME)
            nc.scalar.activation(xk[0][:, :], m.xt_all[:, 0:D], ACT.Copy).then_inc(xs_ok, 1)
            with act.Fori(0, KVT // 2) as g:
                for q in range(2):
                    n = g * 2 + q
                    act.wait_ge(mixed, done_kv(n - 1))
                    act.sem_inc(m.held, 1)
                    nc.scalar.activation(xk[1 - q][:, :], m.xt_all[:, ds((n + 1) * D, D)], ACT.Copy).then_inc(xs_ok, 1)
                    act.wait_ge(mixed, done_kv(n))
                    act.sem_inc(m.held, 1)
                    nc.scalar.activation(m.xt_all[:, ds(n * D, D)], m.ps[4 + q][:, 0:D], ACT.Copy).then_inc(based, 1)

        @block.sync
        def _(sp):
            sp.dma_start(b_row[:, :], bout.rearrange("(a n) -> a n", a=1)).then_inc(m_in, 16)
            sp.wait_ge(w_turned, 4)
            sp.dma_start(wq, Wqkv[0:INNER, :].rearrange("(j p) c -> p j c", p=P)).then_inc(m_in, 16)
            sp.dma_start(wo, Wout.rearrange("(k p) f -> p k f", p=P)).then_inc(m_in, 16)

        @block.vector
        def _(dve):
            done = [0]
            cur = [0]

            def then(ins):
                ins.then_inc(stage_done, 1)
                done[0] += 1
                dve.wait_ge(stage_done, done[0])

            def exchange(dist, mirror=False):
                a, b = keys[cur[0]], keys[1 - cur[0]]
                av = a[:, :].rearrange("p (h two l) -> p h two l", two=2, l=dist)
                bv = b[:, :].rearrange("p (h two l) -> p h two l", two=2, l=dist)
                lo, hi, out_lo, out_hi = av[:, :, 0, :], av[:, :, 1, :], bv[:, :, 0, :], bv[:, :, 1, :]
                if mirror:
                    hi, out_hi = hi[:, :, ::-1], out_hi[:, :, ::-1]
                nc.vector.tensor_tensor(out_lo, lo, hi, ALU.min)
                then(nc.vector.tensor_tensor(out_hi, lo, hi, ALU.max))
                cur[0] ^= 1

            def flip(k):
                a, b = keys[cur[0]], keys[1 - cur[0]]
                then(nc.vector.tensor_scalar(b[:, :], a[:, :], turn[:, k:k + 1], None, ALU.mult))
                cur[0] ^= 1

            def turned_exchange(dist):
                b = keys[1 - cur[0]]
                turns.append((done[0], cur[0]))
                before = 4 * (len(turns) - 1)

                def halves(q):
                    if dist < bank:
                        views = (m.ps[q][:, :], b[:, bank * q:bank * (q + 1)])
                        return [v.rearrange("p (h two l) -> p h two l", two=2, l=dist)[:, :, i, :]
                                for v in views for i in range(2)]
                    return [m.ps[q][:, :], m.ps[q + 2][:, :], b[:, bank * q:bank * (q + 1)],
                            b[:, bank * (q + 2):bank * (q + 3)]]

                def merge(q):
                    lo, _, out_lo, out_hi = halves(q)
                    dve.wait_ge(stage_done, copied[q])
                    nc.vector.tensor_tensor(out_lo, lo, out_hi, ALU.min)
                    return nc.vector.tensor_tensor(out_hi, lo, out_hi, ALU.max)

                steps = 4 if dist < bank else 2
                copied = []
                for q in range(steps):
                    dve.wait_ge(turned, before + q + (1 if dist < bank else 3))
                    _, hi, _, out_hi = halves(q)
                    nc.vector.tensor_copy(out_hi, hi).then_inc(stage_done, 1)
                    done[0] += 1
                    copied.append(done[0])
                    if q > 0:
                        merge(q - 1)
                last = merge(steps - 1)
                then(last)
                cur[0] ^= 1

            for k in range(8):
                last = nc.vector.tensor_scalar(bits[:, k:k + 1], m.lane[:, :], k, 1, ALU.logical_shift_right,
                                               ALU.bitwise_and)
            then(last)
            then(nc.vector.tensor_scalar(sign[:, :], bits[:, :], -2.0, 1.0, ALU.mult, ALU.add))
            nc.vector.tensor_copy(turn[:, 0:1], sign[:, 0:1])
            then(nc.vector.tensor_tensor(turn[:, 1:8], sign[:, 0:7], sign[:, 1:8], ALU.mult))
            then(nc.vector.tensor_scalar(src_sb[:, :], src_sb[:, :], DB, KEY_ONE, ALU.logical_shift_left,
                                         ALU.bitwise_or))
            then(nc.vector.tensor_tensor(keys[0][:, :].bitcast(I32), src_sb[:, :], dst_sb[:, :], ALU.bitwise_or))
            exchange(1, mirror=True)
            dve.wait_ge(w_copied, 4)
            wv = w_kv[:, :, :].rearrange("p k (h d) -> p (k h) d", d=HD)
            nc.vector.tensor_reduce(w_mean[:, :], wv, AX, ALU.add).then_inc(w_ready, 1)
            dve.wait_ge(w_ready, 1)
            nc.vector.tensor_scalar(w_mean[:, :], w_mean[:, :], 1.0 / HD, None, ALU.mult).then_inc(w_ready, 1)
            dve.wait_ge(w_ready, 2)
            nc.vector.tensor_tensor(wv, wv, w_mean[:, :].unsqueeze(2).to_broadcast([P, KC * 2 * MH, HD]),
                                    ALU.subtract).then_inc(w_ready, 1)
            for k in range(2, LB):
                exchange(1 << (k - 1), mirror=True)
                for j in range(k - 2, -1, -1):
                    exchange(1 << j)
            flip(0)
            exchange(1 << (LB - 1), mirror=True)
            for j in range(LB - 2, -1, -1):
                exchange(1 << j)
            for k in range(1, 8):
                flip(k)
                turned_exchange(1 << (k - 1))
                for j in range(k - 2, -1, -1):
                    exchange(1 << j)
                turned_exchange(1 << (LB - 1))
                for j in range(LB - 2, -1 if k < 7 else GB - 1, -1):
                    exchange(1 << j)
            fin = keys[cur[0]]
            then(nc.vector.tensor_reduce(last_int[:, :].bitcast(F32), fin[:, :].rearrange("p (g e) -> p g e", e=GT * P),
                                         AX, ALU.max))
            then(nc.vector.tensor_scalar(last_int[:, :], last_int[:, :], DB, PAD_SRC,
                                         ALU.logical_shift_right, ALU.bitwise_and))
            nc.vector.tensor_copy(last_src[:, :], last_int[:, :])
            then(nc.vector.tensor_scalar(bound[:, :], m.iota[:, 0:NT + 1], float(P), None, ALU.mult))
            then(nc.vector.tensor_tensor(below[:, :, :], last_src[:, :].unsqueeze(1).to_broadcast([P, NT + 1, 2]),
                                         bound[:, :].unsqueeze(2).to_broadcast([P, NT + 1, 2]), ALU.is_lt))
            then(nc.vector.tensor_reduce(belows[:, :], below[:, :, :], AX, ALU.add))
            marks["sum"] = done[0]
            turns.append((done[0], cur[0]))
            code_v = code[:, :].rearrange("q (r c) -> q c r", c=COLS // P)
            rows = ET * P // COLS
            for q in range(4):
                dve.wait_ge(turned, 4 * (len(turns) - 1) + q + 1)
                last = nc.vector.tensor_copy(code_v[:, 4 * q:4 * q + 4, :].bitcast(F32),
                                             m.ps[q][:, :].rearrange("q (c r) -> q c r", r=P)[:, :, 0:rows])
            then(last)
            nc.vector.tensor_scalar(m.dst_of[:, :], code[:, :], PAD_SRC, None, ALU.bitwise_and)
            then(nc.vector.tensor_scalar(code[:, :], code[:, :], DB, PAD_SRC, ALU.logical_shift_right,
                                         ALU.bitwise_and))
            nc.vector.tensor_copy(m.src_of[:, 0:ET], code[:, :])
            nc.vector.memset(m.src_of[:, ET:ET + (AHEAD + 1) * GT], float(PAD_SRC))
            dve.wait_ge(turned, 4 * len(turns) + 1)
            then(nc.vector.tensor_copy(lo_f[:, :], m.ps[4][:, 0:NT + 1]))
            nc.vector.tensor_copy(item[:, 0:1], m.lane[:, :])
            nc.vector.tensor_scalar(item[:, 1:2], m.lane[:, :], float(P), None, ALU.add)
            then(nc.vector.tensor_tensor(first_step[:, :], lo_f[:, :], m.iota[:, 0:NT + 1], ALU.add))
            for what, (begins, until) in enumerate(((lo_f, NT), (first_step, NT + 1))):
                last = nc.vector.tensor_tensor(begun[:, what, :, 0:until - 1],
                                               begins[:, 1:until].unsqueeze(1).to_broadcast([P, 2, until - 1]),
                                               item[:, :].unsqueeze(2).to_broadcast([P, 2, until - 1]), ALU.is_le)
            then(last)
            nc.vector.tensor_reduce(tiles_begun[:, 0:2], begun[:, 0, :, 0:NT - 1], AX, ALU.add)
            then(nc.vector.tensor_reduce(tiles_begun[:, 2:4], begun[:, 1, :, 0:NT], AX, ALU.add))
            marks["rows"] = done[0]
            dve.wait_ge(turned, 4 * len(turns) + 2)
            nc.vector.memset(m.tile_at[:, 0:1], NT)
            begun_row = m.ps[5][0:1, 2 * P:2 * P + STEPS + HOTS]
            nc.vector.tensor_copy(m.tile_at[:, 1:STEPS + HOTS + 1], begun_row)
            nc.vector.memset(m.group_at[:, 0:1], 0)
            nc.vector.tensor_tensor(m.group_at[:, 1:STEPS + HOTS + 1], m.iota_row[:, 0:STEPS + HOTS], begun_row,
                                    ALU.subtract).then_inc(stage_done, 1)
            done[0] += 1
            dve.wait_ge(stage_done, done[0])
            fields = ((m.tile_at[:, 0:STEPS], TILE_BEFORE), (m.tile_at[:, 2:STEPS + 2], TILE_NEXT),
                      (m.tile_at[:, 4:STEPS + 4], TILE_AHEAD), (m.group_at[:, 2:STEPS + 2], GROUP_NEXT))
            for i, (values, shift) in enumerate(fields):
                to = m.plan if i == 0 else field
                then(nc.vector.tensor_scalar(to[:, :], values, shift, None, ALU.logical_shift_left))
                if i > 0:
                    then(nc.vector.tensor_tensor(m.plan[:, :], m.plan[:, :], field[:, :], ALU.bitwise_or))
            nc.vector.memset(m.needed[:, 0:RING], 0)
            then(nc.vector.tensor_copy(group_no[:, :], m.iota_row[0:1, 1:GROUPS - RING + 1]))
            nc.vector.tensor_tensor(m.needed[:, RING:GROUPS], group_no[:, :], m.ps[5][0:1, 0:GROUPS - RING], ALU.add)

        @block.tensor
        def _(pe):
            pe.sem_inc(kv_ok, PRIME)
            pe.sem_inc(dots_ok, PRIME - 1)
            for q in range(4):
                for k in range(KC):
                    for f in range(2):
                        last = nc.tensor.transpose(m.ps[q][:, (2 * k + f) * P:(2 * k + f + 1) * P],
                                                   w_nat[:, 2 * q + f, k * P:(k + 1) * P], m.ident[:, :])
                last.then_inc(w_turned, 1)
            nc.tensor.matmul(ps_dots[:, :], m.zeros[:, 0:P], m.zeros[:, 0:INNER], start=True, stop=False)
            pe.wait_ge(w_ready, 3)

            def dots(n, q):
                pe.wait_ge(ks_ok, done_kv(n))
                for j in range(INNER // P):
                    ins = nc.tensor.matmul(ps_dots[:, j * P:(j + 1) * P], v_sb[q][:, j * P:(j + 1) * P],
                                           ks[q][:, j * P:(j + 1) * P], start=False, stop=False)
                ins.then_inc(dots_ok, 1)

            def project(n, q, bank, column, read, last_use):
                pe.wait_ge(xk_ok, done_kv(n))
                pe.wait_ge(read, done_kv(last_use))
                for k in range(KC):
                    ins = nc.tensor.matmul(bank[:, :], xk[q][:, k * P:(k + 1) * P], w_kv[:, k, column:column + INNER],
                                           start=k == 0, stop=k == KC - 1)
                ins.then_inc(kv_ok, 1)

            def pairs(first, until):
                with pe.Fori(first, until) as g:
                    for q in range(2):
                        n = g * 2 + q
                        project(n + 1, 1 - q, ps_v, INNER, v_read, n)
                        dots(n - 1, 1 - q)
                        project(n + 1, 1 - q, ps_k[1 - q], 0, k_read, n - 1)

            def make_mixer():
                dots(KVT - 1, 1)
                nc.tensor.matmul(ps_dots[:, :], m.zeros[:, 0:P], m.zeros[:, 0:INNER], start=False, stop=True)
                pe.wait_ge(m_in, 48)
                pe.wait_ge(k_read, done_kv(KVT - 1))
                for j in range(PAIRS):
                    for k in range(KC):
                        last = nc.tensor.transpose(m.ps[4 + j // 2][:, (j % 2) * D + k * P:(j % 2) * D + (k + 1) * P],
                                                   wo[:, k, j * P:(j + 1) * P], m.ident[:, :])
                last.then_inc(m_made, 1)
                pe.wait_ge(m_taken, 1)
                for j in range(PAIRS):
                    last = nc.tensor.matmul(m.ps[4 + j // 2][:, (j % 2) * D:(j % 2 + 1) * D], dots_sb[:, j, :],
                                            wo_t[:, j, :], start=True, stop=True)
                last.then_inc(m_made, 1)
                pe.wait_ge(m_taken, 2)
                for k in range(KC):
                    for j in range(PAIRS):
                        last = nc.tensor.matmul(m.ps[6][:, k * D:(k + 1) * D], wq[:, j, k * P:(k + 1) * P],
                                                dw[:, j, :], start=j == 0, stop=j == PAIRS - 1)
                last.then_inc(m_made, 1)
                pe.wait_ge(m_taken, 3)

            def mix(first, until):
                with pe.Fori(first, until) as g:
                    for q in range(2):
                        n = g * 2 + q
                        pe.wait_ge(xs_ok, done_kv(n))
                        pe.wait_ge(based, done_kv(n - 2))
                        for k in range(KC):
                            nc.tensor.matmul(m.ps[4 + q][:, 0:D], xk[q][:, k * P:(k + 1) * P], mixer[:, k, :],
                                             start=k == 0, stop=False)
                        nc.tensor.matmul(m.ps[4 + q][:, 0:D], m.ones[0:1, :], b_row[0:1, :], start=False, stop=False)
                        nc.tensor.matmul(m.ps[4 + q][:, 0:D], m.ident[:, :], m.x_all[:, ds(n * D, D)], start=False,
                                         stop=True).then_inc(mixed, 1)

            pe.sem_inc(mixed, PRIME)
            pe.wait_ge(cleared, 1)
            project(0, 0, ps_v, INNER, v_read, -1)
            project(0, 0, ps_k[0], 0, k_read, -1)
            pairs(0, KV_FIRST)
            made, mixed_pairs = KV_FIRST, 0
            for at, (count, which) in enumerate(turns):
                pe.wait_ge(stage_done, count)
                for q in range(4):
                    for c in range(4):
                        off = bank * q + c * P
                        last = nc.tensor.transpose(m.ps[q][:, c * P:(c + 1) * P], keys[which][:, off:off + P],
                                                   m.ident[:, :])
                    last.then_inc(turned, 1)
                if at in KV_AFTER:
                    pairs(made, made + KV_AFTER[at])
                    made += KV_AFTER[at]
                if at == MIXER_AFTER:
                    make_mixer()
                if at in MIX_AFTER:
                    mix(mixed_pairs, mixed_pairs + MIX_AFTER[at])
                    mixed_pairs += MIX_AFTER[at]
            pe.wait_ge(stage_done, marks["sum"])
            pe.wait_ge(based, done_kv(KVT - 1))
            nc.tensor.matmul(m.ps[4][:, 0:NT + 1], m.ones[:, :], belows[:, :], start=True,
                             stop=True).then_inc(turned, 1)
            pe.wait_ge(stage_done, marks["rows"])
            for c in range(4):
                last = nc.tensor.matmul(m.ps[5][0:1, c * P:(c + 1) * P], tiles_begun[:, c:c + 1], m.ident[:, :],
                                        start=True, stop=True)
            last.then_inc(turned, 1)


def attention_steps(nc, m):
    ctx = ExitStack()
    with ctx:
        sem = lambda n: ctx.enter_context(nc.semaphore(n))
        sb = lambda n, s, d=F32: ctx.enter_context(nc.sbuf_tensor(n, s, d))
        tile_base = sb("e_base", [P, NT + 1])
        index_ok = sem("e_index")
        landed = [sem(f"e_land{r}") for r in range(RING)]
        arrived = sem("e_arrived")
        rows = sb("e_rows", [P, RING * GT * ROW])
        index = [sb(f"e_index{q}", [P, RING * GT], I32) for q in range(2)]
        rel_ok, hot_ok, turned_ok, back_ok, src_ok = (sem(f"e_{n}") for n in ("rel", "hot", "turned", "back", "src"))
        link_s, raw_ok, exp_ok, msg_ok, summed, taken = (sem(f"e_{n}") for n in
                                                         ("link", "raw", "exp", "msg", "sum", "taken"))
        rel = sb("e_relsb", [P, GT])
        hot = sb("e_hotsb", [P, HOTS, GT * P])
        hot_tr = sb("e_hottr", [P, GT * P], BF16)
        vals = sb("e_vals", [P, GT, 2 * HEADS])
        raw = sb("e_rawsb", [P, GT, HEADS])
        msg = sb("e_msgsb", [P, 2, GT, ROW])
        ps_hot, ps_src, ps_out = m.ps[0:2], m.ps[2], m.ps[3:5]
        by_value = ps_src[:, 0:GT * 2 * HEADS * PARTS].rearrange("p (t c s) -> p t c s", c=2 * HEADS, s=PARTS)
        block = ctx.enter_context(nc.Block())

        def done(n, per=1):
            return n * per + (PRIME + per)

        @block.sync
        def _(sp):
            with sp.Fori(0, GROUPS // RING) as n:
                for s in range(RING):
                    sp.wait_ge(landed[s], (n + 1) * (16 * GT))
                    sp.sem_inc(arrived, 1)
            sp.sem_inc(arrived, AHEAD)

        @block.gpsimd
        def _(pool):
            ROUND = RING * GT

            def take_index(n, q):
                nc.gpsimd.tensor_copy(index[q][:, :], m.dst_of[:, ds(n * ROUND, ROUND)]).then_inc(index_ok, 1)

            def round_of(n, q, more):
                for s in range(RING):
                    need = pool.value_load(m.needed[0:1, ds(n * RING + s, 1)], min_val=0, max_val=STEPS)
                    pool.wait_ge(msg_ok, need * 2 + PRIME)
                    pool.sem_inc(m.held, 1)
                    if s == 0:
                        pool.wait_ge(index_ok, n + 1)
                        pool.sem_inc(m.held, 1)
                    if s == RING - 1 and more:
                        take_index(n + 1, 1 - q)
                    for t in range(GT):
                        at = (s * GT + t) * ROW
                        nc.gpsimd.indirect_dma_start(
                            out=rows[:, at:at + ROW], out_offset=None, in_=m.table,
                            in_offset=bass.IndirectOffsetOnAxis(ap=index[q][:, s * GT + t:s * GT + t + 1], axis=0),
                        ).then_inc(landed[s], 16)

            take_index(0, 0)
            rounds = GROUPS // RING
            assert rounds * RING == GROUPS and rounds % 2
            with pool.Fori(0, rounds // 2) as pair:
                for q in range(2):
                    round_of(pair * 2 + q, q, True)
            round_of(rounds - 1, 0, False)

        @block.vector
        def _(dve):
            for s in (rel_ok, hot_ok, link_s, raw_ok, msg_ok, taken):
                dve.sem_inc(s, PRIME)
            nc.vector.tensor_scalar(tile_base[:, :], m.iota[:, 0:NT + 1], float(P), None, ALU.mult).then_inc(rel_ok, 1)
            dve.wait_ge(rel_ok, PRIME + 1)

            def tile(word, shift):
                return nc.s_assert_within((word >> shift) & ((1 << TB) - 1), 0, NT,
                                          skip_runtime_bounds_check_because="tile_at's values are node tiles")

            def one_hot(n, b, i, buf):
                dve.wait_ge(hot_ok, done(n - 1))
                nc.vector.tensor_scalar(rel[:, :], m.src_of[:, ds(i * GT, GT)], tile_base[:, ds(b, 1)], None,
                                        ALU.subtract).then_inc(rel_ok, 1)
                dve.wait_ge(rel_ok, done(n) + 1)
                dve.wait_ge(summed, done(n - HOTS))
                nc.vector.tensor_tensor(hot[:, buf, :].rearrange("p (t e) -> p t e", e=P),
                                        m.iota[:, :].unsqueeze(1).to_broadcast([P, GT, P]),
                                        rel[:, :].unsqueeze(2).to_broadcast([P, GT, P]),
                                        ALU.is_equal).then_inc(hot_ok, 1)

            def logits(n, part):
                dve.wait_ge(src_ok, done(n))
                dve.wait_ge(exp_ok, done(n - 1))
                nc.vector.tensor_reduce(vals[:, :, :], by_value, AX, ALU.add).then_inc(link_s, 1)
                dve.wait_ge(link_s, n * 3 + (PRIME + 1))
                nc.vector.tensor_tensor(raw[:, :, :], part[:, :, D:ROW], vals[:, :, 0:HEADS],
                                        ALU.add).then_inc(link_s, 1)
                dve.wait_ge(link_s, n * 3 + (PRIME + 2))
                nc.vector.scalar_tensor_tensor(out=raw[:, :, :], in0=raw[:, :, :], scalar=ALPHA, in1=raw[:, :, :],
                                               op0=ALU.mult, op1=ALU.max).then_inc(link_s, 1)
                dve.wait_ge(link_s, n * 3 + (PRIME + 3))
                nc.vector.tensor_tensor(raw[:, :, :], raw[:, :, :], vals[:, :, HEADS:2 * HEADS],
                                        ALU.subtract).then_inc(raw_ok, 1)

            def rows_of(i):
                dve.wait_ge(arrived, i + 1)
                slot = (i & (RING - 1)) * (GT * ROW)
                return rows[:, ds(slot, GT * ROW)].rearrange("p (t c) -> p t c", c=ROW)

            def messages(n, part, buf):
                dve.wait_ge(exp_ok, done(n))
                for h in range(2):
                    t = slice(h * HT, (h + 1) * HT)
                    nc.vector.tensor_tensor(msg[:, buf, t, 0:D].rearrange("p t (h d) -> p t h d", h=HEADS),
                                            part[:, t, 0:D].rearrange("p t (h d) -> p t h d", h=HEADS),
                                            msg[:, buf, t, D:ROW].unsqueeze(3).to_broadcast([P, HT, HEADS, HD]),
                                            ALU.mult).then_inc(msg_ok, 1)

            def take(n, b, buf):
                dve.wait_ge(summed, done(n))
                dve.wait_ge(taken, done(n - 1))
                nc.vector.tensor_tensor(m.acc[:, ds(b * ROW, ROW)], m.acc[:, ds(b * ROW, ROW)], ps_out[buf][:, 0:ROW],
                                        ALU.add).then_inc(taken, 1)

            for n in range(HOTS - 1):
                b = dve.value_load(m.tile_at[0:1, n + 1:n + 2], min_val=0, max_val=NT)
                i = dve.value_load(m.group_at[0:1, n + 1:n + 2], min_val=0, max_val=HOTS)
                one_hot(n, b, i, n)
            part = rows_of(0)
            logits(0, part)
            messages(0, part, 0)
            with dve.Fori(0, STEPS // PASS) as g:
                for k in range(PASS):
                    n = g * PASS + k
                    word = dve.value_load(m.plan[0:1, ds(n, 1)], min_val=0,
                                          max_val=(1 << GROUP_NEXT) * (GROUPS + AHEAD))
                    part = rows_of(word >> GROUP_NEXT)
                    logits(n + 1, part)
                    take(n - 1, tile(word, TILE_BEFORE), (k + 1) % 2)
                    b = tile(word, TILE_AHEAD)
                    i = nc.s_assert_within(n + 3 - b, 0, GROUPS + AHEAD,
                                           skip_runtime_bounds_check_because="each tile before took a step more "
                                           "than it ended groups")
                    one_hot(n + 3, b, i, (k + 3) % HOTS)
                    messages(n + 1, part, (k + 1) % 2)
            take(STEPS - 1, dve.value_load(m.tile_at[0:1, STEPS:STEPS + 1], min_val=0, max_val=NT), (STEPS - 1) % 2)

        @block.scalar
        def _(act):
            for s in (back_ok, exp_ok):
                act.sem_inc(s, PRIME)

            def back(n):
                act.wait_ge(src_ok, done(n - 1))
                for h in range(2):
                    act.wait_ge(turned_ok, n * 2 + (PRIME + h + 1))
                    nc.scalar.activation(hot_tr[:, h * HT * P:(h + 1) * HT * P], ps_hot[h][:, :],
                                         ACT.Copy).then_inc(back_ok, 1)

            def exponentials(n, buf):
                act.wait_ge(raw_ok, done(n))
                act.wait_ge(summed, done(n - 2))
                nc.scalar.activation(msg[:, buf, :, D:ROW], raw[:, :, :], ACT.Exp).then_inc(exp_ok, 1)

            back(0)
            back(1)
            exponentials(0, 0)
            with act.Fori(0, STEPS // PASS) as g:
                for k in range(PASS):
                    n = g * PASS + k
                    exponentials(n + 1, (k + 1) % 2)
                    back(n + 2)

        @block.tensor
        def _(pe):
            for s in (turned_ok, src_ok, summed):
                pe.sem_inc(s, PRIME - 1 if s is summed else PRIME)
            nc.tensor.matmul(ps_out[1][:, 0:ROW], m.zeros[:, 0:P], m.zeros[:, 0:ROW], start=True,
                             stop=True).then_inc(summed, 1)

            def tile_of(n):
                return pe.value_load(m.tile_at[0:1, ds(n + 1, 1)], min_val=0, max_val=NT)

            def turn(n, buf):
                pe.wait_ge(hot_ok, done(n))
                pe.wait_ge(back_ok, done(n - 1, 2))
                for h in range(2):
                    for t in range(HT):
                        at = (h * HT + t) * P
                        ins = nc.tensor.transpose(ps_hot[h][:, t * P:(t + 1) * P], hot[:, buf, at:at + P],
                                                  m.ident[:, :])
                    ins.then_inc(turned_ok, 1)

            def look_up(n, b):
                pe.wait_ge(back_ok, done(n, 2))
                pe.wait_ge(raw_ok, done(n - 1))
                w = 2 * HEADS * PARTS
                for t in range(GT):
                    ins = nc.tensor.matmul(ps_src[:, t * w:(t + 1) * w], hot_tr[:, t * P:(t + 1) * P],
                                           m.src_parts[:, ds(b * w, w)], start=True, stop=True)
                ins.then_inc(src_ok, 1)

            def sums(n, hot_buf, buf):
                pe.wait_ge(taken, done(n - 2))
                for h in range(2):
                    pe.wait_ge(msg_ok, n * 2 + (PRIME + h + 1))
                    for t in range(h * HT, (h + 1) * HT):
                        ins = nc.tensor.matmul(ps_out[buf][:, 0:ROW], hot[:, hot_buf, t * P:(t + 1) * P],
                                               msg[:, buf, t, :], start=t == 0, stop=t == GT - 1)
                ins.then_inc(summed, 1)

            turn(0, 0)
            look_up(0, pe.value_load(m.tile_at[0:1, 1:2], min_val=0, max_val=NT))
            turn(1, 1)
            with pe.Fori(0, STEPS // PASS) as g:
                for k in range(PASS):
                    n = g * PASS + k
                    look_up(n + 1, tile_of(n + 1))
                    turn(n + 2, (k + 2) % HOTS)
                    sums(n, k, k % 2)


def sum_and_route(nc, m, gate_w, gate_b, w1, w2, slots):
    ctx = ExitStack()
    with ctx:
        sem = lambda n: ctx.enter_context(nc.semaphore(n))
        sb = lambda n, s, d=F32: ctx.enter_context(nc.sbuf_tensor(n, s, d))
        w_in, early = sem("m_win"), sem("m_early")
        g_w = sb("m_gw", [P, KC, EXPERTS])
        g_row = sb("m_grow", [1, EXPERTS])
        sum_ok, var_ok, std_ok, xn_ok = (sem(f"m_{n}") for n in ("sum", "var", "std", "xn"))
        den = sb("m_den", [P, CT, HEADS])
        stats = sb("m_stats", [P, CT, 6])
        mv = sb("m_mv", [P, CT, 2])
        var, std, rstd = (sb(f"m_{n}sb", [P, CT]) for n in ("var", "std", "rstd"))
        xn = [sb(f"m_xn{q}", [P, CT, D]) for q in range(2)]
        xt_ok, xts_ok, lg_ok = sem("m_xt"), sem("m_xts"), sem("m_lg")
        xts = sb("m_xtsb", [P, CT, D])
        pick_ok, exp_ok, count_ok, place_ok = (sem(f"m_{n}") for n in ("pick", "exp", "count", "place"))
        wide_of = lambda n: sb(n, [P, CT, EXPERTS])
        high, pick, wide, excess, counted = (wide_of(f"m_{n}") for n in ("high", "picksb", "wide", "excess", "counted"))
        peak, first, prob, pos, kept, base, seat = (sb(f"m_{n}", [P, CT]) for n in
                                                    ("peak", "first", "prob", "pos", "kept", "base", "seat"))
        order = sb("m_order", [P, EXPERTS])
        real = sb("m_real", [P, 1])
        carry = sb("m_carry", [P, EXPERTS])
        tot = sb("m_tot", [P, EXPERTS])
        idx = [sb(f"m_idx{q}", [P, CT], I32) for q in range(2)]
        sent, gone = [sem(f"m_sent{q}") for q in range(2)], sem("m_gone")
        lg = [m.ps[4 + q][:, 0:CT * EXPERTS].rearrange("p (t e) -> p t e", e=EXPERTS) for q in range(2)]
        SUMS, PICKS, PLACES = 6, 6, 10
        upto, whole = (m.ps[6 + i][:, 0:CT * EXPERTS].rearrange("p (t e) -> p t e", e=EXPERTS) for i in range(2))
        block = ctx.enter_context(nc.Block())

        def done(g, per=1):
            return g * per + (PRIME + per)

        @block.sync
        def _(sp):
            sp.dma_start(g_w[:, :, :], gate_w.rearrange("(k p) e -> p k e", p=P)).then_inc(w_in, 16)
            sp.dma_start(g_row[:, :], gate_b.rearrange("(a n) -> a n", a=1)).then_inc(w_in, 16)
            for q in range(2):
                load_expert(sp, m, w1, w2, q, q, early)
            sp.sem_inc(gone, PRIME)
            with sp.Fori(0, CH // 2) as pair:
                for q in range(2):
                    sp.wait_ge(sent[q], (pair + 1) * (16 * CT))
                    sp.sem_inc(gone, 1)
            sp.wait_ge(early, 64)

        @block.tensor
        def _(pe):
            for s in (xt_ok, lg_ok, count_ok):
                pe.sem_inc(s, PRIME)
            pe.wait_ge(w_in, 32)

            def chunk(g, q, more):
                for t in range(CT + 1):
                    if t < CT:
                        pe.wait_ge(xn_ok, g * (CT + 1) + (PRIME + t + 2))
                        pe.wait_ge(xts_ok, g * CT + (PRIME + t - 1))
                        for k in range(KC):
                            last = nc.tensor.transpose(m.ps[2 + t % 2][:, k * P:(k + 1) * P],
                                                       xn[q][:, t, k * P:(k + 1) * P], m.ident[:, :])
                        last.then_inc(xt_ok, 1)
                    if t >= 1:
                        pe.wait_ge(xts_ok, g * CT + (PRIME + t))
                        for k in range(KC):
                            nc.tensor.matmul(lg[q][:, t - 1, :], xts[:, t - 1, k * P:(k + 1) * P], g_w[:, k, :],
                                             start=k == 0, stop=False)
                        last = nc.tensor.matmul(lg[q][:, t - 1, :], m.ones[0:1, :], g_row[0:1, :], start=False,
                                                stop=True)
                last.then_inc(lg_ok, 1)
                pe.wait_ge(pick_ok, done(g, PICKS))
                pe.wait_ge(place_ok, done(g - 1, PLACES))
                nc.tensor.matmul(upto[:, :, :], m.tri[:, :], pick[:, :, :], start=True, stop=False)
                for t in range(1, CT):
                    nc.tensor.matmul(upto[:, t:CT, :], m.ones[:, :], pick[:, 0:CT - t, :], start=False, stop=False)
                nc.tensor.matmul(upto[:, :, :], m.ident[:, :], carry[:, :].unsqueeze(1).to_broadcast([P, CT, EXPERTS]),
                                 start=False, stop=True)
                nc.tensor.matmul(whole[:, :, :], m.ones[:, :], pick[:, :, :], start=True,
                                 stop=True).then_inc(count_ok, 1)

            chunks(pe, chunk)

        @block.scalar
        def _(act):
            for s in (std_ok, xts_ok, exp_ok):
                act.sem_inc(s, PRIME)

            def deviations(g):
                act.wait_ge(var_ok, done(g))
                nc.scalar.activation(std[:, :], var[:, :], ACT.Sqrt).then_inc(std_ok, 1)

            def chunk(g, q, more):
                for t in range(CT):
                    act.wait_ge(xt_ok, g * CT + (PRIME + t + 1))
                    act.wait_ge(lg_ok, done(g - 1))
                    nc.scalar.activation(xts[:, t, :], m.ps[2 + t % 2][:, 0:D], ACT.Copy).then_inc(xts_ok, 1)
                if more:
                    deviations(g + 1)
                act.wait_ge(pick_ok, done(g, PICKS))
                act.wait_ge(place_ok, done(g - 1, PLACES))
                nc.scalar.activation(excess[:, :, :], wide[:, :, :], ACT.Exp).then_inc(exp_ok, 1)

            deviations(0)
            chunks(act, chunk)

        @block.vector
        def _(dve):
            for s in (sum_ok, var_ok, xn_ok, pick_ok, place_ok):
                dve.sem_inc(s, PRIME)
            wide3 = lambda a: a[:, :].unsqueeze(2).to_broadcast([P, CT, EXPERTS])
            order3 = order[:, :].unsqueeze(1).to_broadcast([P, CT, EXPERTS])

            def stage(semaphore, g, per):
                count = [0]

                def then(ins):
                    ins.then_inc(semaphore, 1)
                    count[0] += 1
                    dve.wait_ge(semaphore, g * per + (PRIME + count[0]))
                return then

            def sums(g):
                then = stage(sum_ok, g, SUMS)
                acc = m.acc[:, ds(g * CT * ROW, CT * ROW)].rearrange("p (t c) -> p t c", c=ROW)
                then(nc.vector.tensor_scalar(den[:, :, :], acc[:, :, D:ROW], 1e-37, None, ALU.max))
                then(nc.vector.reciprocal(den[:, :, :], den[:, :, :]))
                then(nc.vector.tensor_tensor(acc[:, :, 0:D].rearrange("p t (h d) -> p t h d", h=HEADS),
                                             acc[:, :, 0:D].rearrange("p t (h d) -> p t h d", h=HEADS),
                                             den[:, :, :].unsqueeze(3).to_broadcast([P, CT, HEADS, HD]), ALU.mult))
                then(nc.vector.tensor_tensor(acc[:, :, 0:D], acc[:, :, 0:D],
                                             m.xt_all[:, ds(g * CT * D, CT * D)].rearrange("p (t c) -> p t c", c=D),
                                             ALU.add))
                dve.sem_inc(m.held, 1)
                for t in range(CT):
                    last = nc.vector.bn_stats(stats[:, t, :], m.acc[:, ds((g * CT + t) * ROW, D)])
                then(last)
                dve.sem_inc(m.held, 1)
                for t in range(CT):
                    last = nc.vector.bn_aggr(mv[:, t, :], stats[:, t, :])
                then(last)
                nc.vector.tensor_scalar(var[:, :], mv[:, :, 1], EPS, None, ALU.add).then_inc(var_ok, 1)

            def norm(g, q):
                dve.wait_ge(std_ok, done(g))
                nc.vector.reciprocal(rstd[:, :], std[:, :]).then_inc(xn_ok, 1)
                dve.wait_ge(xn_ok, g * (CT + 1) + (PRIME + 1))
                dve.wait_ge(gone, done(g - 2))
                for t in range(CT):
                    nc.vector.tensor_scalar(xn[q][:, t, :], m.acc[:, ds((g * CT + t) * ROW, D)], mv[:, t, 0:1],
                                            rstd[:, t:t + 1], ALU.subtract, ALU.mult).then_inc(xn_ok, 1)

            def picks(g, q, last=False):
                then = stage(pick_ok, g, PICKS)
                dve.wait_ge(lg_ok, done(g))
                then(nc.vector.tensor_reduce(peak[:, :], lg[q], AX, ALU.max))
                then(nc.vector.tensor_tensor(high[:, :, :], lg[q], wide3(peak), ALU.is_equal))
                then(nc.vector.tensor_tensor(high[:, :, :], high[:, :, :], order3, ALU.mult))
                then(nc.vector.tensor_reduce(first[:, :], high[:, :, :], AX, ALU.max))
                then(nc.vector.tensor_tensor(wide[:, :, :], lg[q], wide3(peak), ALU.subtract))
                if not last:
                    then(nc.vector.tensor_tensor(pick[:, :, :], order3, wide3(first), ALU.is_equal))
                else:
                    nc.vector.tensor_tensor(pick[:, 0:CT - 1, :], order3[:, 0:CT - 1, :],
                                            wide3(first)[:, 0:CT - 1, :], ALU.is_equal)
                    then(nc.vector.scalar_tensor_tensor(
                        out=pick[:, CT - 1, :], in0=order[:, :], scalar=first[:, CT - 1:CT],
                        in1=real[:, 0:1].to_broadcast([P, EXPERTS]), op0=ALU.is_equal, op1=ALU.mult))

            def places(g, q, last=False):
                then = stage(place_ok, g, PLACES)
                at = ds(g * CT, CT)
                dve.wait_ge(exp_ok, done(g))
                then(nc.vector.tensor_reduce(prob[:, :], excess[:, :, :], AX, ALU.add))
                nc.vector.reciprocal(prob[:, :], prob[:, :])
                dve.wait_ge(count_ok, done(g))
                nc.vector.tensor_reduce(tot[:, :], whole.rearrange("p t e -> p e t"), AX, ALU.add)
                then(nc.vector.tensor_tensor(counted[:, :, :], upto, pick[:, :, :], ALU.mult))
                nc.vector.tensor_tensor(carry[:, :], carry[:, :], tot[:, :], ALU.add)
                then(nc.vector.tensor_reduce(pos[:, :], counted[:, :, :], AX, ALU.add))
                if not last:
                    then(nc.vector.tensor_scalar(kept[:, :], pos[:, :], float(CAP), None, ALU.is_le))
                else:
                    nc.vector.tensor_scalar(seat[:, :], pos[:, :], 1.0, None, ALU.is_ge)
                    then(nc.vector.tensor_scalar(kept[:, :], pos[:, :], float(CAP), None, ALU.is_le))
                    nc.vector.tensor_tensor(kept[:, :], kept[:, :], seat[:, :], ALU.mult).then_inc(sum_ok, 1)
                    dve.wait_ge(sum_ok, CH * SUMS + PRIME + 1)
                nc.vector.tensor_scalar(base[:, :], first[:, :], float(-CAP), float(CAP * EXPERTS - 1) + 1e6, ALU.mult,
                                        ALU.add)
                nc.vector.tensor_scalar(seat[:, :], pos[:, :], float(CAP), 1.0, ALU.min, ALU.max)
                then(nc.vector.tensor_tensor(m.weight[:, at], prob[:, :], kept[:, :], ALU.mult))
                then(nc.vector.scalar_tensor_tensor(out=base[:, :], in0=kept[:, :], scalar=-1e6, in1=base[:, :],
                                                    op0=ALU.mult, op1=ALU.add))
                then(nc.vector.tensor_tensor(idx[q][:, :], base[:, :], pos[:, :], ALU.add))
                then(nc.vector.scalar_tensor_tensor(out=seat[:, :], in0=first[:, :], scalar=float(-CAP), in1=seat[:, :],
                                                    op0=ALU.mult, op1=ALU.add))
                then(nc.vector.tensor_scalar(seat[:, :], seat[:, :], float(CAP * EXPERTS - 1), None, ALU.add))
                dve.sem_inc(m.held, 1)
                then(nc.vector.tensor_copy(m.from_slot[:, at], seat[:, :]))

            nc.vector.memset(carry[:, :], 0.0)
            nc.vector.tensor_scalar(order[:, :], m.iota[:, 0:EXPERTS], -1.0, float(EXPERTS), ALU.mult, ALU.add)
            nc.vector.tensor_scalar(real[:, :], m.lane[:, :], float(LAST), None, ALU.is_lt)
            sums(0)
            norm(0, 0)
            with dve.Fori(0, CH // 2) as pair:
                for q in range(2):
                    g = pair * 2 + q
                    sums(g + 1)
                    picks(g, q)
                    norm(g + 1, 1 - q)
                    places(g, q)
            picks(CH - 1, 0, last=True)
            places(CH - 1, 0, last=True)

        @block.gpsimd
        def _(pool):
            def chunk(g, q, more):
                pool.wait_ge(place_ok, done(g, PLACES))
                pool.sem_inc(m.held, 1)
                for t in range(CT):
                    nc.gpsimd.indirect_dma_start(
                        out=slots, out_offset=bass.IndirectOffsetOnAxis(ap=idx[q][:, t:t + 1], axis=0),
                        in_=xn[q][:, t, :], in_offset=None, bounds_check=EXPERTS * CAP - 1,
                        oob_is_err=False).then_inc(sent[q], 16)

            chunks(pool, chunk)
            for q in range(2):
                pool.wait_ge(sent[q], 16 * CT * ((CH + 1 - q) // 2))


def load_expert(sp, m, w1, w2, e, q, loaded):
    sp.dma_start(m.w1_sb[q][:, :, :], w1[ds(e, 1), :, :].rearrange("e (k p) f -> p (e k) f", p=P)).then_inc(loaded, 16)
    sp.dma_start(m.w2_sb[q][:, :, :], w2[ds(e, 1), :, :].rearrange("e (f p) d -> p (e f) d", p=P)).then_inc(loaded, 16)


def experts(nc, m, slots, w1, b1, w2, b2, results):
    ctx = ExitStack()
    with ctx:
        sem = lambda n: ctx.enter_context(nc.semaphore(n))
        sb = lambda n, s, d=F32: ctx.enter_context(nc.sbuf_tensor(n, s, d))
        ST = -(-CAP // P)
        FULL = CAP // P
        TAIL = CAP - FULL * P
        FT = FF // P
        size = lambda j: P if j < FULL else TAIL
        halves = [(0, 512), (512, CAP - 512)]
        b_in, b_turned, b_ok, early = sem("f_bin"), sem("f_bturn"), sem("f_bok"), sem("f_early")
        HALF = 4
        loaded = [sem(f"f_load{q}") for q in range(2)]
        stored = [sem(f"f_store{q}") for q in range(2)]
        turned, turned_ok, mid, mid_ok, y_ok, y_out = (sem(f"f_{n}") for n in
                                                       ("turn", "turnok", "mid", "midok", "y", "yout"))
        b1_nat = sb("f_b1n", [EXPERTS * FT, P])
        b1_t = sb("f_b1t", [P, EXPERTS * FT])
        b2_row = sb("f_b2", [1, EXPERTS * D])
        rows, y_sb = ([m.xt_all[:, at * ST * D:(at + 1) * ST * D].rearrange("p (j d) -> p j d", d=D)
                       for at in places] for places in ((0, 1), (2, 3)))
        rows_t = [sb(f"f_rowst{q}", [P, KC, CAP]) for q in range(2)]
        hidden = sb("f_hidden", [P, FT, CAP])
        PAIRS = EXPERTS // 2
        MIDS = 2 * FT
        block = ctx.enter_context(nc.Block())

        @block.sync
        def _(sp):
            def load_rows(e, q):
                sp.dma_start(rows[q][:, 0:FULL, :], slots[ds(e * CAP, FULL * P), :].rearrange(
                    "(j p) d -> p j d", p=P)).then_inc(loaded[q], 16)
                sp.dma_start(rows[q][0:TAIL, FULL, :], slots[ds(e * CAP + FULL * P, TAIL), :]).then_inc(loaded[q], 16)

            def store(e, q):
                sp.wait_ge(y_out, e * ST + (PRIME + ST))
                sp.dma_start(results[ds(e * CAP, FULL * P), :].rearrange("(j p) d -> p j d", p=P),
                             y_sb[q][:, 0:FULL, :]).then_inc(stored[q], 16)
                sp.dma_start(results[ds(e * CAP + FULL * P, TAIL), :],
                             y_sb[q][0:TAIL, FULL, :]).then_inc(stored[q], 16)

            for q in range(2):
                sp.sem_inc(stored[q], PRIME)
                sp.sem_inc(loaded[q], 32)
            sp.dma_start(b1_nat[:, :], b1.rearrange("e (f p) -> (e f) p", p=P)).then_inc(b_in, 16)
            sp.dma_start(b2_row[:, :], b2.rearrange("e d -> (e d)").rearrange("(a n) -> a n", a=1)).then_inc(b_in, 16)
            sp.dma_start(rows[0][:, 0:HALF, :], slots[0:HALF * P, :].rearrange("(j p) d -> p j d", p=P)
                         ).then_inc(early, 16)
            sp.dma_start(rows[0][:, HALF:FULL, :],
                         slots[HALF * P:FULL * P, :].rearrange("(j p) d -> p j d", p=P)).then_inc(loaded[0], 16)
            sp.dma_start(rows[0][0:TAIL, FULL, :], slots[FULL * P:CAP, :]).then_inc(loaded[0], 16)
            load_rows(1, 1)
            with sp.Fori(0, PAIRS - 1) as pair:
                for q in range(2):
                    e = pair * 2 + q
                    sp.wait_ge(y_ok, e * ST + (PRIME + ST))
                    load_rows(e + 2, q)
                    load_expert(sp, m, w1, w2, e + 2, q, loaded[q])
                    store(e, q)
            for q in range(2):
                store(EXPERTS - 2 + q, q)
            for q in range(2):
                sp.wait_ge(stored[q], PRIME + 32 * PAIRS)

        @block.tensor
        def _(pe):
            pe.sem_inc(y_ok, PRIME)

            def turn(e, q, j):
                pe.wait_ge(turned_ok, e * ST + (PRIME + j - 1))
                n = size(j)
                for k in range(KC):
                    last = nc.tensor.transpose(m.ps[j % 2][:, k * P:k * P + n], rows[q][0:n, j, k * P:(k + 1) * P],
                                               m.ident[0:n, 0:n])
                last.then_inc(turned, 1)

            def expert(pair, q, turn_next):
                e = pair * 2 + q
                pe.wait_ge(turned_ok, e * ST + (PRIME + ST))
                for s, (at, w) in enumerate(halves):
                    for f in range(FT):
                        n = s * FT + f
                        pe.wait_ge(mid_ok, e * MIDS + (PRIME + n - 3))
                        for k in range(KC):
                            last = nc.tensor.matmul(m.ps[2 + n % 4][:, 0:w], m.w1_sb[q][:, k, f * P:(f + 1) * P],
                                                    rows_t[q][:, k, at:at + w], start=k == 0, stop=k == KC - 1)
                        last.then_inc(mid, 1)
                if turn_next:
                    pe.wait_ge(loaded[1 - q], (pair + q) * 64 + 64)
                for j in range(ST):
                    n = size(j)
                    if turn_next:
                        turn(e + 1, 1 - q, j)
                    pe.wait_ge(mid_ok, e * MIDS + (PRIME + (FT if (j + 1) * P <= halves[0][1] else MIDS)))
                    pe.wait_ge(y_out, e * ST + (PRIME + j - 1))
                    for f in range(FT):
                        nc.tensor.matmul(m.ps[6 + j % 2][0:n, 0:D], hidden[:, f, j * P:j * P + n],
                                         m.w2_sb[q][:, f, :], start=f == 0, stop=False)
                    nc.tensor.matmul(m.ps[6 + j % 2][0:n, 0:D], m.ones[0:1, 0:n], b2_row[0:1, ds(e * D, D)],
                                     start=False, stop=True).then_inc(y_ok, 1)

            pe.wait_ge(b_in, 32)
            nc.tensor.transpose(m.ps[2][:, 0:EXPERTS * FT], b1_nat[:, :],
                                m.ident[0:EXPERTS * FT, 0:EXPERTS * FT]).then_inc(b_turned, 1)
            pe.wait_ge(early, 16)
            for j in range(ST):
                if j == HALF:
                    pe.wait_ge(loaded[0], 64)
                turn(0, 0, j)
            pe.wait_ge(b_ok, 1)
            with pe.Fori(0, PAIRS - 1) as pair:
                expert(pair, 0, True)
                expert(pair, 1, True)
            expert(PAIRS - 1, 0, True)
            expert(PAIRS - 1, 1, False)

        @block.scalar
        def _(act):
            act.sem_inc(mid_ok, PRIME)
            act.wait_ge(b_turned, 1)
            nc.scalar.activation(b1_t[:, :], m.ps[2][:, 0:EXPERTS * FT], ACT.Copy).then_inc(b_ok, 1)
            act.wait_ge(b_ok, 1)
            with act.Fori(0, EXPERTS) as e:
                act.wait_ge(y_ok, e * ST + PRIME)
                for s, (at, w) in enumerate(halves):
                    for f in range(FT):
                        n = s * FT + f
                        act.wait_ge(mid, e * MIDS + (n + 1))
                        act.sem_inc(m.held, 1)
                        nc.scalar.activation(hidden[:, f, at:at + w], m.ps[2 + n % 4][:, 0:w], ACT.Relu,
                                             bias=b1_t[:, ds(e * FT + f, 1)]).then_inc(mid_ok, 1)

        @block.vector
        def _(dve):
            for s in (turned_ok, y_out):
                dve.sem_inc(s, PRIME)

            def take_turned(e, q, j):
                n = size(j)
                dve.wait_ge(turned, e * ST + (j + 1))
                nc.vector.tensor_copy(rows_t[q][:, :, j * P:j * P + n],
                                      m.ps[j % 2][:, 0:KC * P].rearrange("p (k s) -> p k s", k=KC)[:, :, 0:n]
                                      ).then_inc(turned_ok, 1)

            def expert(pair, q, turn_next):
                e = pair * 2 + q
                dve.wait_ge(stored[q], pair * 32 + PRIME)
                for j in range(ST):
                    n = size(j)
                    if turn_next:
                        take_turned(e + 1, 1 - q, j)
                    dve.wait_ge(y_ok, e * ST + (PRIME + j + 1))
                    nc.vector.tensor_copy(y_sb[q][0:n, j, :], m.ps[6 + j % 2][0:n, 0:D]).then_inc(y_out, 1)

            for j in range(ST):
                take_turned(0, 0, j)
            with dve.Fori(0, PAIRS - 1) as pair:
                expert(pair, 0, True)
                expert(pair, 1, True)
            expert(PAIRS - 1, 0, True)
            expert(PAIRS - 1, 1, False)


def combine(nc, m, results, out):
    ctx = ExitStack()
    with ctx:
        sem = lambda n: ctx.enter_context(nc.semaphore(n))
        sb = lambda n, s, d=F32: ctx.enter_context(nc.sbuf_tensor(n, s, d))
        FMAX = 3.4028234e38
        landed = [[sem(f"o_land{q}{t}") for t in range(CT)] for q in range(2)]
        idx_ok, weighed, link_v, added, left = (sem(f"o_{n}") for n in ("idx", "weighed", "link", "added", "left"))
        idx = [sb(f"o_idx{q}", [P, CT], I32) for q in range(2)]
        y = [sb(f"o_y{q}", [P, CT, D]) for q in range(2)]
        safe = sb("o_safe", [P, CT, D])
        below = sb("o_below", [P, CT, D])
        finite = sb("o_finite", [P, CT, D], I32)
        block = ctx.enter_context(nc.Block())

        @block.gpsimd
        def _(pool):
            for g in range(CH):
                q = g % 2
                if g >= 2:
                    pool.wait_ge(added, g - 1)
                nc.gpsimd.tensor_copy(idx[q][:, :], m.from_slot[:, g * CT:(g + 1) * CT]).then_inc(idx_ok, 1)
                pool.wait_ge(idx_ok, g + 1)
                for t in range(CT):
                    nc.gpsimd.indirect_dma_start(
                        out=y[q][:, t, :], out_offset=None, in_=results,
                        in_offset=bass.IndirectOffsetOnAxis(ap=idx[q][:, t:t + 1], axis=0)).then_inc(landed[q][t], 16)

        @block.scalar
        def _(act):
            for g in range(CH):
                for t in range(CT):
                    act.wait_ge(landed[g % 2][t], (g // 2 + 1) * 16)
                    nc.scalar.activation(y[g % 2][:, t, :], y[g % 2][:, t, :], ACT.Copy,
                                         scale=m.weight[:, g * CT + t:g * CT + t + 1]).then_inc(weighed, 1)

        @block.vector
        def _(dve):
            LINKS = 3
            for g in range(CH):
                q = g % 2
                dve.wait_ge(weighed, (g + 1) * CT)
                nc.vector.tensor_scalar(finite[:, :, :], y[q][:, :, :], 0.0, 0.0, ALU.mult, ALU.is_equal)
                nc.vector.tensor_scalar(safe[:, :, :], y[q][:, :, :], FMAX, 1e4, ALU.is_gt, ALU.mult)
                nc.vector.tensor_scalar(below[:, :, :], y[q][:, :, :], -FMAX, -1e4, ALU.is_lt,
                                        ALU.mult).then_inc(link_v, 1)
                dve.wait_ge(link_v, g * LINKS + 1)
                nc.vector.tensor_tensor(safe[:, :, :], safe[:, :, :], below[:, :, :], ALU.add).then_inc(link_v, 1)
                dve.wait_ge(link_v, g * LINKS + 2)
                nc.vector.copy_predicated(safe[:, :, :], finite[:, :, :], y[q][:, :, :]).then_inc(link_v, 1)
                dve.wait_ge(link_v, g * LINKS + 3)
                x = m.x_sum[:, g * CT:(g + 1) * CT, 0:D]
                nc.vector.tensor_tensor(x, x, safe[:, :, :], ALU.add).then_inc(added, 1)
                dve.wait_ge(added, g + 1)

        @block.sync
        def _(sp):
            rows = out[0:(NT - 1) * P, :].rearrange("(t p) c -> p t c", p=P)
            for g in range(CH):
                n = CT if g < CH - 1 else CT - 1
                sp.wait_ge(added, g + 1)
                sp.dma_start(rows[:, g * CT:g * CT + n, :],
                             m.x_sum[:, g * CT:g * CT + n, 0:D]
                             ).then_inc(left, 16)
            sp.dma_start(out[(NT - 1) * P:NODES, :], m.x_sum[0:LAST, NT - 1, 0:D]).then_inc(left, 16)
            sp.wait_ge(left, 16 * (CH + 1))


class Memory:

    def __init__(self, nc, ctx):
        def sb(n, s, d=F32):
            return ctx.enter_context(nc.sbuf_tensor(n, s, d))

        self.ident = sb("ident", [P, P])
        self.ones = sb("ones", [P, P])
        self.tri = sb("tri", [P, P])
        self.zeros = sb("zeros", [P, INNER])
        self.lane = sb("lane", [P, 1], I32)
        self.iota = sb("iota", [P, P])
        self.iota_row = sb("iota_row", [1, STEPS + HOTS])
        self.acc = sb("acc", [P, (NT + 1) * ROW])
        self.x_all = self.acc[:, 0:(NT + 1) * D]
        self.x_sum = self.acc[:, 0:NT * ROW].rearrange("p (t c) -> p t c", c=ROW)
        self.hlr = sb("hlr", [P, (NT + 1) * 2 * HEADS])
        self.src_parts = sb("src_parts", [P, (NT + 1) * 2 * HEADS * PARTS], BF16)
        self.group_at = sb("group_at", [1, STEPS + HOTS + 1], I32)
        self.tile_at = sb("tile_at", [1, STEPS + HOTS + 1], I32)
        self.plan = sb("plan", [1, STEPS], I32)
        self.needed = sb("needed", [1, GROUPS], I32)
        self.weight = sb("weight", [P, NT])
        self.from_slot = sb("from_slot", [P, NT], I32)
        self.ps = [ctx.enter_context(nc.psum_tensor(f"ps{i}", [P, 512], F32)) for i in range(8)]
        self.held = ctx.enter_context(nc.semaphore("held"))


def gps_layer(nc, x, src, dst, W, a_l, a_r, Wqkv, Wout, bout, gate_w, gate_b, w1, b1, w2, b2, out):
    table = nc.dram_tensor("node_table", [NT * P, ROW], F32).ap()
    slots = nc.dram_tensor("expert_slots", [EXPERTS * CAP, D], F32).ap()
    results = nc.dram_tensor("expert_results", [EXPERTS * CAP, D], F32).ap()
    ctx = ExitStack()
    with ctx:
        m = Memory(nc, ctx)
        m.table = table
        with nc.sbuf_tensor("xt_all", [P, (NT + 2) * D], F32) as m.xt_all:
            with nc.sbuf_tensor("src_of", [P, ET + (AHEAD + 1) * GT], F32) as m.src_of, \
                    nc.sbuf_tensor("dst_of", [P, ET], I32) as m.dst_of:
                with nc.sbuf_tensor("keys0", [P, COLS], F32) as keys0, \
                        nc.sbuf_tensor("keys1", [P, COLS], F32) as keys1, \
                        nc.sbuf_tensor("dst_in", [P, COLS], I32) as m.dst_sb, \
                        nc.sbuf_tensor("w_kv_nat", [P, 2 * INNER // P, D], F32) as m.w_nat:
                    m.keys, m.src_sb = [keys0, keys1], keys1[:, :].bitcast(I32)
                    setup_consts(nc, m)
                    node_rows(nc, m, x, W, a_l, a_r, slots, src, dst, Wqkv)
                    edge_sort(nc, m, Wqkv, Wout, bout)
                attention_steps(nc, m)
            with nc.sbuf_tensor("w1_a", [P, KC, FF], F32) as w1_a, nc.sbuf_tensor("w1_b", [P, KC, FF], F32) as w1_b, \
                    nc.sbuf_tensor("w2_a", [P, FF // P, D], F32) as w2_a, \
                    nc.sbuf_tensor("w2_b", [P, FF // P, D], F32) as w2_b:
                m.w1_sb, m.w2_sb = (w1_a, w1_b), (w2_a, w2_b)
                sum_and_route(nc, m, gate_w, gate_b, w1, w2, slots)
                experts(nc, m, slots, w1, b1, w2, b2, results)
        combine(nc, m, results, out)


_INS = ["x", "src", "dst", "L0_gnn_W", "L0_gnn_a_l", "L0_gnn_a_r", "L0_mix_Wqkv", "L0_mix_Wout", "L0_mix_bout",
        "L0_ffn_gate_w", "L0_ffn_gate_b", "L0_ffn_w1", "L0_ffn_b1", "L0_ffn_w2", "L0_ffn_b2"]


def kernel(**inputs):
    import numpy as _np
    import concourse.bacc as _bacc
    from concourse import mybir as _mybir
    from concourse.bass_utils import run_bass_kernel_spmd as _run

    nc = _bacc.Bacc("TRN2", target_bir_lowering=False, num_devices=1)
    arrays, args = {}, []
    for name in _INS:
        a = _np.ascontiguousarray(inputs[name])
        arrays[f"in_{name}"] = a
        args.append(nc.dram_tensor(f"in_{name}", a.shape, _mybir.dt.from_np(a.dtype), kind="ExternalInput").ap())
    out = nc.dram_tensor("out_x", (NODES, D), F32, kind="ExternalOutput").ap()
    gps_layer(nc, *args, out)
    r = _run(nc, [arrays], core_ids=[0])
    return r.results[0]["out_x"]
```
